# Optimizing a Trainium2 kernel written in Bass

```python
import numpy as np
import jax
import jax.numpy as jnp

def _softmax(x, axis=-1):
    return jax.nn.softmax(x, axis=axis)

def _gelu(x):
    return jax.nn.gelu(x, approximate=True)

def _silu(x):
    return jax.nn.silu(x)

def _sigmoid(x):
    return jax.nn.sigmoid(x)

def _layernorm(x, axis=-1, eps=1e-05):
    m = jnp.mean(x, axis=axis, keepdims=True)
    v = jnp.var(x, axis=axis, keepdims=True)
    return (x - m) / jnp.sqrt(v + eps)

def _scatter_add(tgt, idx, src, axis=0):
    return tgt.at[idx].add(src)

def _segment_sum(src, seg, n):
    return jax.ops.segment_sum(src, seg, n)
kernel_name = 'mk_recurrent_d1_jaxref_r8_4da4af'

def setup_inputs(seed: int=0):
    np.random.seed(seed)
    _w = jnp.asarray

    def _L0_attn_setup():
        import jax, jax.numpy as jnp
        import numpy as np
        B, S, D, L = (4, 256, 128, 4)

        def _retention(x, wkqv):
            d = x.shape[-1]
            k, q, v = jnp.split(x @ wkqv, 3, axis=-1)
            qkt = jnp.einsum('bid,bjd->bij', q, k) / jnp.sqrt(jnp.float32(d))
            s = x.shape[1]
            row_norm = 1.0 + jnp.sqrt(jnp.arange(s, dtype=x.dtype))[None, :, None]
            r = jnp.tril(qkt) / row_norm
            denom = jnp.clip(jnp.abs(r.sum(-1, keepdims=True)), 1.0, None)
            r = r / denom
            return jnp.einsum('bij,bjd->bid', r, v)

        def _groupnorm1(y, g, b, eps=1e-05):
            mu = y.mean(axis=(1, 2), keepdims=True)
            var = y.var(axis=(1, 2), keepdims=True)
            return (y - mu) / jnp.sqrt(var + eps) * g + b

        def _layernorm(y, g, b, eps=1e-05):
            mu = y.mean(-1, keepdims=True)
            var = y.var(-1, keepdims=True)
            return (y - mu) / jnp.sqrt(var + eps) * g + b
        key = jax.random.key(seed)
        ks = jax.random.split(key, 6)
        w = lambda k, shape: jax.random.normal(k, shape, jnp.float32) * 0.02
        return {'x': jax.random.normal(ks[0], (B, S, D), jnp.float32), 'Wkqv': w(ks[1], (L, D, 3 * D)), 'Wm1': w(ks[2], (L, D, 2 * D)), 'bm1': jnp.zeros((L, 2 * D), jnp.float32), 'Wm2': w(ks[3], (L, D, D)), 'bm2': jnp.zeros((L, D), jnp.float32), 'gn_g': jnp.ones((L, D), jnp.float32), 'gn_b': jnp.zeros((L, D), jnp.float32), 'Wf1': w(ks[4], (L, D, 2 * D)), 'bf1': jnp.zeros((L, 2 * D), jnp.float32), 'Wf2': w(ks[5], (L, 2 * D, D)), 'bf2': jnp.zeros((L, D), jnp.float32), 'ln_g': jnp.ones((L, D), jnp.float32), 'ln_b': jnp.zeros((L, D), jnp.float32)}
    _L0_attn_in = _L0_attn_setup()

    def _L0_ffn_setup():
        import jax, jax.numpy as jnp
        import numpy as np
        NUM_EXPERTS = 8
        N_EMBD = 128
        D_FF = 4 * N_EMBD
        B, S = (4, 256)
        key = jax.random.key(seed)
        ks = jax.random.split(key, 6)
        x = jax.random.normal(ks[0], (B, S, N_EMBD), dtype=jnp.float32)
        gate_w = jax.random.normal(ks[1], (N_EMBD, NUM_EXPERTS), dtype=jnp.float32) * 0.02
        w1 = jax.random.normal(ks[2], (NUM_EXPERTS, N_EMBD, D_FF), dtype=jnp.float32) * 0.02
        b1 = jnp.zeros((NUM_EXPERTS, D_FF), dtype=jnp.float32)
        w2 = jax.random.normal(ks[3], (NUM_EXPERTS, D_FF, N_EMBD), dtype=jnp.float32) * 0.02
        b2 = jnp.zeros((NUM_EXPERTS, N_EMBD), dtype=jnp.float32)
        return {'x': x, 'gate_w': gate_w, 'w1': w1, 'b1': b1, 'w2': w2, 'b2': b2}
    _L0_ffn_in = _L0_ffn_setup()
    _d = {'L0_attn_x': _L0_attn_in['x'], 'L0_attn_Wkqv': _L0_attn_in['Wkqv'], 'L0_attn_Wm1': _L0_attn_in['Wm1'], 'L0_attn_bm1': _L0_attn_in['bm1'], 'L0_attn_Wm2': _L0_attn_in['Wm2'], 'L0_attn_bm2': _L0_attn_in['bm2'], 'L0_attn_gn_g': _L0_attn_in['gn_g'], 'L0_attn_gn_b': _L0_attn_in['gn_b'], 'L0_attn_Wf1': _L0_attn_in['Wf1'], 'L0_attn_bf1': _L0_attn_in['bf1'], 'L0_attn_Wf2': _L0_attn_in['Wf2'], 'L0_attn_bf2': _L0_attn_in['bf2'], 'L0_attn_ln_g': _L0_attn_in['ln_g'], 'L0_attn_ln_b': _L0_attn_in['ln_b'], 'L0_ffn_gate_w': _L0_ffn_in['gate_w'], 'L0_ffn_w1': _L0_ffn_in['w1'], 'L0_ffn_b1': _L0_ffn_in['b1'], 'L0_ffn_w2': _L0_ffn_in['w2'], 'L0_ffn_b2': _L0_ffn_in['b2']}
    _x0 = _d['L0_attn_x']
    _d['L0_attn_x'] = jax.random.normal(jax.random.fold_in(jax.random.key(seed), 1), (8, 512, 128), dtype=_x0.dtype)
    del _x0
    return _d

def reference(L0_attn_x, L0_attn_Wkqv, L0_attn_Wm1, L0_attn_bm1, L0_attn_Wm2, L0_attn_bm2, L0_attn_gn_g, L0_attn_gn_b, L0_attn_Wf1, L0_attn_bf1, L0_attn_Wf2, L0_attn_bf2, L0_attn_ln_g, L0_attn_ln_b, L0_ffn_gate_w, L0_ffn_w1, L0_ffn_b1, L0_ffn_w2, L0_ffn_b2):

    def _L0_attn_ref(x, Wkqv, Wm1, bm1, Wm2, bm2, gn_g, gn_b, Wf1, bf1, Wf2, bf2, ln_g, ln_b):
        import jax, jax.numpy as jnp
        import numpy as np
        B, S, D, L = (4, 256, 128, 4)

        def _retention(x, wkqv):
            d = x.shape[-1]
            k, q, v = jnp.split(x @ wkqv, 3, axis=-1)
            qkt = jnp.einsum('bid,bjd->bij', q, k) / jnp.sqrt(jnp.float32(d))
            s = x.shape[1]
            row_norm = 1.0 + jnp.sqrt(jnp.arange(s, dtype=x.dtype))[None, :, None]
            r = jnp.tril(qkt) / row_norm
            denom = jnp.clip(jnp.abs(r.sum(-1, keepdims=True)), 1.0, None)
            r = r / denom
            return jnp.einsum('bij,bjd->bid', r, v)

        def _groupnorm1(y, g, b, eps=1e-05):
            mu = y.mean(axis=(1, 2), keepdims=True)
            var = y.var(axis=(1, 2), keepdims=True)
            return (y - mu) / jnp.sqrt(var + eps) * g + b

        def _layernorm(y, g, b, eps=1e-05):
            mu = y.mean(-1, keepdims=True)
            var = y.var(-1, keepdims=True)
            return (y - mu) / jnp.sqrt(var + eps) * g + b

        def block(h, p):
            wk, w1, b1, w2, b2, gg, gb, wf1, bf1_, wf2, bf2_, lg, lb = p
            r = _retention(h, wk)
            m = r @ w1 + b1
            a, gate = jnp.split(m, 2, axis=-1)
            m = a * jax.nn.silu(gate) @ w2 + b2
            m = _groupnorm1(m, gg, gb)
            y = m + h
            f = jax.nn.gelu(y @ wf1 + bf1_, approximate=False) @ wf2 + bf2_
            return (_layernorm(f + y, lg, lb), None)
        params = (Wkqv, Wm1, bm1, Wm2, bm2, gn_g, gn_b, Wf1, bf1, Wf2, bf2, ln_g, ln_b)
        out, _ = jax.lax.scan(block, x, params)
        return out

    def _L0_ffn_ref(x, gate_w, w1, b1, w2, b2):
        import jax, jax.numpy as jnp
        import numpy as np
        NUM_EXPERTS = 8
        N_EMBD = 128
        D_FF = 4 * N_EMBD
        B, S = (4, 256)
        Bb, Ss, D = x.shape
        x_flat = x.reshape(-1, D)
        router_logits = x_flat @ gate_w
        router_probs = jax.nn.softmax(router_logits, axis=-1)
        expert_idx = jnp.argmax(router_probs, axis=-1)
        expert_w = jnp.take_along_axis(router_probs, expert_idx[:, None], axis=1)[:, 0]
        out = jnp.zeros_like(x_flat)
        for e in range(NUM_EXPERTS):
            h = jax.nn.gelu(x_flat @ w1[e] + b1[e], approximate=False)
            y = h @ w2[e] + b2[e]
            sel = expert_idx == e
            out = out + jnp.where(sel, expert_w, 0.0)[:, None] * y
        return out.reshape(Bb, Ss, D)
    x = L0_attn_x
    xn = _layernorm(x, axis=-1)
    s = _L0_attn_ref(xn, L0_attn_Wkqv, L0_attn_Wm1, L0_attn_bm1, L0_attn_Wm2, L0_attn_bm2, L0_attn_gn_g, L0_attn_gn_b, L0_attn_Wf1, L0_attn_bf1, L0_attn_Wf2, L0_attn_bf2, L0_attn_ln_g, L0_attn_ln_b)
    g = _silu(_L0_ffn_ref(xn, L0_ffn_gate_w, L0_ffn_w1, L0_ffn_b1, L0_ffn_w2, L0_ffn_b2))
    x = x + s * g
    return x

_drawn_inputs = setup_inputs


def setup_inputs(seed=0):
    import zlib

    import numpy as np

    out = dict(_drawn_inputs(seed))
    spreads = {'L0_attn_bm1': (0.0, 0.8),
     'L0_attn_bm2': (0.0, 0.583),
     'L0_attn_gn_g': (1.0, 0.6),
     'L0_attn_gn_b': (0.0, 0.8),
     'L0_attn_bf1': (0.0, 0.8),
     'L0_attn_bf2': (0.0, 0.8),
     'L0_attn_ln_g': (1.0, 0.6),
     'L0_attn_ln_b': (0.0, 0.8),
     'L0_ffn_b1': (0.0, 0.8),
     'L0_ffn_b2': (0.0, 0.8)}
    factors = {'L0_attn_Wkqv': 8.0,
     'L0_attn_Wm1': 8.0,
     'L0_attn_Wm2': 8.0,
     'L0_attn_Wf1': 8.0,
     'L0_attn_Wf2': 8.0,
     'L0_ffn_gate_w': 5.782,
     'L0_ffn_w1': 8.0,
     'L0_ffn_w2': 8.0}
    for name, (base, spread) in spreads.items():
        noise = np.random.default_rng([zlib.crc32(name.encode()), seed]).standard_normal(out[name].shape)
        drawn = base * np.exp(spread * noise) if base else spread * noise
        out[name] = jnp.asarray(drawn.astype(out[name].dtype))
    for name, factor in factors.items():
        out[name] = (out[name] * factor).astype(out[name].dtype)
    return out
```

```python
import concourse.bass as bass
from concourse import mybir
from contextlib import ExitStack



def retention_moe_kernel(nc, x, Wkqv, Wm1, bm1, Wm2, bm2, gn_g, gn_b, Wf1, bf1, Wf2, bf2, ln_g, ln_b,
                         gate_w, w1, b1, w2, b2, row_floor, out):
    f32 = mybir.dt.float32
    i32 = mybir.dt.int32
    u32 = mybir.dt.uint32
    ALU = mybir.AluOpType
    ACT = mybir.ActivationFunctionType
    AX = mybir.AxisListType.X

    B, S, D = x.shape
    L = Wkqv.shape[0]
    E, FF = w1.shape[0], w1.shape[2]
    P = 128
    C = S // P
    KF = FF // P
    NT = B * C
    TOK = B * S
    SLOT_TILES = (TOK + E * (P - 1)) // P
    H1 = D + 1
    ROW = D + 2
    EPS = 1e-5
    UN = 3
    assert D == P and SLOT_TILES % UN == 0 and KF == C

    x_slots = nc.dram_tensor("x_slots", [SLOT_TILES * P, ROW], f32, kind="Internal").ap()
    y_rows = nc.dram_tensor("y_rows", [TOK + SLOT_TILES * P, D], f32, kind="Internal").ap()

    ctx = ExitStack()
    with ctx:
        def sb(name, shape, dt=f32):
            return ctx.enter_context(nc.sbuf_tensor(name, shape, dt))

        def sem(name):
            return ctx.enter_context(nc.semaphore(name))

        pair = ctx.enter_context(nc.psum_tensor("pair", [P, 2, 512], f32))
        bank = {k: ctx.enter_context(nc.psum_tensor(f"bank{k}", [P, 512], f32)) for k in range(2, 8)}

        x_sb = sb("x_sb", [P, NT, D])
        xn = sb("xn", [P, NT, ROW])
        htok = sb("htok", [P, NT, H1])
        hT = sb("hT", [P, B, S])
        moe_w1 = sb("moe_w1", [P, E, FF])
        moe_w2 = sb("moe_w2", [P, E, KF, D])
        moe_b1 = sb("moe_b1", [P, E, FF])
        moe_b2 = sb("moe_b2", [P, E, D])
        all_m = sb("all_m", [P, L, D])
        all_w = sb("all_w", [P, L, 2 * D])
        all_w2 = sb("all_w2", [P, L, D])
        all_f1 = sb("all_f1", [P, L, 2 * D])
        all_f2 = sb("all_f2", [P, L, 2, D])
        all_lg = sb("all_lg", [P, L, D])
        all_lb = sb("all_lb", [P, L, D])
        NPAR = 9
        GATE_B, VAL_B, W2_B, GN_G, GN_B, F_B, LN_G, LN_B = 0, 1, 2, 3, 4, 5, 7, 8
        all_par = sb("all_par", [P, L, NPAR])
        m_l = sb("m_l", [P, D])
        w_l = sb("w_l", [P, 2 * D])
        w2_l = sb("w2_l", [P, D])
        f1_l = sb("f1_l", [P, 2 * D])
        f2_l = sb("f2_l", [P, 2, D])
        lg_l = sb("lg_l", [P, D])
        lb_l = sb("lb_l", [P, D])
        par = sb("par", [P, NPAR])
        ident = sb("ident", [P, P])
        causal = sb("causal", [P, P])
        before = sb("before", [P, P])
        ones = sb("ones", [P, 2 * P])
        mean_of = sb("mean_of", [P, P])
        half_neg = sb("half_neg", [P, C])
        floor_sb = sb("floor_sb", [P, C])
        gate_sb = sb("gate_sb", [P, E])
        q_sb = sb("q_sb", [P, S])
        A_sb = sb("A_sb", [P, C, P])
        S_sb = sb("S_sb", [P, C - 1, H1])
        u_sb = sb("u_sb", [P, C, D])
        uT_sb = sb("uT_sb", [P, S])
        gg_sb = sb("gg_sb", [P, S])
        th_sb = sb("th_sb", [P, S])
        gate_t = sb("gate_t", [P, S])
        act_sb = sb("act_sb", [P, S])
        gn_sb = sb("gn_sb", [P, S])
        y_sb = sb("y_sb", [P, S])
        G_sb = sb("G_sb", [P, 2, S])
        zhat = sb("zhat", [P, 2, C, D])
        hg = sb("hg", [P, C, D])
        rs1 = sb("rs1", [P, C])
        rs2 = sb("rs2", [P, C])
        rs3 = sb("rs3", [P, C])
        ln_st = sb("ln_st", [P, 2, C, 6])
        ln_mv = sb("ln_mv", [P, 2, C, 2])
        ln_ve = sb("ln_ve", [P, 2, C])
        ln_rs = sb("ln_rs", [P, 2, C])
        gs_st = sb("gs_st", [P, 6])
        gs_mv = sb("gs_mv", [P, 2])
        gs = sb("gs", [P, 2])
        gn_m = sb("gn_m", [P, 2])
        gn_nv = sb("gn_nv", [P, 1])
        gn_ve = sb("gn_ve", [P, 1])
        gn_rs = sb("gn_rs", [P, 1])
        gn_sc = sb("gn_sc", [P, 1])
        gn_d = sb("gn_d", [P, 1])
        gn_bi = sb("gn_bi", [P, 1])

        NROWS = 10 * L
        R_BM1, R_BM2, R_GG, R_GB, R_BF1, R_BF2, R_LG, R_LB = (L * k for k in (0, 2, 3, 4, 5, 7, 8, 9))
        rows = sb("rows", [NROWS, P])
        rowsT = sb("rowsT", [P, NROWS])
        wkqv_sb = moe_b1[:, 0:3, :].rearrange("p e f -> p (e f)").rearrange("p (l f) -> p l f", l=L)
        wm1_sb = moe_b1[:, 3:5, :].rearrange("p e f -> p (e f)").rearrange("p (l f) -> p l f", l=L)
        wT_sb = moe_b1[:, 5, 0:3 * D]
        fill = moe_b1[:, 6, 0:H1]
        fill_id = sb("fill_id", [P, SLOT_TILES], i32)
        TE = NT * E
        r_lg = sb("r_lg", [P, NT, E])
        r_a = sb("r_a", [P, NT, E])
        r_c = sb("r_c", [P, NT, E])
        r_oh = sb("r_oh", [P, NT, E])
        r_tot = sb("r_tot", [P, E, NT])
        r_cum = sb("r_cum", [P, E, NT])
        r_mx = sb("r_mx", [P, NT])
        r_ix = sb("r_ix", [P, NT])
        r_sum = sb("r_sum", [P, NT])
        weight = sb("weight", [P, NT])
        posf = sb("posf", [P, NT])
        pos = sb("pos", [P, NT], i32)
        iota_e = sb("iota_e", [P, E])
        tile_at = sb("tile_at", [P, SLOT_TILES])
        filled = sb("filled", [P, NT])
        r_prev = sb("r_prev", [P, E])
        r_n = sb("r_n", [P, E])
        r_nt = sb("r_nt", [P, E])
        r_end = sb("r_end", [P, E])
        r_base = sb("r_base", [P, E])
        r_k = sb("r_k", [P, E, NT])
        r_te = sb("r_te", [P, SLOT_TILES, E])
        tile_ef = sb("tile_ef", [P, SLOT_TILES])
        tile_e = sb("tile_e", [P, SLOT_TILES], i32)
        xt = [sb(f"xt{i}", [P, ROW]) for i in range(UN)]
        yt = [sb(f"yt{i}", [P, D]) for i in range(UN)]
        xtT = sb("xtT", [P, P])
        slot_ids = sb("slot_ids", [P, SLOT_TILES], i32)
        tile_ids = [sb(f"tile_ids{i}", [P, 1], i32) for i in range(UN)]
        h_in, h_act = gg_sb, th_sb
        h_T = act_sb
        yg = G_sb[:, :, :]

        x_in = [sem(f"x_in{b}") for b in range(B)]
        kqv_in, m1_in, rows_in, small_in = sem("kqv_in"), sem("m1_in"), sem("rows_in"), sem("small_in")
        w2_in, f1_in, f2_in, ln_in = sem("w2_in"), sem("f1_in"), sem("f2_in"), sem("ln_in")
        experts_in, bias1_in = sem("experts_in"), sem("bias1_in")
        const_made = sem("const_made")
        fill_made, filled_out = sem("fill_made"), sem("filled_out")
        col_made, ids_made = sem("col_made"), sem("ids_made")
        ln_chain, ln_var, ln_rstd = sem("ln_chain"), sem("ln_var"), sem("ln_rstd")
        xn_done, pe_xT, xT_done, pe_gate = sem("xn_done"), sem("pe_xT"), sem("xT_done"), sem("pe_gate")
        pe_wT, wT_done, pe_prod, prod_done = sem("pe_wT"), sem("wT_done"), sem("pe_prod"), sem("prod_done")
        pe_rows, rows_done, par_chain, par_done = sem("pe_rows"), sem("rows_done"), sem("par_chain"), sem("par_done")
        r_step, r_exp, pe_prefix, route_done = sem("r_step"), sem("r_exp"), sem("pe_prefix"), sem("route_done")
        r_shift = sem("r_shift")
        scattered = sem("scattered")
        m_set, w_set, w2_set, f_set, ln_set = sem("m_set"), sem("w_set"), sem("w2_set"), sem("f_set"), sem("ln_set")
        pe_S, pe_q, pe_A, pe_u, pe_uT = sem("pe_S"), sem("pe_q"), sem("pe_A"), sem("pe_u"), sem("pe_uT")
        pe_g, pe_a, pe_w2, pe_gn, pe_f1 = sem("pe_g"), sem("pe_a"), sem("pe_w2"), sem("pe_gn"), sem("pe_f1")
        pe_z, pe_zT = sem("pe_z"), sem("pe_zT")
        S_part, S_done, q_done, A_done = sem("S_part"), sem("S_done"), sem("q_done"), sem("A_done")
        u_chain, u_done, uT_done = sem("u_chain"), sem("u_done"), sem("uT_done")
        gg_done, th_done, gt_done, act_done = sem("gg_done"), sem("th_done"), sem("gt_done"), sem("act_done")
        gs_chain, gs_done = sem("gs_chain"), sem("gs_done")
        gn_chain, gn_var, gn_rstd, gn_affine = sem("gn_chain"), sem("gn_var"), sem("gn_rstd"), sem("gn_affine")
        gn_done, y_done, G_done = sem("gn_done"), sem("y_done"), sem("G_done")
        z_done, hg_done, htok_done, hT_done = sem("z_done"), sem("hg_done"), sem("htok_done"), sem("hT_done")
        xt_in = [sem(f"xt_in{i}") for i in range(UN)]
        yt_out = [sem(f"yt_out{i}") for i in range(UN)]
        ids_in, ids_set = sem("ids_in"), sem("ids_set")
        pe_xt, xtT_done, pe_h, hb_done, h_done = sem("pe_xt"), sem("xtT_done"), sem("pe_h"), sem("hb_done"), sem("h_done")
        pe_hT, hT_copied, pe_y, yt_done = sem("pe_hT"), sem("hT_copied"), sem("pe_y"), sem("yt_done")
        yg_in = [sem(f"yg_in{i}") for i in range(2)]
        e_f, e_th, e_t, e_s, e_o = sem("e_f"), sem("e_th"), sem("e_t"), sem("e_s"), sem("e_o")
        out_done, passed = sem("out_done"), sem("passed")

        block = ctx.enter_context(nc.Block())

        def need(eng, s, v):
            if not isinstance(v, int) or v > 0:
                eng.wait_ge(s, v)

        def alone(eng, s, v):
            eng.wait_ge(s, v)
            if not isinstance(v, int):
                eng.sem_inc(passed, 1)

        def steps(eng, step, turns, width, lag):
            for t in range(width):
                step(0, t)
            with eng.Fori(1, turns) as l:
                for t in range(width):
                    step(l, t)
            for t in range(lag):
                step(turns, t)

        def at(l, t, late, width, count):
            b, l = (t - late) % width, l + (t - late) // width
            if isinstance(l, int) and (l < 0 or l * width + b >= count):
                return None
            return l * width + b, b, l

        LB = L * B
        LAG = 3

        @block.sync
        def _(sp):
            for b in range(B):
                sp.dma_start(x_sb[:, b * C:(b + 1) * C, :],
                             x[b].rearrange("(c p) d -> p c d", p=P)).then_inc(x_in[b], 16)
            sp.dma_start(all_w2[:, :, :], Wm2.rearrange("l p d -> p l d")).then_inc(w2_in, 16)
            sp.dma_start(all_f2[:, :, :, :].rearrange("p l k d -> p (l k) d"),
                         Wf2.rearrange("l (k p) d -> p (l k) d", p=P)).then_inc(f2_in, 16)
            sp.wait_ge(fill_made, 2)
            slots = x_slots.rearrange("(t p) w -> p t w", p=P)
            sp.dma_start(slots[:, :, 0:H1],
                         fill.unsqueeze(1).broadcast_to([P, SLOT_TILES, H1])).then_inc(filled_out, 16)
            with nc.allow_non_contiguous_dma(reason="one word a slot"):
                sp.dma_start(slots[:, :, H1:ROW].rearrange("p t w -> p (t w)"),
                             fill_id[:, :].bitcast(f32)).then_inc(filled_out, 16)
            sp.dma_start(moe_w1[:, :, :], w1.rearrange("e p f -> p e f")).then_inc(experts_in, 16)
            sp.dma_start(moe_w2[:, :, :, :].rearrange("p e k d -> p (e k) d"),
                         w2.rearrange("e (k p) d -> p (e k) d", p=P)).then_inc(experts_in, 16)
            sp.dma_start(moe_b2[:, :, :], b2.partition_broadcast(P)).then_inc(experts_in, 16)
            sp.wait_ge(prod_done, L)
            sp.wait_ge(filled_out, 32)
            sp.dma_start(moe_b1[:, :, :], b1.partition_broadcast(P)).then_inc(bias1_in, 16)
            sp.wait_ge(scattered, 16 * NT)
            with nc.allow_non_contiguous_dma(reason="one word a slot"):
                sp.dma_start(slot_ids[:, :].bitcast(f32), slots[:, :, H1:ROW].rearrange("p t w -> p (t w)"))\
                    .then_inc(ids_in, 16)

            def load_step(g, t):
                w = at(g, t, 0, UN, SLOT_TILES)
                if w is None:
                    return
                n, i, _ = w
                if not isinstance(n, int):
                    alone(sp, pe_xt, n - UN + 1)
                sp.dma_start(xt[i][:, :], x_slots[bass.ds(n * P, P), :]).then_inc(xt_in[i], 16)

            for t in range(UN):
                load_step(0, t)
            with sp.Fori(1, SLOT_TILES // UN) as g:
                for t in range(UN):
                    load_step(g, t)
            for i in range(UN):
                sp.wait_ge(yt_out[i], 16 * (SLOT_TILES // UN))
            for b in range(B):
                need(sp, e_f, b - 1)
                sp.dma_start(yg[:, b % 2, :].rearrange("p (c d) -> p c d", c=C),
                             y_rows[b * S:(b + 1) * S, :].rearrange("(c p) d -> p c d", p=P))\
                    .then_inc(yg_in[b % 2], 16)
            for b in range(B):
                sp.wait_ge(e_o, b + 1)
                sp.dma_start(out[b].rearrange("(c p) d -> p c d", p=P),
                             x_sb[:, b * C:(b + 1) * C, :]).then_inc(out_done, 16)
            sp.wait_ge(out_done, 16 * B)

        @block.gpsimd
        def _(pool):
            pool.memset(ones[:, :], 1.0).then_inc(const_made, 1)
            pool.memset(half_neg[:, :], -0.5).then_inc(const_made, 1)
            pool.memset(mean_of[:, :], 1.0 / D).then_inc(const_made, 1)
            pool.wait_ge(const_made, 1)
            pool.affine_select(out=ident[:, :], in_=ones[:, 0:P], compare_op=ALU.is_equal, fill=0.0, base=0,
                               pattern=[[-1, P]], channel_multiplier=1).then_inc(const_made, 1)
            pool.affine_select(out=causal[:, :], in_=ones[:, 0:P], compare_op=ALU.is_ge, fill=0.0, base=0,
                               pattern=[[1, P]], channel_multiplier=-1).then_inc(const_made, 1)
            pool.affine_select(out=before[:, :], in_=ones[:, 0:P], compare_op=ALU.is_gt, fill=0.0, base=0,
                               pattern=[[1, P]], channel_multiplier=-1).then_inc(const_made, 1)
            pool.memset(fill, 0.0).then_inc(fill_made, 1)
            pool.iota(fill_id[:, :], pattern=[[P, SLOT_TILES]], base=TOK, channel_multiplier=1)\
                .then_inc(fill_made, 1)
            pool.memset(xn[:, :, D:H1], 1.0).then_inc(col_made, 1)
            pool.memset(htok[:, :, D:H1], 1.0).then_inc(col_made, 1)
            pool.iota(xn[:, :, H1:ROW].rearrange("p t w -> p (t w)").bitcast(i32), pattern=[[P, NT]],
                      base=0, channel_multiplier=1).then_inc(ids_made, 1)
            pool.iota(iota_e[:, :], pattern=[[1, E]], base=-E, channel_multiplier=0,
                      allow_small_or_imprecise_dtypes=True).then_inc(ids_made, 1)
            pool.iota(tile_at[:, :], pattern=[[1, SLOT_TILES]], base=0, channel_multiplier=0,
                      allow_small_or_imprecise_dtypes=True).then_inc(ids_made, 1)
            pool.iota(filled[:, :], pattern=[[P, NT]], base=0, channel_multiplier=0,
                      allow_small_or_imprecise_dtypes=True).then_inc(ids_made, 1)

            def ln_pow(k, b):
                pool.wait_ge(ln_var, k + 1)
                pool.tensor_tensor(ln_rs[:, b % 2, :], ln_ve[:, b % 2, :], half_neg[:, :], ALU.pow)\
                    .then_inc(ln_rstd, 1)

            pool.wait_ge(const_made, 6)
            for b in range(B):
                ln_pow(b, b)

            def set_m(l):
                need(pool, pe_q, l * B)
                pool.tensor_copy(m_l[:, :], all_m[:, l, :]).then_inc(m_set, 1)

            def set_w(l):
                need(pool, pe_a, l * B)
                need(pool, th_done, l * B)
                need(pool, act_done, l * B)
                pool.tensor_copy(par[:, GATE_B:VAL_B + 1], all_par[:, l, GATE_B:VAL_B + 1])
                pool.tensor_copy(w_l[:, :], all_w[:, l, :]).then_inc(w_set, 1)

            def set_w2(l):
                need(pool, pe_w2, l * B)
                need(pool, gn_affine, l * B)
                pool.tensor_copy(par[:, W2_B:GN_B + 1], all_par[:, l, W2_B:GN_B + 1])
                pool.tensor_copy(w2_l[:, :], all_w2[:, l, :]).then_inc(w2_set, 1)

            def set_f(l):
                need(pool, pe_z, l * B)
                need(pool, G_done, l * B * 2)
                pool.tensor_copy(par[:, F_B:F_B + 2], all_par[:, l, F_B:F_B + 2])
                pool.tensor_copy(f1_l[:, :], all_f1[:, l, :])
                pool.tensor_copy(f2_l[:, :, :], all_f2[:, l, :, :]).then_inc(f_set, 1)

            def set_ln(l):
                need(pool, hT_done, l * B)
                need(pool, htok_done, l * B)
                pool.tensor_copy(par[:, LN_G:LN_B + 1], all_par[:, l, LN_G:LN_B + 1])
                pool.tensor_copy(lg_l[:, :], all_lg[:, l, :])
                pool.tensor_copy(lb_l[:, :], all_lb[:, l, :]).then_inc(ln_set, 1)

            pool.wait_ge(prod_done, L)
            pool.wait_ge(par_done, 1)
            pool.wait_ge(w2_in, 16)
            pool.wait_ge(f1_in, 16)
            pool.wait_ge(f2_in, 16)
            pool.wait_ge(ln_in, 32)

            def scatter(b):
                for c in range(C):
                    k = b * C + c
                    pool.indirect_dma_start(x_slots[:, :], bass.IndirectOffsetOnAxis(ap=pos[:, k:k + 1], axis=0),
                                            xn[:, k, :], None).then_inc(scattered, 16)

            def step(l, t):
                if t == 0 and not (isinstance(l, int) and l == L):
                    set_m(l)
                first = isinstance(l, int) and l == 0
                if w := at(l, t, 2, B, LB):
                    pool.wait_ge(gn_var, w[0] + 1)
                    pool.tensor_tensor(gn_rs[:, :], gn_ve[:, :], half_neg[:, 0:1], ALU.pow).then_inc(gn_rstd, 1)
                if w := at(l, t, 3, B, LB):
                    ln_pow(w[0] + B, w[1])
                if not (isinstance(l, int) and l == L):
                    if t == 1:
                        set_w(l)
                        set_w2(l)
                    elif t == 2:
                        set_f(l)
                    elif t == 3:
                        set_ln(l)
                if w := at(l, t, 2, B, LB):
                    n, b, _ = w
                    pool.wait_ge(gn_done, n + 1)
                    pool.tensor_tensor(y_sb[:, :], gn_sb[:, :], hT[:, b, :], ALU.add).then_inc(y_done, 1)
                if w := at(l, t, 3, B, LB):
                    n, b, _ = w
                    if b == 0:
                        pool.wait_ge(ln_set, w[2] + 1)
                    pool.wait_ge(z_done, n + 1)
                    pool.tensor_tensor(hg[:, :, :], zhat[:, b % 2, :, :],
                                       lg_l[:, :].unsqueeze(1).broadcast_to([P, C, D]), ALU.mult)\
                        .then_inc(hg_done, 1)
                    pool.wait_ge(hg_done, n + 1)
                    pool.tensor_tensor(htok[:, b * C:(b + 1) * C, 0:D], hg[:, :, :],
                                       lb_l[:, :].unsqueeze(1).broadcast_to([P, C, D]), ALU.add)\
                        .then_inc(htok_done, 1)
                if first:
                    if t == 0:
                        pool.wait_ge(route_done, 1)
                        pool.wait_ge(filled_out, 32)
                    scatter(t)

            steps(pool, step, L, B, LAG)

            pool.wait_ge(ids_in, 16)

            def tile_step(g, t):
                if w := at(g, t, 3, UN, SLOT_TILES):
                    n, i, k = w
                    need(pool, yt_out[i], 16 * k)
                    pool.tensor_copy(tile_ids[i][:, :], slot_ids[:, bass.ds(n, 1)]).then_inc(ids_set, 1)
                    alone(pool, ids_set, n + 1)
                    alone(pool, yt_done, n + 1)
                    pool.indirect_dma_start(y_rows[:, :],
                                            bass.IndirectOffsetOnAxis(ap=tile_ids[i][:, :], axis=0),
                                            yt[i][:, :], None).then_inc(yt_out[i], 16)

            steps(pool, tile_step, SLOT_TILES // UN, UN, 3)
            for b in range(B):
                pool.wait_ge(e_s, b + 1)
                pool.tensor_tensor(x_sb[:, b * C:(b + 1) * C, :], x_sb[:, b * C:(b + 1) * C, :],
                                   u_sb[:, :, :] if b % 2 else A_sb[:, :, :], ALU.add).then_inc(e_o, 1)

        @block.scalar
        def _(act):
            act.dma_start(wkqv_sb, Wkqv.rearrange("l p f -> p l f")).then_inc(kqv_in, 16)
            act.dma_start(wm1_sb, Wm1.rearrange("l p f -> p l f")).then_inc(m1_in, 16)
            for v, r in ((bm1.rearrange("l (k p) -> (l k) p", p=P), R_BM1), (bm2, R_BM2), (gn_g, R_GG),
                         (gn_b, R_GB), (bf1.rearrange("l (k p) -> (l k) p", p=P), R_BF1), (bf2, R_BF2),
                         (ln_g, R_LG), (ln_b, R_LB)):
                act.dma_start(rows[r:r + v.shape[0], :], v).then_inc(rows_in, 16)
            act.dma_start(gate_sb[:, :], gate_w).then_inc(small_in, 16)
            act.dma_start(floor_sb[:, :], row_floor).then_inc(small_in, 16)
            act.dma_start(all_f1[:, :, :], Wf1.rearrange("l p f -> p l f")).then_inc(f1_in, 16)
            act.dma_start(all_lg[:, :, :], ln_g.partition_broadcast(P)).then_inc(ln_in, 16)
            act.dma_start(all_lb[:, :, :], ln_b.partition_broadcast(P)).then_inc(ln_in, 16)
            for l in range(L):
                act.wait_ge(pe_wT, l + 1)
                if l:
                    act.wait_ge(pe_prod, l)
                act.activation(wT_sb, bank[2][:, 0:3 * D], ACT.Copy).then_inc(wT_done, 1)
            for b in range(B):
                act.wait_ge(pe_xT, b + 1)
                act.activation(hT[:, b, :], pair[:, b % 2, :], ACT.Copy).then_inc(xT_done, 1)
            act.wait_ge(r_shift, 1)
            act.activation(r_a[:, :, :], r_c[:, :, :], ACT.Exp).then_inc(r_exp, 1)

            def step(l, t):
                if w := at(l, t, 1, B, LB):
                    act.wait_ge(pe_uT, w[0] + 1)
                    act.activation(uT_sb[:, :], bank[2][:, :], ACT.Copy).then_inc(uT_done, 1)
                if w := at(l, t, 0, B, LB):
                    act.wait_ge(pe_q, w[0] + 1)
                    act.activation(q_sb[:, :], pair[:, 0, :], ACT.Copy).then_inc(q_done, 1)
                if w := at(l, t, 2, B, LB):
                    act.wait_ge(gn_affine, w[0] + 1)
                    act.activation(gn_sb[:, :], bank[6][:, :], ACT.Identity, bias=gn_bi[:, :],
                                   scale=gn_sc[:, :]).then_inc(gn_done, 1)
                if w := at(l, t, 1, B, LB):
                    act.wait_ge(pe_g, w[0] + 1)
                    act.activation(th_sb[:, :], bank[3][:, :], ACT.Tanh, bias=par[:, GATE_B:GATE_B + 1],
                                   scale=0.5).then_inc(th_done, 1)
                    act.activation(gg_sb[:, :], bank[3][:, :], ACT.Identity, bias=par[:, GATE_B:GATE_B + 1],
                                   scale=0.5).then_inc(gg_done, 1)
                if w := at(l, t, 3, B, LB):
                    n, b, _ = w
                    act.wait_ge(pe_zT, n + 1)
                    if b == 0:
                        act.wait_ge(ln_set, w[2] + 1)
                    act.activation(hT[:, b, :], pair[:, 1, :], ACT.Identity, bias=par[:, LN_B:LN_B + 1],
                                   scale=par[:, LN_G:LN_G + 1]).then_inc(hT_done, 1)
                if w := at(l, t, 2, B, LB):
                    for k in range(2):
                        act.wait_ge(pe_f1, w[0] * 2 + k + 1)
                        act.activation(G_sb[:, k, :], bank[4 + k][:, :], ACT.Gelu,
                                       bias=par[:, F_B + k:F_B + k + 1]).then_inc(G_done, 1)

            steps(act, step, L, B, LAG)

            def tile_step(g, t):
                if w := at(g, t, 1, UN, SLOT_TILES):
                    n = w[0]
                    act.wait_ge(hb_done, n + 1)
                    need(act, pe_hT, n)
                    act.activation(h_act[:, :], h_in[:, :], ACT.Gelu).then_inc(h_done, 1)
                if w := at(g, t, 2, UN, SLOT_TILES):
                    act.wait_ge(pe_hT, w[0] + 1)
                    act.activation(h_T[:, :], bank[4][:, :], ACT.Copy).then_inc(hT_copied, 1)

            steps(act, tile_step, SLOT_TILES // UN, UN, 3)
            for b in range(B):
                act.wait_ge(e_f, b + 1)
                act.activation(h_act[:, :], h_in[:, :], ACT.Tanh, scale=0.5).then_inc(e_th, 1)

        @block.vector
        def _(dve):
            def ln_stats(k, b, src):
                for c in range(C):
                    last = dve.bn_stats(ln_st[:, b % 2, c, :], src(c))
                last.then_inc(ln_chain, 1)
                alone(dve, ln_chain, 2 * k + 1)
                for c in range(C):
                    last = dve.bn_aggr(ln_mv[:, b % 2, c, :], ln_st[:, b % 2, c, :])
                last.then_inc(ln_chain, 1)
                dve.wait_ge(ln_chain, 2 * k + 2)
                dve.tensor_scalar(ln_ve[:, b % 2, :], ln_mv[:, b % 2, :, 1], EPS, None, ALU.add)\
                    .then_inc(ln_var, 1)

            def ln_apply(k, b, dst, src, done):
                dve.wait_ge(ln_rstd, k + 1)
                for c in range(C):
                    last = dve.tensor_scalar(dst(c), src(c), ln_mv[:, b % 2, c, 0:1], ln_rs[:, b % 2, c:c + 1],
                                             ALU.subtract, ALU.mult)
                last.then_inc(done, 1)

            for b in range(B + 1):
                if b < B:
                    dve.wait_ge(x_in[b], 16)
                    ln_stats(b, b, lambda c: x_sb[:, b * C + c, :])
                if b:
                    a = b - 1
                    ln_apply(a, a, lambda c: xn[:, a * C + c, 0:D], lambda c: x_sb[:, a * C + c, :], xn_done)

            dve.wait_ge(pe_rows, 1)
            dve.tensor_copy(rowsT[:, :], bank[6][:, 0:NROWS]).then_inc(rows_done, 1)
            dve.wait_ge(rows_done, 1)
            bm1T = rowsT[:, R_BM1:R_BM1 + 2 * L].rearrange("p (l k) -> p l k", k=2)
            bf1T = rowsT[:, R_BF1:R_BF1 + 2 * L].rearrange("p (l k) -> p l k", k=2)
            dve.tensor_scalar(all_par[:, :, GATE_B], bm1T[:, :, 1], 0.5, None, ALU.mult)
            dve.tensor_copy(all_par[:, :, VAL_B], bm1T[:, :, 0])
            dve.tensor_copy(all_par[:, :, W2_B], rowsT[:, R_BM2:R_BM2 + L])
            dve.tensor_copy(all_par[:, :, GN_G], rowsT[:, R_GG:R_GG + L])
            dve.tensor_tensor(all_par[:, :, GN_B], rowsT[:, R_GB:R_GB + L], rowsT[:, R_BF2:R_BF2 + L], ALU.add)
            dve.tensor_copy(all_par[:, :, LN_G], rowsT[:, R_LG:R_LG + L])
            dve.tensor_copy(all_par[:, :, LN_B], rowsT[:, R_LB:R_LB + L]).then_inc(par_done, 1)
            for l in range(L):
                dve.wait_ge(pe_prod, l + 1)
                dve.tensor_copy(all_m[:, l, :], bank[4][:, 0:D])
                dve.tensor_copy(all_w[:, l, :], bank[4][:, D:3 * D])
                dve.tensor_tensor(all_par[:, l, F_B:F_B + 2], bf1T[:, l, :], bank[4][:, 3 * D:3 * D + 2],
                                  ALU.subtract).then_inc(prod_done, 1)

            done = [0]

            def chain(inst):
                inst.then_inc(r_step, 1)
                done[0] += 1
                dve.wait_ge(r_step, done[0])

            def over_e(v):
                return v.unsqueeze(2).broadcast_to([P, NT, E])

            def over_t(v):
                return v.unsqueeze(1).broadcast_to([P, NT, E])

            dve.wait_ge(ids_made, 4)
            dve.wait_ge(pe_gate, B)
            chain(dve.tensor_copy(r_lg[:, :, :].rearrange("p t e -> p (t e)"), bank[7][:, 0:TE]))
            chain(dve.tensor_reduce(r_mx[:, :], r_lg[:, :, :], AX, ALU.max))
            dve.tensor_tensor(r_c[:, :, :], r_lg[:, :, :], over_e(r_mx[:, :]), ALU.subtract).then_inc(r_shift, 1)
            chain(dve.tensor_tensor(r_oh[:, :, :], r_lg[:, :, :], over_e(r_mx[:, :]), ALU.is_equal))
            chain(dve.tensor_tensor(r_lg[:, :, :], r_oh[:, :, :], over_t(iota_e[:, :]), ALU.mult))
            chain(dve.tensor_reduce(r_ix[:, :], r_lg[:, :, :], AX, ALU.min))
            dve.tensor_tensor(r_oh[:, :, :], over_t(iota_e[:, :]), over_e(r_ix[:, :]), ALU.is_equal)\
                .then_inc(r_shift, 1)
            dve.wait_ge(r_exp, 1)
            chain(dve.tensor_reduce(r_sum[:, :], r_a[:, :, :], AX, ALU.add))
            chain(dve.reciprocal(weight[:, :], r_sum[:, :]))
            dve.wait_ge(pe_prefix, 1)
            prefix = bank[5][:, 0:TE].rearrange("p (t e) -> p t e", e=E)
            total = bank[5][:, TE:2 * TE].rearrange("p (t e) -> p t e", e=E)
            chain(dve.tensor_copy(r_tot[:, :, :], total.rearrange("p t e -> p e t")))
            chain(dve.tensor_tensor_scan(r_cum[:, :, :].rearrange("p e t -> p (e t)"), ones[:, 0:TE],
                                         r_tot[:, :, :].rearrange("p e t -> p (e t)"), 0.0, ALU.mult, ALU.add))
            chain(dve.memset(r_prev[:, :], 0.0))
            chain(dve.tensor_copy(r_prev[:, 1:E], r_cum[:, 0:E - 1, NT - 1]))
            chain(dve.tensor_tensor(r_n[:, :], r_cum[:, :, NT - 1], r_prev[:, :], ALU.subtract))
            chain(dve.tensor_tensor(r_k[:, :, :], r_n[:, :].unsqueeze(2).broadcast_to([P, E, NT]),
                                    filled[:, :].unsqueeze(1).broadcast_to([P, E, NT]), ALU.is_gt))
            chain(dve.tensor_reduce(r_nt[:, :], r_k[:, :, :], AX, ALU.add))
            chain(dve.tensor_tensor_scan(r_end[:, :], ones[:, 0:E], r_nt[:, :], 0.0, ALU.mult, ALU.add))
            chain(dve.tensor_tensor(r_base[:, :], r_end[:, :], r_nt[:, :], ALU.subtract))
            chain(dve.scalar_tensor_tensor(r_base[:, :], r_base[:, :], float(P), r_prev[:, :], ALU.mult, ALU.subtract))
            chain(dve.tensor_tensor(r_lg[:, :, :], r_cum[:, :, :].rearrange("p e t -> p t e"), total, ALU.subtract))
            chain(dve.tensor_tensor(r_lg[:, :, :], r_lg[:, :, :], prefix, ALU.add))
            chain(dve.tensor_tensor(r_lg[:, :, :], r_lg[:, :, :], over_t(r_base[:, :]), ALU.add))
            chain(dve.tensor_tensor(r_lg[:, :, :], r_lg[:, :, :], r_oh[:, :, :], ALU.mult))
            chain(dve.tensor_reduce(posf[:, :], r_lg[:, :, :], AX, ALU.add))
            chain(dve.tensor_copy(pos[:, :], posf[:, :]))
            chain(dve.tensor_tensor(r_te[:, :, :], tile_at[:, :].unsqueeze(2).broadcast_to([P, SLOT_TILES, E]),
                                    r_end[:, :].unsqueeze(1).broadcast_to([P, SLOT_TILES, E]), ALU.is_ge))
            chain(dve.tensor_reduce(tile_ef[:, :], r_te[:, :, :], AX, ALU.add))
            dve.tensor_scalar(tile_e[:, :], tile_ef[:, :], float(E - 1), None, ALU.min).then_inc(route_done, 1)

            u_pair = pair[:, :, 0:2 * H1].rearrange("p k (c w) -> p k c w", c=2)

            def step(l, t):
                if w := at(l, t, 2, B, LB):
                    n, b, _ = w
                    dve.wait_ge(pe_gn, n + 1)
                    dve.tensor_copy(gn_m[:, :], bank[3][:, 0:2]).then_inc(gn_chain, 1)
                    dve.wait_ge(gn_chain, n * 4 + 1)
                    dve.scalar_tensor_tensor(gn_nv[:, :], gn_m[:, 0:1], gn_m[:, 0:1], gn_m[:, 1:2],
                                             ALU.mult, ALU.subtract).then_inc(gn_chain, 1)
                    dve.wait_ge(gn_chain, n * 4 + 2)
                    dve.tensor_scalar(gn_ve[:, :], gn_nv[:, :], -1.0, EPS, ALU.mult, ALU.add).then_inc(gn_var, 1)
                if w := at(l, t, 3, B, LB):
                    dve.wait_ge(pe_z, w[0] + 1)
                    ln_stats(w[0] + B, w[1], lambda c: bank[7][:, c * D:(c + 1) * D])
                if w := at(l, t, 2, B, LB):
                    n, b, _ = w
                    dve.wait_ge(gn_rstd, n + 1)
                    dve.tensor_tensor(gn_sc[:, :], gn_rs[:, :], par[:, GN_G:GN_G + 1], ALU.mult).then_inc(gn_chain, 1)
                    dve.tensor_tensor(gn_d[:, :], par[:, W2_B:W2_B + 1], gn_m[:, 0:1], ALU.subtract)\
                        .then_inc(gn_chain, 1)
                    dve.wait_ge(gn_chain, n * 4 + 4)
                    dve.scalar_tensor_tensor(gn_bi[:, :], gn_d[:, :], gn_sc[:, :], par[:, GN_B:GN_B + 1],
                                             ALU.mult, ALU.add).then_inc(gn_affine, 1)
                if w := at(l, t, 0, B, LB):
                    n, b, _ = w
                    dve.wait_ge(pe_S, n + 1)
                    dve.tensor_copy(S_sb[:, 0, :], pair[:, 1, 0:H1]).then_inc(S_part, 1)
                    for c in range(1, C - 1):
                        dve.wait_ge(S_part, n * (C - 2) + c)
                        dve.tensor_tensor(S_sb[:, c, :], pair[:, 1, c * H1:(c + 1) * H1], S_sb[:, c - 1, :], ALU.add)\
                            .then_inc(S_part if c < C - 2 else S_done, 1)
                if w := at(l, t, 3, B, LB):
                    n, b, _ = w
                    need(dve, hg_done, n - 1)
                    ln_apply(n + B, b, lambda c: zhat[:, b % 2, c, :], lambda c: bank[7][:, c * D:(c + 1) * D], z_done)
                if w := at(l, t, 0, B, LB):
                    n, b, _ = w
                    dve.wait_ge(pe_A, n + 1)
                    dve.tensor_tensor(A_sb[:, :, :], pair[:, 0, :].rearrange("p (c i) -> p c i", c=C),
                                      causal[:, :].unsqueeze(1).broadcast_to([P, C, P]), ALU.mult)\
                        .then_inc(A_done, 1)
                if w := at(l, t, 1, B, LB):
                    n, b, _ = w
                    dve.wait_ge(gg_done, n + 1)
                    dve.wait_ge(th_done, n + 1)
                    dve.scalar_tensor_tensor(gate_t[:, :], th_sb[:, :], 1.0, gg_sb[:, :], ALU.add, ALU.mult)\
                        .then_inc(gt_done, 1)
                    dve.wait_ge(gt_done, n + 1)
                    dve.wait_ge(pe_a, n + 1)
                    dve.scalar_tensor_tensor(act_sb[:, :], bank[2][:, :], par[:, VAL_B:VAL_B + 1], gate_t[:, :],
                                             ALU.add, ALU.mult).then_inc(act_done, 1)
                if w := at(l, t, 0, B, LB):
                    n, b, _ = w
                    dve.wait_ge(pe_u, n + 1)
                    row_sum = u_pair[:, :, :, D]
                    two = lambda v: v[:, :].rearrange("p (k c) -> p k c", k=2)
                    dve.tensor_tensor(two(rs1), row_sum, two(floor_sb), ALU.max).then_inc(u_chain, 1)
                    dve.wait_ge(u_chain, n * 3 + 1)
                    dve.scalar_tensor_tensor(two(rs2), row_sum, -1.0, two(rs1), ALU.mult, ALU.max)\
                        .then_inc(u_chain, 1)
                    dve.wait_ge(u_chain, n * 3 + 2)
                    dve.reciprocal(rs3[:, :], rs2[:, :]).then_inc(u_chain, 1)
                    dve.wait_ge(u_chain, n * 3 + 3)
                    dve.tensor_tensor(u_sb[:, :, :].rearrange("p (k c) d -> p k c d", k=2), u_pair[:, :, :, 0:D],
                                      rs3[:, :].rearrange("p (k c) -> p k c", k=2).unsqueeze(3)
                                      .broadcast_to([P, 2, C // 2, D]), ALU.mult).then_inc(u_done, 1)
                if w := at(l, t, 1, B, LB):
                    n, b, _ = w
                    dve.wait_ge(pe_w2, n + 1)
                    if b == 0:
                        dve.wait_ge(w2_set, w[2] + 1)
                    dve.bn_stats(gs_st[:, :], bank[6][:, :]).then_inc(gs_chain, 1)
                    alone(dve, gs_chain, n * 3 + 1)
                    dve.bn_aggr(gs_mv[:, :], gs_st[:, :]).then_inc(gs_chain, 1)
                    dve.wait_ge(gs_chain, n * 3 + 2)
                    dve.tensor_tensor(gs[:, 0:1], gs_mv[:, 0:1], par[:, W2_B:W2_B + 1], ALU.add).then_inc(gs_chain, 1)
                    dve.wait_ge(gs_chain, n * 3 + 3)
                    dve.scalar_tensor_tensor(gs[:, 1:2], gs[:, 0:1], gs[:, 0:1], gs_mv[:, 1:2], ALU.mult, ALU.add)\
                        .then_inc(gs_done, 1)

            steps(dve, step, L, B, LAG)

            dve.wait_ge(experts_in, 48)
            dve.wait_ge(bias1_in, 16)

            def tile_step(g, t):
                if w := at(g, t, 1, UN, SLOT_TILES):
                    n = w[0]
                    e = dve.value_load(tile_e[0:1, bass.ds(n, 1)], min_val=0, max_val=E - 1)
                    dve.wait_ge(pe_h, n + 1)
                    need(dve, h_done, n)
                    dve.tensor_tensor(h_in[:, :], bank[3][:, :], moe_b1[:, bass.ds(e, 1), :]
                                      .rearrange("p a f -> p (a f)"), ALU.add).then_inc(hb_done, 1)
                if w := at(g, t, 3, UN, SLOT_TILES):
                    n, i, k = w
                    e = dve.value_load(tile_e[0:1, bass.ds(n, 1)], min_val=0, max_val=E - 1)
                    dve.wait_ge(pe_y, n + 1)
                    if not (isinstance(n, int) and n < UN):
                        dve.wait_ge(yt_out[i], 16 * k)
                    dve.tensor_tensor(yt[i][:, :], bank[6][:, 0:D], moe_b2[:, bass.ds(e, 1), :]
                                      .rearrange("p a f -> p (a f)"), ALU.add).then_inc(yt_done, 1)
                if w := at(g, t, 0, UN, SLOT_TILES):
                    n = w[0]
                    dve.wait_ge(pe_xt, n + 1)
                    need(dve, pe_h, n)
                    dve.tensor_copy(xtT[:, :], bank[7][:, 0:P]).then_inc(xtT_done, 1)

            steps(dve, tile_step, SLOT_TILES // UN, UN, 3)

            for b in range(B):
                dve.wait_ge(yg_in[b % 2], 16 * (b // 2 + 1))
                need(dve, e_t, b)
                dve.tensor_tensor(h_in[:, :].rearrange("p (c d) -> p c d", c=C),
                                  yg[:, b % 2, :].rearrange("p (c d) -> p c d", c=C),
                                  weight[:, b * C:(b + 1) * C].unsqueeze(2).broadcast_to([P, C, D]), ALU.mult)\
                    .then_inc(e_f, 1)
                dve.wait_ge(e_f, b + 1)
                dve.wait_ge(e_th, b + 1)
                dve.scalar_tensor_tensor(gate_t[:, :], h_act[:, :], 1.0, h_in[:, :], ALU.add, ALU.mult).then_inc(e_t, 1)
                dve.wait_ge(e_t, b + 1)
                need(dve, e_o, b - 1)
                dve.scalar_tensor_tensor((u_sb if b % 2 else A_sb)[:, :, :],
                                         gate_t[:, :].rearrange("p (c d) -> p c d", c=C), 0.5,
                                         htok[:, b * C:(b + 1) * C, 0:D], ALU.mult, ALU.mult).then_inc(e_s, 1)

        @block.tensor
        def _(pe):
            mm = nc.tensor.matmul
            pe.wait_ge(const_made, 6)
            pe.wait_ge(rows_in, 16 * 8)
            pe.transpose(bank[6][:, 0:NROWS], rows[:, :], ident[0:NROWS, 0:NROWS]).then_inc(pe_rows, 1)
            pe.wait_ge(kqv_in, 16)
            pe.wait_ge(m1_in, 16)
            pe.wait_ge(f1_in, 16)
            for l in range(L):
                need(pe, wT_done, l)
                for j, part in enumerate((1, 0, 2)):
                    last = pe.transpose(bank[2][:, j * D:(j + 1) * D], wkqv_sb[:, l, part * D:(part + 1) * D],
                                        ident[:, :])
                last.then_inc(pe_wT, 1)
                pe.wait_ge(wT_done, l + 1)
                if l:
                    pe.wait_ge(prod_done, l)
                else:
                    pe.wait_ge(rows_done, 1)
                mm(bank[4][:, 0:D], wT_sb[:, 0:D], wT_sb[:, D:2 * D], start=True, stop=True)
                mm(bank[4][:, D:3 * D], wT_sb[:, 2 * D:3 * D], wm1_sb[:, l, :], start=True, stop=True)
                for k in range(2):
                    last = mm(bank[4][:, 3 * D + k:3 * D + k + 1], all_f1[:, l, k * D:(k + 1) * D],
                              rowsT[:, R_BF2 + l:R_BF2 + l + 1], start=True, stop=True)
                last.then_inc(pe_prod, 1)
            pe.wait_ge(small_in, 32)
            for b in range(B + 1):
                if b < B:
                    pe.wait_ge(xn_done, b + 1)
                    need(pe, xT_done, b - 1)
                    for c in range(C):
                        last = pe.transpose(pair[:, b % 2, c * P:(c + 1) * P], xn[:, b * C + c, 0:D], ident[:, :])
                    last.then_inc(pe_xT, 1)
                if b:
                    pe.wait_ge(xT_done, b)
                    for c in range(C):
                        k = (b - 1) * C + c
                        last = mm(bank[7][:, k * E:(k + 1) * E], hT[:, b - 1, c * P:(c + 1) * P], gate_sb[:, :],
                                  start=True, stop=True)
                    last.then_inc(pe_gate, 1)
            pe.wait_ge(r_shift, 2)
            oh = r_oh[:, :, :].rearrange("p t e -> p (t e)")
            mm(bank[5][:, 0:TE], before[:, :], oh, start=True, stop=True)
            mm(bank[5][:, TE:2 * TE], ones[:, 0:P], oh, start=True, stop=True).then_inc(pe_prefix, 1)
            pe.wait_ge(col_made, 2)

            def step(l, t):
                first = isinstance(l, int) and l == 0
                if w := at(l, t, 0, B, LB):
                    n, b, _ = w
                    tok = (lambda c: xn[:, b * C + c, 0:H1]) if first else (lambda c: htok[:, b * C + c, :])
                    if b == 0:
                        pe.wait_ge(m_set, w[2] + 1)
                    if not first:
                        pe.wait_ge(htok_done, n - B + 1)
                        pe.wait_ge(hT_done, n - B + 1)
                    need(pe, u_done, n)
                    for c in range(C - 1):
                        last = mm(pair[:, 1, c * H1:(c + 1) * H1], tok(c)[:, 0:D], tok(c), start=True, stop=True)
                    last.then_inc(pe_S, 1)
                    mm(pair[:, 0, :], m_l[:, :], hT[:, b, :], start=True, stop=True).then_inc(pe_q, 1)
                if w := at(l, t, 1, B, LB):
                    n, b, _ = w
                    pe.wait_ge(uT_done, n + 1)
                    if b == 0:
                        pe.wait_ge(w_set, w[2] + 1)
                    need(pe, gn_chain, 4 * n - 3)
                    mm(bank[3][:, :], w_l[:, D:2 * D], uT_sb[:, :], start=True, stop=True).then_inc(pe_g, 1)
                    mm(bank[2][:, :], w_l[:, 0:D], uT_sb[:, :], start=True, stop=True).then_inc(pe_a, 1)
                if w := at(l, t, 0, B, LB):
                    n, b, _ = w
                    pe.wait_ge(q_done, n + 1)
                    for c in range(C):
                        at_c = slice(c * P, (c + 1) * P)
                        last = mm(pair[:, 0, at_c], hT[:, b, at_c], q_sb[:, at_c], start=True, stop=True)
                    last.then_inc(pe_A, 1)
                if w := at(l, t, 3, B, LB):
                    n, b, _ = w
                    pe.wait_ge(z_done, n + 1)
                    need(pe, S_done, n + LAG + 1 if not (isinstance(n, int) and n + LAG >= LB) else LB)
                    need(pe, u_done, n + LAG if not (isinstance(n, int) and n + LAG >= LB) else LB)
                    for c in range(C):
                        last = pe.transpose(pair[:, 1, c * P:(c + 1) * P], zhat[:, b % 2, c, :], ident[:, :])
                    last.then_inc(pe_zT, 1)
                if w := at(l, t, 2, B, LB):
                    n, b, _ = w
                    pe.wait_ge(y_done, n + 1)
                    if b == 0:
                        pe.wait_ge(f_set, w[2] + 1)
                    need(pe, G_done, 2 * n)
                    for k in range(2):
                        mm(bank[4 + k][:, :], f1_l[:, k * D:(k + 1) * D], y_sb[:, :], start=True, stop=True)\
                            .then_inc(pe_f1, 1)
                if w := at(l, t, 0, B, LB):
                    n, b, _ = w
                    tok = (lambda c: xn[:, b * C + c, 0:H1]) if first else (lambda c: htok[:, b * C + c, :])
                    pe.wait_ge(A_done, n + 1)
                    pe.wait_ge(S_done, n + 1)
                    need(pe, hT_done, n - LAG + 1)
                    for c in range(C):
                        dst = pair[:, c // 2, (c % 2) * H1:(c % 2 + 1) * H1]
                        last = mm(dst, A_sb[:, c, :], tok(c), start=True, stop=c == 0)
                        if c:
                            last = mm(dst, q_sb[:, c * P:(c + 1) * P], S_sb[:, c - 1, :], start=False, stop=True)
                    last.then_inc(pe_u, 1)
                if w := at(l, t, 1, B, LB):
                    n, b, _ = w
                    pe.wait_ge(act_done, n + 1)
                    if b == 0:
                        pe.wait_ge(w2_set, w[2] + 1)
                    need(pe, gn_done, n)
                    mm(bank[6][:, :], w2_l[:, :], act_sb[:, :], start=True, stop=True).then_inc(pe_w2, 1)
                if w := at(l, t, 2, B, LB):
                    n, b, _ = w
                    need(pe, z_done, n)
                    pe.wait_ge(G_done, 2 * n + 2)
                    for c in range(C):
                        at_c = slice(c * P, (c + 1) * P)
                        mm(bank[7][:, at_c], y_sb[:, at_c], ident[:, :], start=True, stop=False, is_transpose=TR)
                        for k in range(2):
                            last = mm(bank[7][:, at_c], G_sb[:, k, at_c], f2_l[:, k, :], start=False, stop=k == 1)
                    last.then_inc(pe_z, 1)
                if w := at(l, t, 0, B, LB):
                    n, b, _ = w
                    pe.wait_ge(u_done, n + 1)
                    need(pe, act_done, n)
                    for c in range(C):
                        last = pe.transpose(bank[2][:, c * P:(c + 1) * P], u_sb[:, c, :], ident[:, :])
                    last.then_inc(pe_uT, 1)
                if w := at(l, t, 1, B, LB):
                    n, b, _ = w
                    pe.wait_ge(gs_done, n + 1)
                    pe.wait_ge(th_done, n + 1)
                    pe.wait_ge(gg_done, n + 1)
                    mm(bank[3][:, 0:2], mean_of[:, :], gs[:, :], start=True, stop=True).then_inc(pe_gn, 1)

            steps(pe, step, L, B, LAG)

            pe.wait_ge(experts_in, 48)
            pe.wait_ge(hT_done, LB)
            pe.wait_ge(route_done, 1)

            def tile_step(g, t):
                if w := at(g, t, 1, UN, SLOT_TILES):
                    n = w[0]
                    e = pe.value_load(tile_e[0:1, bass.ds(n, 1)], min_val=0, max_val=E - 1)
                    pe.wait_ge(xtT_done, n + 1)
                    need(pe, hb_done, n)
                    mm(bank[3][:, :], xtT[:, :], moe_w1[:, bass.ds(e, 1), :].rearrange("p a f -> p (a f)"),
                       start=True, stop=True).then_inc(pe_h, 1)
                if w := at(g, t, 3, UN, SLOT_TILES):
                    n = w[0]
                    e = pe.value_load(tile_e[0:1, bass.ds(n, 1)], min_val=0, max_val=E - 1)
                    pe.wait_ge(hT_copied, n + 1)
                    need(pe, yt_done, n)
                    for k in range(KF):
                        last = mm(bank[6][:, 0:D], h_T[:, k * P:(k + 1) * P],
                                  moe_w2[:, bass.ds(e, 1), k, :].rearrange("p a d -> p (a d)"),
                                  start=k == 0, stop=k == KF - 1)
                    last.then_inc(pe_y, 1)
                if w := at(g, t, 2, UN, SLOT_TILES):
                    n = w[0]
                    pe.wait_ge(h_done, n + 1)
                    need(pe, hT_copied, n)
                    for k in range(KF):
                        last = pe.transpose(bank[4][:, k * P:(k + 1) * P], h_act[:, k * P:(k + 1) * P], ident[:, :])
                    last.then_inc(pe_hT, 1)
                if w := at(g, t, 0, UN, SLOT_TILES):
                    n, i, k = w
                    pe.wait_ge(xt_in[i], 16 * (k + 1))
                    need(pe, xtT_done, n)
                    pe.transpose(bank[7][:, 0:P], xt[i][:, 0:D], ident[:, :]).then_inc(pe_xt, 1)

            steps(pe, tile_step, SLOT_TILES // UN, UN, 3)


TR = True

_INS = ['L0_attn_x', 'L0_attn_Wkqv', 'L0_attn_Wm1', 'L0_attn_bm1', 'L0_attn_Wm2', 'L0_attn_bm2', 'L0_attn_gn_g',
        'L0_attn_gn_b', 'L0_attn_Wf1', 'L0_attn_bf1', 'L0_attn_Wf2', 'L0_attn_bf2', 'L0_attn_ln_g', 'L0_attn_ln_b',
        'L0_ffn_gate_w', 'L0_ffn_w1', 'L0_ffn_b1', 'L0_ffn_w2', 'L0_ffn_b2']


def kernel(**inputs):
    import numpy as np
    import concourse.bacc as bacc
    from concourse import mybir as mb
    from concourse.bass_utils import run_bass_kernel_spmd

    nc = bacc.Bacc("TRN2", target_bir_lowering=False, num_devices=1)
    arrays, args = {}, []
    for name in _INS:
        a = np.ascontiguousarray(inputs[name])
        arrays[f"in_{name}"] = a
        args.append(nc.dram_tensor(f"in_{name}", a.shape, mb.dt.from_np(a.dtype), kind="ExternalInput").ap())
    B, S, D = inputs['L0_attn_x'].shape
    i = np.arange(S, dtype=np.float32).reshape(S // 128, 128).T
    arrays["row_floor"] = np.ascontiguousarray(np.sqrt(np.float32(D)) * (1 + np.sqrt(i))).astype(np.float32)
    args.append(nc.dram_tensor("row_floor", arrays["row_floor"].shape, mb.dt.float32, kind="ExternalInput").ap())
    out = nc.dram_tensor("out", (B, S, D), mb.dt.float32, kind="ExternalOutput").ap()
    retention_moe_kernel(nc, *args, out)
    r = run_bass_kernel_spmd(nc, [arrays], core_ids=[0])
    return r.results[0]["out"]
```

```python
import concourse.bass as bass
from concourse import mybir
from contextlib import ExitStack



def retention_moe_kernel(nc, x, Wkqv, Wm1, bm1, Wm2, bm2, gn_g, gn_b, Wf1, bf1, Wf2, bf2, ln_g, ln_b,
                         gate_w, w1, b1, w2, b2, row_floor, out):
    f32 = mybir.dt.float32
    i32 = mybir.dt.int32
    u32 = mybir.dt.uint32
    ALU = mybir.AluOpType
    ACT = mybir.ActivationFunctionType
    AX = mybir.AxisListType.X

    B, S, D = x.shape
    L = Wkqv.shape[0]
    E, FF = w1.shape[0], w1.shape[2]
    P = 128
    C = S // P
    KF = FF // P
    NT = B * C
    TOK = B * S
    SLOT_TILES = (TOK + E * (P - 1)) // P
    H1 = D + 1
    ROW = D + 2
    EPS = 1e-5
    TILE_LAG = 3
    TURN_TILES = SLOT_TILES // (L - 1)
    TILES = SLOT_TILES + TILE_LAG
    assert D == P and SLOT_TILES % (L - 1) == 0 and KF == C and B == 2 * L and TURN_TILES == 13

    x_slots = nc.dram_tensor("x_slots", [TILES * P, ROW], f32, kind="Internal").ap()
    y_rows = nc.dram_tensor("y_rows", [TOK + TILES * P, D], f32, kind="Internal").ap()

    ctx = ExitStack()
    with ctx:
        def sb(name, shape, dt=f32):
            return ctx.enter_context(nc.sbuf_tensor(name, shape, dt))

        def sem(name):
            return ctx.enter_context(nc.semaphore(name))

        pair = ctx.enter_context(nc.psum_tensor("pair", [P, 2, 512], f32))
        bank = {k: ctx.enter_context(nc.psum_tensor(f"bank{k}", [P, 512], f32)) for k in range(2, 8)}

        x_sb = sb("x_sb", [P, NT, D])
        xn = sb("xn", [P, NT, ROW])
        htok = sb("htok", [P, NT, H1])
        hT = sb("hT", [P, B, S])
        moe_w1 = sb("moe_w1", [P, E, FF])
        moe_w2 = sb("moe_w2", [P, E, KF, D])
        moe_b1 = sb("moe_b1", [P, E, FF])
        moe_b2 = sb("moe_b2", [P, E, D])
        next_m = sb("next_m", [P, L, D])
        all_w = sb("all_w", [P, L, 2 * D])
        all_w2 = sb("all_w2", [P, L, D])
        all_f1 = sb("all_f1", [P, L, 2 * D])
        all_f2 = sb("all_f2", [P, L, 2, D])
        all_lg = sb("all_lg", [P, L, D])
        all_lb = sb("all_lb", [P, L, D])
        NPAR = 9
        GATE_B, VAL_B, W2_B, GN_G, GN_B, F_B, LN_G, LN_B = 0, 1, 2, 3, 4, 5, 7, 8
        all_par = sb("all_par", [P, L, NPAR])
        m_l = sb("m_l", [P, D])
        w_l = sb("w_l", [P, 2 * D])
        w2_l = sb("w2_l", [P, D])
        f1_l = sb("f1_l", [P, 2 * D])
        f2_l = sb("f2_l", [P, 2, D])
        lg_l = sb("lg_l", [P, D])
        lb_l = sb("lb_l", [P, D])
        par = sb("par", [P, NPAR])
        ident = sb("ident", [P, P])
        causal = sb("causal", [P, P])
        before = sb("before", [P, P])
        ones = sb("ones", [P, 2 * P])
        mean_of = sb("mean_of", [P, P])
        half_neg = sb("half_neg", [P, C])
        floor_sb = sb("floor_sb", [P, C])
        gate_sb = sb("gate_sb", [P, E])
        q_sb = sb("q_sb", [P, S])
        A_sb = sb("A_sb", [P, C, P])
        S_sb = sb("S_sb", [P, C - 1, H1])
        u_sb = sb("u_sb", [P, C, D])
        uT_sb = sb("uT_sb", [P, S])
        gg_sb = sb("gg_sb", [P, S])
        th_sb = sb("th_sb", [P, S])
        gate_t = sb("gate_t", [P, S])
        act_sb = sb("act_sb", [P, S])
        gn_sb = sb("gn_sb", [P, S])
        y_sb = sb("y_sb", [P, S])
        G_sb = sb("G_sb", [P, 2, S])
        zhat = sb("zhat", [P, 2, C, D])
        hg = sb("hg", [P, C, D])
        rs1 = sb("rs1", [P, C])
        rs2 = sb("rs2", [P, C])
        rs3 = sb("rs3", [P, C])
        ln_st = sb("ln_st", [P, 2, C, 6])
        ln_mv = sb("ln_mv", [P, 2, C, 2])
        ln_ve = sb("ln_ve", [P, 2, C])
        ln_rs = sb("ln_rs", [P, 2, C])
        ln_nb = sb("ln_nb", [P, 2, C])
        x_st = sb("x_st", [P, NT, 6])
        x_mv = sb("x_mv", [P, NT, 2])
        x_ve = sb("x_ve", [P, NT])
        x_rs = sb("x_rs", [P, NT])
        x_nb = sb("x_nb", [P, NT])
        gs_st = sb("gs_st", [P, 6])
        gs_mv = sb("gs_mv", [P, 2])
        gs = sb("gs", [P, 2])
        gn_m = sb("gn_m", [P, 2])
        gn_nv = sb("gn_nv", [P, 1])
        gn_ve = sb("gn_ve", [P, 1])
        gn_rs = sb("gn_rs", [P, 1])
        gn_sc = sb("gn_sc", [P, 1])
        gn_d = sb("gn_d", [P, 1])
        gn_bi = sb("gn_bi", [P, 1])

        NROWS = 10 * L
        R_BM1, R_BM2, R_GG, R_GB, R_BF1, R_BF2, R_LG, R_LB = (L * k for k in (0, 2, 3, 4, 5, 7, 8, 9))
        rows = sb("rows", [NROWS, P])
        rowsT = sb("rowsT", [P, NROWS])
        wkqv_sb = moe_b1[:, 0:3, :].rearrange("p e f -> p (e f)").rearrange("p (l f) -> p l f", l=L)
        wm1_sb = moe_b1[:, 3:5, :].rearrange("p e f -> p (e f)").rearrange("p (l f) -> p l f", l=L)
        wT_sb = [moe_b1[:, 5 + i, 0:3 * D] for i in range(2)]
        fill = moe_b1[:, 7, 0:H1]
        fill_id = sb("fill_id", [P, TILES], i32)
        TE = NT * E
        r_lg = sb("r_lg", [P, NT, E])
        r_a = sb("r_a", [P, NT, E])
        r_c = sb("r_c", [P, NT, E])
        r_oh = sb("r_oh", [P, NT, E])
        r_tot = sb("r_tot", [P, E, NT])
        r_cum = sb("r_cum", [P, E, NT])
        r_mx = sb("r_mx", [P, NT])
        r_ix = sb("r_ix", [P, NT])
        r_sum = sb("r_sum", [P, NT])
        weight = sb("weight", [P, NT])
        posf = sb("posf", [P, NT])
        pos = sb("pos", [P, NT], i32)
        iota_e = sb("iota_e", [P, E])
        tile_at = sb("tile_at", [P, TILES])
        filled = sb("filled", [P, NT])
        r_prev = sb("r_prev", [P, E])
        r_n = sb("r_n", [P, E])
        r_nt = sb("r_nt", [P, E])
        r_end = sb("r_end", [P, E])
        r_base = sb("r_base", [P, E])
        r_k = sb("r_k", [P, E, NT])
        r_te = sb("r_te", [P, TILES, E])
        tile_ef = sb("tile_ef", [P, TILES])
        tile_e = sb("tile_e", [P, TILES], i32)
        xt = [sb(f"xt{i}", [P, ROW]) for i in range(5)]
        yt = [sb(f"yt{i}", [P, D]) for i in range(5)]
        tile_ids = [sb(f"tile_ids{i}", [P, 1], i32) for i in range(5)]
        slot_ids = sb("slot_ids", [P, TILES], i32)
        xtT = sb("xtT", [P, P])
        h_in = sb("h_in", [P, FF])
        h_act = sb("h_act", [P, FF])
        h_T = sb("h_T", [P, FF])
        half_w = sb("half_w", [P, NT])
        y_tok = moe_w1
        th_y = xn

        x_in = [sem(f"x_in{b}") for b in range(B)]
        kqv_in, m1_in, rows_in, gate_in, floor_in = sem("kqv_in"), sem("m1_in"), sem("rows_in"), sem("gate_in"), sem("floor_in")
        w2_in, f1_in, f2_in, ln_in = sem("w2_in"), sem("f1_in"), sem("f2_in"), sem("ln_in")
        experts_in, bias1_in = sem("experts_in"), sem("bias1_in")
        const_made = sem("const_made")
        fill_made, filled_out = sem("fill_made"), sem("filled_out")
        col_made, ids_made = sem("col_made"), sem("ids_made")
        ln_chain, ln_var, ln_rstd = sem("ln_chain"), sem("ln_var"), sem("ln_rstd")
        ln_shift = sem("ln_shift")
        x_chain, x_var, x_rstd, x_shift = sem("x_chain"), sem("x_var"), sem("x_rstd"), sem("x_shift")
        xn_last = sem("xn_last")
        xn_done, pe_xT, xT_done, pe_gate = sem("xn_done"), sem("pe_xT"), sem("xT_done"), sem("pe_gate")
        pe_wT, wT_done, pe_prod, prod_done = sem("pe_wT"), sem("wT_done"), sem("pe_prod"), sem("prod_done")
        pe_rows, rows_done, pe_fb, fb_done = sem("pe_rows"), sem("rows_done"), sem("pe_fb"), sem("fb_done")
        par_done = sem("par_done")
        r_step, r_exp, pe_prefix, route_done = sem("r_step"), sem("r_exp"), sem("pe_prefix"), sem("route_done")
        slots_found = sem("slots_found")
        r_shift = sem("r_shift")
        scattered = sem("scattered")
        m_set, w_set, w2_set = sem("m_set"), sem("w_set"), sem("w2_set")
        f1_set, f2_set, ln_set = sem("f1_set"), sem("f2_set"), sem("ln_set")
        pe_S, pe_q, pe_A, pe_u, pe_uT = sem("pe_S"), sem("pe_q"), sem("pe_A"), sem("pe_u"), sem("pe_uT")
        pe_g, pe_a, pe_w2, pe_gn, pe_f1 = sem("pe_g"), sem("pe_a"), sem("pe_w2"), sem("pe_gn"), sem("pe_f1")
        pe_z, pe_zT = sem("pe_z"), sem("pe_zT")
        S_part, S_done, q_done, A_done = sem("S_part"), sem("S_done"), sem("q_done"), sem("A_done")
        u_chain, u_done, uT_done = sem("u_chain"), sem("u_done"), sem("uT_done")
        gg_done, th_done, gt_done, act_done = sem("gg_done"), sem("th_done"), sem("gt_done"), sem("act_done")
        gs_chain, gs_done = sem("gs_chain"), sem("gs_done")
        gn_chain, gn_var, gn_rstd, gn_affine = sem("gn_chain"), sem("gn_var"), sem("gn_rstd"), sem("gn_affine")
        gn_done, y_done, G_done = sem("gn_done"), sem("y_done"), sem("G_done")
        z_half = sem("z_half")
        z_done, hg_done, htok_done, hT_done = sem("z_done"), sem("hg_done"), sem("htok_done"), sem("hT_done")
        xt_in = [sem(f"xt_in{i}") for i in range(5)]
        yt_out = [sem(f"yt_out{i}") for i in range(5)]
        yt_zeroed = sem("yt_zeroed")
        ids_in, ids_set = sem("ids_in"), sem("ids_set")
        pe_xt, xtT_done, pe_h, hb_done, h_done = sem("pe_xt"), sem("xtT_done"), sem("pe_h"), sem("hb_done"), sem("h_done")
        pe_hT, hT_copied, pe_y, yt_done = sem("pe_hT"), sem("hT_copied"), sem("pe_y"), sem("yt_done")
        y_in = [sem(f"y_in{b}") for b in range(B)]
        e_half, e_th, e_silu, e_weighed = sem("e_half"), sem("e_th"), sem("e_silu"), sem("e_weighed")
        e_s, e_last, dve_out, pool_out = sem("e_s"), sem("e_last"), sem("dve_out"), sem("pool_out")
        out_done, passed = sem("out_done"), sem("passed")

        block = ctx.enter_context(nc.Block())

        def need(eng, s, v):
            if not isinstance(v, int) or v > 0:
                eng.wait_ge(s, v)

        def alone(eng, s, v):
            eng.wait_ge(s, v)
            if not isinstance(v, int):
                eng.sem_inc(passed, 1)

        def steps(eng, step, turns, width, lag):
            for t in range(width):
                step(0, t)
            with eng.Fori(1, turns) as l:
                for t in range(width):
                    step(l, t)
            for t in range(lag):
                step(turns, t)

        def at(l, t, late, width, count):
            b, l = (t - late) % width, l + (t - late) // width
            if isinstance(l, int) and (l < 0 or l * width + b >= count):
                return None
            return l * width + b, b, l

        LB = L * B
        LAG = 3

        EARLY, LATE, LAST = range(3)
        FIRST_TURNS = [(B - 1, EARLY), (B - 1, LATE), (B - 1, LAST)]
        TURNS = [[LATE] if t in (0, 3, 5) else [EARLY, LATE] for t in range(B)]
        assert sum(map(len, TURNS)) == TURN_TILES

        def turn(l, t, place):
            if isinstance(l, int) and (l == 0 or l >= L):
                if l == 0 and (t, place) in FIRST_TURNS:
                    j = FIRST_TURNS.index((t, place))
                    return j, TURN_TILES - TILE_LAG + j
                return None
            if place not in TURNS[t]:
                return None
            k = sum(map(len, TURNS[:t])) + TURNS[t].index(place)
            return (l - 1) * TURN_TILES + TILE_LAG + k, k

        def turns_before(l, t, place):
            if isinstance(l, int) and l == 0:
                return sum(at < (t, place) for at in FIRST_TURNS)
            if isinstance(l, int) and l >= L:
                return TILES
            k = sum(map(len, TURNS[:t])) + sum(p < place for p in TURNS[t])
            return (l - 1) * TURN_TILES + TILE_LAG + k

        def expert(eng, loaded, j, k, behind):
            if behind == TILE_LAG and k >= 2:
                return loaded[k - 2]
            e = eng.value_load(tile_e[0:1, bass.ds(j - behind, 1)], min_val=0, max_val=E - 1)
            if behind == 1:
                loaded[k] = e
            return e

        def halves(l, t):
            return (0, 1) if turn(l, t, EARLY) else (1, 0)

        def first_turns(j):
            return isinstance(j, int) and j < TILE_LAG

        def buffer_of(k):
            return k % 4 if k < 12 else 4

        def used_before(l, k):
            return (l - 1) * (3 if k < 12 else 1) + (k // 4 if k < 12 else 0)

        LAST_B = B - 1
        ORDER = [LAST_B] + list(range(B - 1))
        DVE_OUT = [0, 1, LAST_B, 5, 6]
        POOL_OUT = [2, 3, 4]
        assert sorted(DVE_OUT + POOL_OUT) == list(range(B))

        def nth(order, b):
            return order.index(b) + 1

        @block.sync
        def _(sp):
            def load_x(b):
                sp.dma_start(x_sb[:, b * C:(b + 1) * C, :],
                             x[b].rearrange("(c p) d -> p c d", p=P)).then_inc(x_in[b], 16)

            load_x(0)
            load_x(1)
            sp.dma_start(wm1_sb, Wm1.rearrange("l p f -> p l f")).then_inc(m1_in, 16)
            for b in range(2, 6):
                load_x(b)
            sp.dma_start(gate_sb[:, :], gate_w).then_inc(gate_in, 16)
            load_x(6)
            load_x(7)
            for v, r in ((bm1.rearrange("l (k p) -> (l k) p", p=P), R_BM1), (bm2, R_BM2), (gn_g, R_GG),
                         (gn_b, R_GB), (bf1.rearrange("l (k p) -> (l k) p", p=P), R_BF1), (bf2, R_BF2),
                         (ln_g, R_LG), (ln_b, R_LB)):
                sp.dma_start(rows[r:r + v.shape[0], :], v).then_inc(rows_in, 16)
            sp.dma_start(all_f1[:, :, :], Wf1.rearrange("l p f -> p l f")).then_inc(f1_in, 16)
            sp.dma_start(floor_sb[:, :], row_floor).then_inc(floor_in, 16)
            sp.dma_start(all_w2[:, :, :], Wm2.rearrange("l p d -> p l d")).then_inc(w2_in, 16)
            sp.dma_start(all_f2[:, :, :, :].rearrange("p l k d -> p (l k) d"),
                         Wf2.rearrange("l (k p) d -> p (l k) d", p=P)).then_inc(f2_in, 16)
            sp.dma_start(all_lg[:, :, :], ln_g.partition_broadcast(P)).then_inc(ln_in, 16)
            sp.dma_start(all_lb[:, :, :], ln_b.partition_broadcast(P)).then_inc(ln_in, 16)
            sp.wait_ge(fill_made, 2)
            slots = x_slots.rearrange("(t p) w -> p t w", p=P)
            sp.dma_start(slots[:, :, 0:H1],
                         fill.unsqueeze(1).broadcast_to([P, TILES, H1])).then_inc(filled_out, 16)
            with nc.allow_non_contiguous_dma(reason="one word a slot"):
                sp.dma_start(slots[:, :, H1:ROW].rearrange("p t w -> p (t w)"),
                             fill_id[:, :].bitcast(f32)).then_inc(filled_out, 16)
            sp.dma_start(moe_w1[:, :, :], w1.rearrange("e p f -> p e f")).then_inc(experts_in, 16)
            sp.dma_start(moe_w2[:, :, :, :].rearrange("p e k d -> p (e k) d"),
                         w2.rearrange("e (k p) d -> p (e k) d", p=P)).then_inc(experts_in, 16)
            sp.dma_start(moe_b2[:, :, :], b2.partition_broadcast(P)).then_inc(experts_in, 16)
            sp.wait_ge(prod_done, L)
            sp.wait_ge(filled_out, 32)
            sp.dma_start(moe_b1[:, :, :], b1.partition_broadcast(P)).then_inc(bias1_in, 16)
            sp.wait_ge(scattered, 16 * NT)

            def load_tile(j, k):
                if not isinstance(j, int):
                    alone(sp, pe_xt, j - TILE_LAG + 1)
                q = buffer_of(k)
                sp.dma_start(xt[q][:, :], x_slots[bass.ds(j * P, P), :]).then_inc(xt_in[q], 16)

            for j in range(TILE_LAG):
                load_tile(j, TURN_TILES - TILE_LAG + j)
            with nc.allow_non_contiguous_dma(reason="one word a slot"):
                sp.dma_start(slot_ids[:, :].bitcast(f32), slots[:, :, H1:ROW].rearrange("p t w -> p (t w)"))\
                    .then_inc(ids_in, 16)
            with sp.Fori(1, L) as l:
                for k in range(TURN_TILES):
                    load_tile((l - 1) * TURN_TILES + TILE_LAG + k, k)
            for q in range(5):
                sp.wait_ge(yt_out[q], 16 * (1 + used_before(L, q if q < 4 else 12)))
            sp.wait_ge(pe_h, TILES - 1)
            for b in ORDER:
                sp.dma_start(y_tok[:, b, :].rearrange("p (c d) -> p c d", c=C),
                             y_rows[b * S:(b + 1) * S, :].rearrange("(c p) d -> p c d", p=P)).then_inc(y_in[b], 16)
            for b in (0, 1, LAST_B, 2, 3, 5, 4, 6):
                if b in DVE_OUT:
                    sp.wait_ge(dve_out, nth(DVE_OUT, b))
                else:
                    sp.wait_ge(pool_out, nth(POOL_OUT, b))
                sp.dma_start(out[b].rearrange("(c p) d -> p c d", p=P),
                             y_tok[:, b, :].rearrange("p (c d) -> p c d", c=C)).then_inc(out_done, 16)
            sp.wait_ge(out_done, 16 * B)

        @block.gpsimd
        def _(pool):
            pool.memset(ones[:, :], 1.0).then_inc(const_made, 1)
            pool.memset(half_neg[:, :], -0.5).then_inc(const_made, 1)
            pool.memset(mean_of[:, :], 1.0 / D).then_inc(const_made, 1)
            pool.wait_ge(const_made, 1)
            pool.affine_select(out=ident[:, :], in_=ones[:, 0:P], compare_op=ALU.is_equal, fill=0.0, base=0,
                               pattern=[[-1, P]], channel_multiplier=1).then_inc(const_made, 1)
            pool.affine_select(out=causal[:, :], in_=ones[:, 0:P], compare_op=ALU.is_ge, fill=0.0, base=0,
                               pattern=[[1, P]], channel_multiplier=-1).then_inc(const_made, 1)
            pool.affine_select(out=before[:, :], in_=ones[:, 0:P], compare_op=ALU.is_gt, fill=0.0, base=0,
                               pattern=[[1, P]], channel_multiplier=-1).then_inc(const_made, 1)
            pool.memset(fill, 0.0).then_inc(fill_made, 1)
            pool.iota(fill_id[:, :], pattern=[[P, TILES]], base=TOK, channel_multiplier=1)\
                .then_inc(fill_made, 1)
            pool.memset(xn[:, :, D:H1], 1.0).then_inc(col_made, 1)
            pool.memset(htok[:, :, D:H1], 1.0).then_inc(col_made, 1)
            pool.iota(xn[:, :, H1:ROW].rearrange("p t w -> p (t w)").bitcast(i32), pattern=[[P, NT]],
                      base=0, channel_multiplier=1).then_inc(ids_made, 1)
            pool.iota(iota_e[:, :], pattern=[[1, E]], base=-E, channel_multiplier=0,
                      allow_small_or_imprecise_dtypes=True).then_inc(ids_made, 1)
            pool.iota(tile_at[:, :], pattern=[[1, TILES]], base=0, channel_multiplier=0,
                      allow_small_or_imprecise_dtypes=True).then_inc(ids_made, 1)
            pool.iota(filled[:, :], pattern=[[P, NT]], base=0, channel_multiplier=0,
                      allow_small_or_imprecise_dtypes=True).then_inc(ids_made, 1)

            def ln_pow(k, b):
                pool.wait_ge(ln_var, k + 1)
                pool.tensor_tensor(ln_rs[:, b % 2, :], ln_ve[:, b % 2, :], half_neg[:, :], ALU.pow)\
                    .then_inc(ln_rstd, 1)

            pool.wait_ge(const_made, 6)
            for b in range(B):
                of_b = slice(b * C, (b + 1) * C)
                pool.wait_ge(x_var, b + 1)
                pool.tensor_tensor(x_rs[:, of_b], x_ve[:, of_b], half_neg[:, :], ALU.pow).then_inc(x_rstd, 1)

            def set_m(l):
                need(pool, pe_q, (l + 1) * B)
                pool.tensor_copy(m_l[:, :], next_m[:, l, :]).then_inc(m_set, 1)

            def set_w(l):
                need(pool, pe_a, l * B)
                need(pool, th_done, l * B)
                need(pool, gg_done, l * B)
                need(pool, act_done, l * B)
                pool.tensor_copy(par[:, GATE_B:VAL_B + 1], all_par[:, l, GATE_B:VAL_B + 1])
                pool.tensor_copy(w_l[:, :], all_w[:, l, :]).then_inc(w_set, 1)

            def set_w2(l):
                need(pool, pe_w2, l * B)
                need(pool, gn_affine, l * B)
                pool.tensor_copy(w2_l[:, :], all_w2[:, l, :])
                pool.tensor_copy(par[:, W2_B:GN_B + 1], all_par[:, l, W2_B:GN_B + 1]).then_inc(w2_set, 1)

            def set_f1(l):
                need(pool, G_done, l * B * 2)
                if isinstance(l, int) and l == 0:
                    pool.wait_ge(fb_done, 1)
                pool.tensor_copy(par[:, F_B:F_B + 2], all_par[:, l, F_B:F_B + 2])
                pool.tensor_copy(f1_l[:, :], all_f1[:, l, :]).then_inc(f1_set, 1)

            def set_f2(l):
                need(pool, pe_z, l * B)
                pool.tensor_copy(f2_l[:, :, :], all_f2[:, l, :, :]).then_inc(f2_set, 1)

            def set_ln(l):
                need(pool, hT_done, l * B)
                need(pool, htok_done, l * B)
                pool.tensor_copy(par[:, LN_G:LN_B + 1], all_par[:, l, LN_G:LN_B + 1])
                pool.tensor_copy(lg_l[:, :], all_lg[:, l, :])
                pool.tensor_copy(lb_l[:, :], all_lb[:, l, :]).then_inc(ln_set, 1)

            pool.wait_ge(prod_done, L)
            pool.tensor_copy(m_l[:, :], next_m[:, L - 1, :]).then_inc(m_set, 1)
            pool.wait_ge(par_done, 1)
            pool.wait_ge(w2_in, 16)
            pool.wait_ge(f1_in, 16)
            pool.wait_ge(f2_in, 16)
            pool.wait_ge(ln_in, 32)

            before_powers = [5 + NT // 4 * i for i in range(4)]
            after_powers = [NT // 4 * (i + 1) for i in range(4)]

            def scatter(first, last):
                for k in range(first, last):
                    pool.indirect_dma_start(x_slots[:, :], bass.IndirectOffsetOnAxis(ap=pos[:, k:k + 1], axis=0),
                                            xn[:, k, :], None).then_inc(scattered, 16)

            def weigh(b):
                pool.wait_ge(e_silu, nth(ORDER, b))
                y = y_tok[:, b, :].rearrange("p (c d) -> p c d", c=C)
                pool.tensor_tensor(y, y, half_w[:, b * C:(b + 1) * C].unsqueeze(2).broadcast_to([P, C, D]),
                                   ALU.mult).then_inc(e_weighed, 1)

            def add_x(b):
                pool.wait_ge(e_s, b + 1)
                pool.tensor_tensor(y_tok[:, b, :], y_tok[:, b, :],
                                   x_sb[:, b * C:(b + 1) * C, :].rearrange("p c d -> p (c d)"), ALU.add)\
                    .then_inc(pool_out, 1)

            def step(l, t):
                first = isinstance(l, int) and l == 0
                ends = isinstance(l, int) and l == L
                if not ends and t in (1, 2):
                    (set_w2 if t == 1 else set_f2)(l)
                w = at(l, t, 3, B, LB)
                if w and w[0] is not LB - 1:
                    n, b, _ = w
                    if b == 0:
                        pool.wait_ge(ln_set, w[2] + 1)
                    pool.wait_ge(z_done, n + 1)
                    pool.tensor_tensor(hg[:, :, :], zhat[:, b % 2, :, :],
                                       lg_l[:, :].unsqueeze(1).broadcast_to([P, C, D]), ALU.mult)\
                        .then_inc(hg_done, 1)
                    pool.wait_ge(hg_done, n + 1)
                    pool.tensor_tensor(htok[:, b * C:(b + 1) * C, 0:D], hg[:, :, :],
                                       lb_l[:, :].unsqueeze(1).broadcast_to([P, C, D]), ALU.add)\
                        .then_inc(htok_done, 1)
                tile_rows(l, t, EARLY)
                if first and 2 < t < B - 1:
                    scatter(before_powers[t - 3], after_powers[t - 3])
                if not ends and t in (0, 1, 2, B - 1):
                    if not (first and t == 1):
                        {0: set_w, 1: set_f1, 2: set_ln, B - 1: set_m}[t](l)
                tile_rows(l, t, LATE)
                if ends and t == 1:
                    weigh(2)
                if w := at(l, t, 1, B, LB):
                    pool.wait_ge(gn_var, w[0] + 1)
                    pool.tensor_tensor(gn_rs[:, :], gn_ve[:, :], half_neg[:, 0:1], ALU.pow).then_inc(gn_rstd, 1)
                if w := at(l, t, 2, B, LB):
                    ln_pow(w[0], w[1])
                if first and t == 1:
                    set_f1(l)
                if first and 2 <= t < B - 2:
                    if t == 2:
                        pool.wait_ge(slots_found, 1)
                        pool.wait_ge(filled_out, 32)
                    scatter(after_powers[t - 3] if t > 2 else 0, before_powers[t - 2])
                if ends and t == 0:
                    for b in (LAST_B, 0, 1):
                        weigh(b)
                if ends and t == 1:
                    for b in (3, 4, 5, 6):
                        weigh(b)
                if ends and t == 2:
                    for b in POOL_OUT:
                        add_x(b)

            def tile_rows(l, t, place):
                w = turn(l, t, place)
                if w is None or first_turns(w[0]):
                    return
                j, k = w
                q = buffer_of(k)
                pool.wait_ge(yt_out[q], 16 * (1 + used_before(l, k)))
                pool.tensor_copy(tile_ids[q][:, :], slot_ids[:, bass.ds(j - TILE_LAG, 1)]).then_inc(ids_set, 1)
                alone(pool, ids_set, j - TILE_LAG + 1)
                alone(pool, yt_done, j - TILE_LAG + 1)
                pool.indirect_dma_start(y_rows[:, :], bass.IndirectOffsetOnAxis(ap=tile_ids[q][:, :], axis=0),
                                        yt[q][:, :], None).then_inc(yt_out[q], 16)

            def first_rows():
                for q in range(5):
                    pool.memset(yt[q][:, :], 0.0).then_inc(yt_zeroed, 1)
                    pool.tensor_copy(tile_ids[q][:, :], fill_id[:, q:q + 1]).then_inc(yt_zeroed, 1)
                pool.wait_ge(yt_zeroed, 10)
                for q in range(5):
                    pool.indirect_dma_start(y_rows[:, :], bass.IndirectOffsetOnAxis(ap=tile_ids[q][:, :], axis=0),
                                            yt[q][:, :], None).then_inc(yt_out[q], 16)

            for t in range(B):
                step(0, t)
                if t == 0:
                    first_rows()
            pool.wait_ge(ids_in, 16)
            with pool.Fori(1, L) as l:
                for t in range(B):
                    step(l, t)
            for t in range(LAG):
                step(L, t)


        @block.scalar
        def _(act):
            act.dma_start(wkqv_sb, Wkqv.rearrange("l p f -> p l f")).then_inc(kqv_in, 16)

            for b in range(B + 1):
                if b < B:
                    act.wait_ge(x_shift, b + 1)
                    for c in range(C - 1):
                        k = b * C + c
                        last = act.activation(xn[:, k, 0:D], x_sb[:, k, :], ACT.Identity, bias=x_nb[:, k:k + 1],
                                              scale=x_rs[:, k:k + 1])
                    last.then_inc(xn_done, 1)
                if b:
                    act.wait_ge(pe_xT, b)
                    act.activation(hT[:, b - 1, :], pair[:, (b - 1) % 2, :], ACT.Copy).then_inc(xT_done, 1)
                if 1 <= b <= L:
                    act.wait_ge(pe_wT, b)
                    need(act, pe_prod, b - 2)
                    act.activation(wT_sb[(b - 1) % 2], bank[2 + (b - 1) % 2][:, 0:3 * D], ACT.Copy)\
                        .then_inc(wT_done, 1)

            def tile_in(l, t, place):
                w = turn(l, t, place)
                if w is not None and not (isinstance(w[0], int) and w[0] < 2):
                    act.wait_ge(pe_hT, w[0] - 1)
                    act.activation(h_T[:, :], bank[4][:, :], ACT.Copy).then_inc(hT_copied, 1)

            def tile_gelu(w):
                if w is not None and not (isinstance(w[0], int) and w[0] < 1):
                    act.wait_ge(hb_done, w[0])
                    act.activation(h_act[:, :], h_in[:, :], ACT.Gelu).then_inc(h_done, 1)

            def last_turn(l, t):
                if isinstance(l, int) and (l == 0 or t > 0):
                    return None
                return turn(l, t - 1, LATE) if t else ((l - 1) * TURN_TILES + TILE_LAG - 1, TURN_TILES - 1)

            def tanh_y(b):
                act.wait_ge(y_in[b], 16)
                for c in range(C):
                    k = b * C + c
                    last = act.activation(th_y[:, k, 0:D], y_tok[:, b, c * D:(c + 1) * D], ACT.Tanh,
                                          scale=half_w[:, k:k + 1])
                last.then_inc(e_th, 1)

            def step(l, t):
                first = isinstance(l, int) and l == 0
                ends = isinstance(l, int) and l == L
                if w := at(l, t, 0, B, LB):
                    act.wait_ge(pe_q, w[0] + 1)
                    act.activation(q_sb[:, :], pair[:, 0, :], ACT.Copy).then_inc(q_done, 1)
                tile_gelu(last_turn(l, t))
                if w := at(l, t, 3, B, LB):
                    n, b, _ = w
                    act.wait_ge(z_half, n + 1)
                    for c in range(C // 2, C):
                        last = act.activation(zhat[:, b % 2, c, :], bank[7][:, c * D:(c + 1) * D], ACT.Identity,
                                              bias=ln_nb[:, b % 2, c:c + 1], scale=ln_rs[:, b % 2, c:c + 1])
                    last.then_inc(z_done, 1)
                if w := at(l, t, 1, B, LB):
                    act.wait_ge(pe_g, w[0] + 1)
                    act.activation(th_sb[:, :], bank[3][:, :], ACT.Tanh, bias=par[:, GATE_B:GATE_B + 1],
                                   scale=0.5).then_inc(th_done, 1)
                    act.activation(gg_sb[:, :], bank[3][:, :], ACT.Identity, bias=par[:, GATE_B:GATE_B + 1],
                                   scale=0.5).then_inc(gg_done, 1)
                if first and t == 1:
                    act.wait_ge(r_shift, 1)
                    act.activation(r_a[:, :, :], r_c[:, :, :], ACT.Exp).then_inc(r_exp, 1)
                tile_in(l, t, EARLY)
                w = at(l, t, 3, B, LB)
                if w and w[0] is not LB - 1:
                    n, b, _ = w
                    act.wait_ge(pe_zT, n + 1)
                    if b == 0:
                        act.wait_ge(ln_set, w[2] + 1)
                    act.activation(hT[:, b, :], pair[:, 1, :], ACT.Identity, bias=par[:, LN_B:LN_B + 1],
                                   scale=par[:, LN_G:LN_G + 1]).then_inc(hT_done, 1)
                tile_gelu(turn(l, t, EARLY))
                if w := at(l, t, 2, B, LB):
                    for i, k in enumerate(halves(l, t)):
                        act.wait_ge(pe_f1, w[0] * 2 + i + 1)
                        act.activation(G_sb[:, k, :], bank[3 + k][:, :], ACT.Gelu,
                                       bias=par[:, F_B + k:F_B + k + 1]).then_inc(G_done, 1)
                if ends and t == 0:
                    act.wait_ge(e_half, 1)
                    act.wait_ge(scattered, 16 * NT)
                    for b in ORDER[:3]:
                        tanh_y(b)
                if ends and t == 1:
                    for b in ORDER[3:]:
                        tanh_y(b)
                tile_in(l, t, LATE)
                if w := at(l, t, 0, B, LB):
                    act.wait_ge(pe_uT, w[0] + 1)
                    act.activation(uT_sb[:, :], bank[2][:, :], ACT.Copy).then_inc(uT_done, 1)
                if w := at(l, t, 1, B, LB):
                    act.wait_ge(gn_affine, w[0] + 1)
                    act.activation(gn_sb[:, :], bank[6][:, :], ACT.Identity, bias=gn_bi[:, :],
                                   scale=gn_sc[:, :]).then_inc(gn_done, 1)
                if first:
                    tile_gelu(turn(l, t, LATE))
                    tile_in(l, t, LAST)

            steps(act, step, L, B, LAG)

        @block.vector
        def _(dve):
            loaded = {}

            def ln_stats(k, b):
                for c in range(C):
                    last = dve.bn_stats(ln_st[:, b % 2, c, :], bank[7][:, c * D:(c + 1) * D])
                last.then_inc(ln_chain, 1)
                alone(dve, ln_chain, 2 * k + 1)
                for c in range(C):
                    last = dve.bn_aggr(ln_mv[:, b % 2, c, :], ln_st[:, b % 2, c, :])
                last.then_inc(ln_chain, 1)
                dve.wait_ge(ln_chain, 2 * k + 2)
                dve.tensor_scalar(ln_ve[:, b % 2, :], ln_mv[:, b % 2, :, 1], EPS, None, ALU.add)\
                    .then_inc(ln_var, 1)

            def ln_shifts(k, b):
                dve.wait_ge(ln_rstd, k + 1)
                dve.scalar_tensor_tensor(ln_nb[:, b % 2, :], ln_mv[:, b % 2, :, 0], -1.0, ln_rs[:, b % 2, :],
                                         ALU.mult, ALU.mult).then_inc(ln_shift, 1)

            bm1T = rowsT[:, R_BM1:R_BM1 + 2 * L].rearrange("p (l k) -> p l k", k=2)
            bf1T = rowsT[:, R_BF1:R_BF1 + 2 * L].rearrange("p (l k) -> p l k", k=2)

            def products(l):
                dve.wait_ge(pe_prod, l + 1)
                src = bank[4 + l % 2]
                dve.tensor_copy(next_m[:, (l - 1) % L, :], src[:, 0:D])
                dve.tensor_copy(all_w[:, l, :], src[:, D:3 * D]).then_inc(prod_done, 1)

            x_steps = [0]

            def x_step(inst):
                inst.then_inc(x_chain, 1)
                x_steps[0] += 1
                return x_steps[0]

            for b in range(B + 2):
                if b < B:
                    dve.wait_ge(x_in[b], 16)
                    for c in range(C):
                        last = dve.bn_stats(x_st[:, b * C + c, :], x_sb[:, b * C + c, :])
                    alone(dve, x_chain, x_step(last))
                    for c in range(C):
                        last = dve.bn_aggr(x_mv[:, b * C + c, :], x_st[:, b * C + c, :])
                    dve.wait_ge(x_chain, x_step(last))
                    of_b = slice(b * C, (b + 1) * C)
                    dve.tensor_scalar(x_ve[:, of_b], x_mv[:, of_b, 1], EPS, None, ALU.add).then_inc(x_var, 1)
                if 1 <= b <= B:
                    of_b = slice((b - 1) * C, b * C)
                    dve.wait_ge(x_rstd, b)
                    dve.scalar_tensor_tensor(x_nb[:, of_b], x_mv[:, of_b, 0], -1.0, x_rs[:, of_b],
                                             ALU.mult, ALU.mult).then_inc(x_shift, 1)
                if 1 <= b <= B:
                    k = b * C - 1
                    dve.wait_ge(x_shift, b)
                    dve.tensor_scalar(xn[:, k, 0:D], x_sb[:, k, :], x_rs[:, k:k + 1], x_nb[:, k:k + 1],
                                      ALU.mult, ALU.add).then_inc(xn_last, 1)
                if 4 <= b < 4 + L:
                    products(b - 4)
            dve.wait_ge(pe_rows, 1)
            dve.tensor_copy(rowsT[:, :], bank[6][:, 0:NROWS]).then_inc(rows_done, 1)
            dve.wait_ge(rows_done, 1)
            dve.tensor_scalar(all_par[:, :, GATE_B], bm1T[:, :, 1], 0.5, None, ALU.mult)
            dve.tensor_copy(all_par[:, :, VAL_B], bm1T[:, :, 0])
            dve.tensor_copy(all_par[:, :, W2_B], rowsT[:, R_BM2:R_BM2 + L])
            dve.tensor_copy(all_par[:, :, GN_G], rowsT[:, R_GG:R_GG + L])
            dve.tensor_tensor(all_par[:, :, GN_B], rowsT[:, R_GB:R_GB + L], rowsT[:, R_BF2:R_BF2 + L], ALU.add)
            dve.tensor_copy(all_par[:, :, LN_G], rowsT[:, R_LG:R_LG + L])
            dve.tensor_copy(all_par[:, :, LN_B], rowsT[:, R_LB:R_LB + L]).then_inc(par_done, 1)

            def gelu_bias():
                dve.wait_ge(pe_fb, 1)
                dve.tensor_tensor(all_par[:, :, F_B:F_B + 2], bf1T, bank[7][:, 0:2 * L]
                                  .rearrange("p (l k) -> p l k", k=2), ALU.subtract).then_inc(fb_done, 1)

            done = [0]

            def chain(inst):
                inst.then_inc(r_step, 1)
                done[0] += 1
                dve.wait_ge(r_step, done[0])

            def over_e(v):
                return v.unsqueeze(2).broadcast_to([P, NT, E])

            def over_t(v):
                return v.unsqueeze(1).broadcast_to([P, NT, E])

            def shift_logits():
                dve.wait_ge(ids_made, 4)
                dve.wait_ge(pe_gate, B)
                chain(dve.tensor_copy(r_lg[:, :, :].rearrange("p t e -> p (t e)"), bank[7][:, 0:TE]))
                chain(dve.tensor_reduce(r_mx[:, :], r_lg[:, :, :], AX, ALU.max))
                dve.tensor_tensor(r_c[:, :, :], r_lg[:, :, :], over_e(r_mx[:, :]), ALU.subtract).then_inc(r_shift, 1)

            def choose_expert():
                chain(dve.tensor_tensor(r_oh[:, :, :], r_lg[:, :, :], over_e(r_mx[:, :]), ALU.is_equal))
                chain(dve.tensor_tensor(r_lg[:, :, :], r_oh[:, :, :], over_t(iota_e[:, :]), ALU.mult))
                chain(dve.tensor_reduce(r_ix[:, :], r_lg[:, :, :], AX, ALU.min))
                dve.tensor_tensor(r_oh[:, :, :], over_t(iota_e[:, :]), over_e(r_ix[:, :]), ALU.is_equal)\
                    .then_inc(r_shift, 1)

            def expert_weight():
                dve.wait_ge(r_exp, 1)
                chain(dve.tensor_reduce(r_sum[:, :], r_a[:, :, :], AX, ALU.add))
                chain(dve.reciprocal(weight[:, :], r_sum[:, :]))
                dve.tensor_scalar(half_w[:, :], weight[:, :], 0.5, None, ALU.mult).then_inc(e_half, 1)

            prefix = bank[5][:, 0:TE].rearrange("p (t e) -> p t e", e=E)
            total = bank[5][:, TE:2 * TE].rearrange("p (t e) -> p t e", e=E)

            def count_tokens():
                dve.wait_ge(pe_prefix, 1)
                chain(dve.tensor_copy(r_tot[:, :, :], total.rearrange("p t e -> p e t")))
                chain(dve.tensor_tensor_scan(r_cum[:, :, :].rearrange("p e t -> p (e t)"), ones[:, 0:TE],
                                             r_tot[:, :, :].rearrange("p e t -> p (e t)"), 0.0, ALU.mult, ALU.add))
                chain(dve.memset(r_prev[:, :], 0.0))
                chain(dve.tensor_copy(r_prev[:, 1:E], r_cum[:, 0:E - 1, NT - 1]))
                chain(dve.tensor_tensor(r_n[:, :], r_cum[:, :, NT - 1], r_prev[:, :], ALU.subtract))

            def count_tiles():
                chain(dve.tensor_tensor(r_k[:, :, :], r_n[:, :].unsqueeze(2).broadcast_to([P, E, NT]),
                                        filled[:, :].unsqueeze(1).broadcast_to([P, E, NT]), ALU.is_gt))
                chain(dve.tensor_reduce(r_nt[:, :], r_k[:, :, :], AX, ALU.add))
                chain(dve.tensor_tensor_scan(r_end[:, :], ones[:, 0:E], r_nt[:, :], 0.0, ALU.mult, ALU.add))
                chain(dve.tensor_tensor(r_base[:, :], r_end[:, :], r_nt[:, :], ALU.subtract))
                chain(dve.scalar_tensor_tensor(r_base[:, :], r_base[:, :], float(P), r_prev[:, :], ALU.mult, ALU.subtract))

            def find_slots():
                chain(dve.tensor_tensor(r_lg[:, :, :], r_cum[:, :, :].rearrange("p e t -> p t e"), total, ALU.subtract))
                chain(dve.tensor_tensor(r_lg[:, :, :], r_lg[:, :, :], prefix, ALU.add))
                chain(dve.tensor_tensor(r_lg[:, :, :], r_lg[:, :, :], over_t(r_base[:, :]), ALU.add))
                chain(dve.tensor_tensor(r_lg[:, :, :], r_lg[:, :, :], r_oh[:, :, :], ALU.mult))
                chain(dve.tensor_reduce(posf[:, :], r_lg[:, :, :], AX, ALU.add))
                dve.tensor_copy(pos[:, :], posf[:, :]).then_inc(slots_found, 1)

            def find_experts():
                chain(dve.tensor_tensor(r_te[:, :, :], tile_at[:, :].unsqueeze(2).broadcast_to([P, TILES, E]),
                                        r_end[:, :].unsqueeze(1).broadcast_to([P, TILES, E]), ALU.is_ge))
                chain(dve.tensor_reduce(tile_ef[:, :], r_te[:, :, :], AX, ALU.add))
                dve.tensor_scalar(tile_e[:, :], tile_ef[:, :], float(E - 1), None, ALU.min).then_inc(route_done, 1)

            u_pair = pair[:, :, 0:2 * H1].rearrange("p k (c w) -> p k c w", c=2)

            def tokens(v, b):
                return v[:, b * C:(b + 1) * C, 0:D]

            def silu_y(b):
                dve.wait_ge(e_th, nth(ORDER, b))
                y = y_tok[:, b, :].rearrange("p (c d) -> p c d", c=C)
                dve.scalar_tensor_tensor(y, tokens(th_y, b), 1.0, y, ALU.add, ALU.mult).then_inc(e_silu, 1)

            def times_s(b):
                dve.wait_ge(e_weighed, nth(ORDER, b))
                if b > 4:
                    dve.wait_ge(htok_done, LB - B + b + 1)
                y = y_tok[:, b, :].rearrange("p (c d) -> p c d", c=C)
                dve.tensor_tensor(y, y, tokens(htok, b), ALU.mult).then_inc(e_s, 1)

            def add_x(b):
                dve.wait_ge(e_s, b + 1)
                y = y_tok[:, b, :].rearrange("p (c d) -> p c d", c=C)
                dve.tensor_tensor(y, y, tokens(x_sb, b), ALU.add).then_inc(dve_out, 1)

            def prepare_last():
                y = y_tok[:, LAST_B, :].rearrange("p (c d) -> p c d", c=C)
                over_c = lambda v: v[:, :].unsqueeze(1).broadcast_to([P, C, D])
                dve.wait_ge(e_weighed, 1)
                dve.tensor_tensor(tokens(th_y, LAST_B), y, over_c(lg_l), ALU.mult).then_inc(e_last, 1)
                dve.wait_ge(e_last, 1)
                dve.tensor_tensor(y, y, over_c(lb_l), ALU.mult).then_inc(e_last, 1)
                dve.wait_ge(e_last, 2)
                dve.tensor_tensor(y, y, tokens(x_sb, LAST_B), ALU.add).then_inc(e_last, 1)

            def finish_last():
                y = y_tok[:, LAST_B, :].rearrange("p (c d) -> p c d", c=C)
                g = tokens(th_y, LAST_B)
                dve.wait_ge(z_done, LB)
                dve.wait_ge(e_last, 3)
                dve.tensor_tensor(g, zhat[:, LAST_B % 2, :, :], g, ALU.mult).then_inc(e_last, 1)
                dve.wait_ge(e_last, 4)
                dve.tensor_tensor(y, y, g, ALU.add).then_inc(dve_out, 1)

            def step(l, t):
                first = isinstance(l, int) and l == 0
                ends = isinstance(l, int) and l == L
                if w := at(l, t, 0, B, LB):
                    n, b, _ = w
                    dve.wait_ge(pe_S, n + 1)
                    dve.tensor_copy(S_sb[:, 0, :], pair[:, 1, 0:H1]).then_inc(S_part, 1)
                    for c in range(1, C - 1):
                        dve.wait_ge(S_part, n * (C - 2) + c)
                        dve.tensor_tensor(S_sb[:, c, :], pair[:, 1, c * H1:(c + 1) * H1], S_sb[:, c - 1, :], ALU.add)\
                            .then_inc(S_part if c < C - 2 else S_done, 1)
                if first and t == 1:
                    choose_expert()
                if first and t == 2:
                    count_tiles()
                tile_out(l, t, EARLY)
                tile_expert(l, t, EARLY)
                if w := at(l, t, 0, B, LB):
                    n, b, _ = w
                    dve.wait_ge(pe_A, n + 1)
                    dve.tensor_tensor(A_sb[:, :, :], pair[:, 0, :].rearrange("p (c i) -> p c i", c=C),
                                      causal[:, :].unsqueeze(1).broadcast_to([P, C, P]), ALU.mult)\
                        .then_inc(A_done, 1)
                if w := at(l, t, 1, B, LB):
                    n, b, _ = w
                    dve.wait_ge(gg_done, n + 1)
                    dve.wait_ge(th_done, n + 1)
                    dve.scalar_tensor_tensor(gate_t[:, :], th_sb[:, :], 1.0, gg_sb[:, :], ALU.add, ALU.mult)\
                        .then_inc(gt_done, 1)
                tile_in(l, t, EARLY)
                if w := at(l, t, 1, B, LB):
                    n, b, _ = w
                    dve.wait_ge(gt_done, n + 1)
                    dve.wait_ge(pe_a, n + 1)
                    dve.scalar_tensor_tensor(act_sb[:, :], bank[2][:, :], par[:, VAL_B:VAL_B + 1], gate_t[:, :],
                                             ALU.add, ALU.mult).then_inc(act_done, 1)
                if first and t == 1:
                    expert_weight()
                if first and t == 2:
                    find_slots()
                tile_hidden(l, t, EARLY)
                if w := at(l, t, 0, B, LB):
                    n, b, _ = w
                    dve.wait_ge(pe_u, n + 1)
                    if isinstance(n, int) and n == 0:
                        dve.wait_ge(floor_in, 16)
                    row_sum = u_pair[:, :, :, D]
                    two = lambda v: v[:, :].rearrange("p (k c) -> p k c", k=2)
                    dve.tensor_tensor(two(rs1), row_sum, two(floor_sb), ALU.max).then_inc(u_chain, 1)
                    dve.wait_ge(u_chain, n * 3 + 1)
                    dve.scalar_tensor_tensor(two(rs2), row_sum, -1.0, two(rs1), ALU.mult, ALU.max)\
                        .then_inc(u_chain, 1)
                    dve.wait_ge(u_chain, n * 3 + 2)
                    dve.reciprocal(rs3[:, :], rs2[:, :]).then_inc(u_chain, 1)
                    dve.wait_ge(u_chain, n * 3 + 3)
                    dve.tensor_tensor(u_sb[:, :, :].rearrange("p (k c) d -> p k c d", k=2), u_pair[:, :, :, 0:D],
                                      rs3[:, :].rearrange("p (k c) -> p k c", k=2).unsqueeze(3)
                                      .broadcast_to([P, 2, C // 2, D]), ALU.mult).then_inc(u_done, 1)
                if w := at(l, t, 1, B, LB):
                    n, b, _ = w
                    dve.wait_ge(pe_w2, n + 1)
                    if b == 0:
                        dve.wait_ge(w2_set, w[2] + 1)
                    dve.bn_stats(gs_st[:, :], bank[6][:, :]).then_inc(gs_chain, 1)
                    alone(dve, gs_chain, n * 3 + 1)
                    dve.bn_aggr(gs_mv[:, :], gs_st[:, :]).then_inc(gs_chain, 1)
                    dve.wait_ge(gs_chain, n * 3 + 2)
                    dve.tensor_tensor(gs[:, 0:1], gs_mv[:, 0:1], par[:, W2_B:W2_B + 1], ALU.add).then_inc(gs_chain, 1)
                    dve.wait_ge(gs_chain, n * 3 + 3)
                    dve.scalar_tensor_tensor(gs[:, 1:2], gs[:, 0:1], gs[:, 0:1], gs_mv[:, 1:2], ALU.mult, ALU.add)\
                        .then_inc(gs_done, 1)

                if first and t == 0:
                    shift_logits()
                if first and t == 1:
                    gelu_bias()
                    count_tokens()
                if first and t == 2:
                    find_experts()
                if ends and t == 1:
                    prepare_last()
                    for b in (0, 1):
                        times_s(b)
                        add_x(b)
                    for b in (2, 3):
                        silu_y(b)
                tile_out(l, t, LATE)
                tile_expert(l, t, LATE)
                if w := at(l, t, 1, B, LB):
                    n, b, _ = w
                    dve.wait_ge(pe_gn, n + 1)
                    dve.tensor_copy(gn_m[:, :], bank[3][:, 0:2]).then_inc(gn_chain, 1)
                    dve.wait_ge(gn_chain, n * 4 + 1)
                    dve.scalar_tensor_tensor(gn_nv[:, :], gn_m[:, 0:1], gn_m[:, 0:1], gn_m[:, 1:2],
                                             ALU.mult, ALU.subtract).then_inc(gn_chain, 1)
                    dve.wait_ge(gn_chain, n * 4 + 2)
                    dve.tensor_scalar(gn_ve[:, :], gn_nv[:, :], -1.0, EPS, ALU.mult, ALU.add).then_inc(gn_var, 1)
                if w := at(l, t, 2, B, LB):
                    dve.wait_ge(pe_z, w[0] + 1)
                    ln_stats(w[0], w[1])
                if ends and t == 1:
                    silu_y(4)
                if w := at(l, t, 1, B, LB):
                    n, b, _ = w
                    dve.wait_ge(gn_rstd, n + 1)
                    dve.tensor_tensor(gn_sc[:, :], gn_rs[:, :], par[:, GN_G:GN_G + 1], ALU.mult).then_inc(gn_chain, 1)
                    dve.tensor_tensor(gn_d[:, :], par[:, W2_B:W2_B + 1], gn_m[:, 0:1], ALU.subtract)\
                        .then_inc(gn_chain, 1)
                    dve.wait_ge(gn_chain, n * 4 + 4)
                    dve.scalar_tensor_tensor(gn_bi[:, :], gn_d[:, :], gn_sc[:, :], par[:, GN_B:GN_B + 1],
                                             ALU.mult, ALU.add).then_inc(gn_affine, 1)
                tile_in(l, t, LATE)
                tile_hidden(l, t, LATE)
                if w := at(l, t, 2, B, LB):
                    n, b, _ = w
                    ln_shifts(n, b)
                    need(dve, hg_done, n - 1)
                    dve.wait_ge(ln_shift, n + 1)
                    for c in range(C // 2):
                        last = dve.tensor_scalar(zhat[:, b % 2, c, :], bank[7][:, c * D:(c + 1) * D],
                                                 ln_rs[:, b % 2, c:c + 1], ln_nb[:, b % 2, c:c + 1], ALU.mult, ALU.add)
                    last.then_inc(z_half, 1)
                if w := at(l, t, 1, B, LB):
                    n, b, _ = w
                    dve.wait_ge(gn_done, n + 1)
                    dve.tensor_tensor(y_sb[:, :], gn_sb[:, :], hT[:, b, :], ALU.add).then_inc(y_done, 1)
                if ends and t == 0:
                    for b in ORDER[:3]:
                        silu_y(b)
                if ends and t == 1:
                    for b in (5, 6):
                        silu_y(b)
                    finish_last()
                if ends and t == 2:
                    for b in (2, 3, 4):
                        times_s(b)
                    for b in (5, 6):
                        times_s(b)
                        add_x(b)
                tile_expert(l, t, LAST)
                tile_in(l, t, LAST)
                tile_hidden(l, t, LAST)

            def tile_out(l, t, place_):
                w = turn(l, t, place_)
                if w is None or first_turns(w[0]):
                    return
                j, k = w
                q = buffer_of(k)
                e = expert(dve, loaded, j, k, TILE_LAG)
                bias = moe_b2[:, bass.ds(e, 1), :].rearrange("p a f -> p (a f)")
                dve.wait_ge(yt_out[q], 16 * (1 + used_before(l, k)))
                dve.wait_ge(pe_y, j - TILE_LAG + 1)
                dve.tensor_tensor(yt[q][:, :], bank[5][:, 0:D], bias, ALU.add).then_inc(yt_done, 1)

            def tile_expert(l, t, place_):
                w = turn(l, t, place_)
                if w is not None and not (isinstance(w[0], int) and w[0] < 1):
                    expert(dve, loaded, w[0], w[1], 1)

            def tile_in(l, t, place_):
                if w := turn(l, t, place_):
                    dve.wait_ge(pe_xt, w[0] + 1)
                    dve.tensor_copy(xtT[:, :], bank[4][:, 0:P]).then_inc(xtT_done, 1)

            def tile_hidden(l, t, place_):
                w = turn(l, t, place_)
                if w is None:
                    return
                j, k = w
                if not (isinstance(j, int) and j < 1):
                    if isinstance(j, int) and j == 1:
                        dve.wait_ge(experts_in, 48)
                        dve.wait_ge(bias1_in, 16)
                    need(dve, h_done, j - 1)
                    dve.wait_ge(pe_h, j)
                    dve.tensor_tensor(h_in[:, :], bank[5][:, :], moe_b1[:, bass.ds(loaded[k], 1), :]
                                      .rearrange("p a f -> p (a f)"), ALU.add).then_inc(hb_done, 1)

            steps(dve, step, L, B, LAG)

        @block.tensor
        def _(pe):
            mm = nc.tensor.matmul
            loaded = {}
            pe.wait_ge(const_made, 6)
            def weights_T(l):
                need(pe, wT_done, l - 1)
                for j, part in enumerate((1, 0, 2)):
                    last = pe.transpose(bank[2 + l % 2][:, j * D:(j + 1) * D],
                                        wkqv_sb[:, l, part * D:(part + 1) * D], ident[:, :])
                last.then_inc(pe_wT, 1)

            def products(l):
                pe.wait_ge(wT_done, l + 1)
                need(pe, prod_done, l - 1)
                dst, src = bank[4 + l % 2], wT_sb[l % 2]
                mm(dst[:, 0:D], src[:, 0:D], src[:, D:2 * D], start=True, stop=True)
                mm(dst[:, D:3 * D], src[:, 2 * D:3 * D], wm1_sb[:, l, :], start=True, stop=True).then_inc(pe_prod, 1)

            def logits(b):
                pe.wait_ge(xT_done, b + 1)
                for c in range(C):
                    k = b * C + c
                    last = mm(bank[7][:, k * E:(k + 1) * E], hT[:, b, c * P:(c + 1) * P], gate_sb[:, :],
                              start=True, stop=True)
                last.then_inc(pe_gate, 1)

            for _ in range(8):
                mm(bank[7][:, 0:2 * P], ident[:, :], ones[:, :], start=True, stop=True)
            for b in range(B):
                pe.wait_ge(xn_done, b + 1)
                pe.wait_ge(xn_last, b + 1)
                need(pe, xT_done, b - 1)
                for c in range(C):
                    last = pe.transpose(pair[:, b % 2, c * P:(c + 1) * P], xn[:, b * C + c, 0:D], ident[:, :])
                last.then_inc(pe_xT, 1)
                if b == 0:
                    pe.wait_ge(kqv_in, 16)
                if b < L:
                    weights_T(b)
                if 2 <= b < 2 + L:
                    if b == 2:
                        pe.wait_ge(m1_in, 16)
                    products(b - 2)
                if b >= L:
                    if b == L:
                        pe.wait_ge(gate_in, 16)
                    logits(b - L)
                if b == B - 2:
                    pe.wait_ge(rows_in, 16 * 8)
                    pe.transpose(bank[6][:, 0:NROWS], rows[:, :], ident[0:NROWS, 0:NROWS]).then_inc(pe_rows, 1)
            pe.wait_ge(col_made, 2)
            pe.wait_ge(prod_done, L)
            pe.wait_ge(xT_done, B)

            def tile_back(l, t, place, gelu_read):
                w = turn(l, t, place)
                if w is None:
                    return
                j, k = w
                if not first_turns(j):
                    e = expert(pe, loaded, j, k, TILE_LAG)
                    of_e = [moe_w2[:, bass.ds(e, 1), i, :].rearrange("p a d -> p (a d)") for i in range(KF)]
                    pe.wait_ge(hT_copied, j - 2)
                    pe.wait_ge(hb_done, j - 1)
                    for i in range(KF):
                        last = mm(bank[5][:, 0:D], h_T[:, i * P:(i + 1) * P], of_e[i],
                                  start=i == 0, stop=i == KF - 1)
                    last.then_inc(pe_y, 1)
                if not (isinstance(j, int) and j < 2):
                    pe.wait_ge(h_done, j - 1)
                    pe.wait_ge(xtT_done, j)
                    pe.wait_ge(G_done, gelu_read)
                    for i in range(KF):
                        last = pe.transpose(bank[4][:, i * P:(i + 1) * P], h_act[:, i * P:(i + 1) * P], ident[:, :])
                    last.then_inc(pe_hT, 1)

            def tile_front(l, t, place, gelu_read):
                w = turn(l, t, place)
                if w is None:
                    return
                j, k = w
                if not (isinstance(j, int) and j < 1):
                    e = expert(pe, loaded, j, k, 1)
                    of_e = moe_w1[:, bass.ds(e, 1), :].rearrange("p a f -> p (a f)")
                    if isinstance(j, int) and j == 1:
                        pe.wait_ge(experts_in, 48)
                    pe.wait_ge(xtT_done, j)
                    if isinstance(j, int):
                        need(pe, hb_done, j - 1)
                    need(pe, yt_done, j - 2)
                    mm(bank[5][:, :], xtT[:, :], of_e,
                       start=True, stop=True).then_inc(pe_h, 1)
                q = buffer_of(k)
                before_l = used_before(l, k) + (1 if q >= 2 else 0) if not isinstance(l, int) else 0
                pe.wait_ge(xt_in[q], 16 * (before_l + 1))
                need(pe, hT_copied, j - 1)
                pe.wait_ge(G_done, gelu_read)
                pe.transpose(bank[4][:, 0:P], xt[q][:, 0:D], ident[:, :]).then_inc(pe_xt, 1)

            def gelu_first(l, t, i):
                if w := at(l, t, 2, B, LB):
                    n, b, _ = w
                    k = halves(l, t)[i]
                    pe.wait_ge(y_done, n + 1)
                    if b == 0:
                        pe.wait_ge(f1_set, w[2] + 1)
                    need(pe, G_done, 2 * n)
                    if k == 0:
                        need(pe, gg_done, n + 2 if not (isinstance(n, int) and n + 2 > LB) else LB)
                    else:
                        need(pe, xtT_done, turns_before(l, t, LATE))
                    mm(bank[3 + k][:, :], f1_l[:, k * D:(k + 1) * D], y_sb[:, :], start=True, stop=True)\
                        .then_inc(pe_f1, 1)

            def step(l, t):
                first = isinstance(l, int) and l == 0
                start = first and t == 0
                if w := at(l, t, 0, B, LB):
                    n, b, _ = w
                    tok = (lambda c: xn[:, b * C + c, 0:H1]) if first else (lambda c: htok[:, b * C + c, :])
                    if not first:
                        pe.wait_ge(htok_done, n - B + 1)
                        pe.wait_ge(hT_done, n - B + 1)
                    need(pe, u_done, n)
                    for c in range(C - 1):
                        last = mm(pair[:, 1, c * H1:(c + 1) * H1], tok(c)[:, 0:D], tok(c), start=True, stop=True)
                    last.then_inc(pe_S, 1)
                    if b == 0:
                        pe.wait_ge(m_set, w[2] + 1)
                    mm(pair[:, 0, :], m_l[:, :], hT[:, b, :], start=True, stop=True).then_inc(pe_q, 1)
                    if start:
                        logits(L)
                if w := at(l, t, 1, B, LB):
                    n, b, _ = w
                    pe.wait_ge(uT_done, n + 1)
                    if b == 0:
                        pe.wait_ge(w_set, w[2] + 1)
                    need(pe, gn_chain, 4 * n - 3)
                    mm(bank[3][:, :], w_l[:, D:2 * D], uT_sb[:, :], start=True, stop=True).then_inc(pe_g, 1)
                    mm(bank[2][:, :], w_l[:, 0:D], uT_sb[:, :], start=True, stop=True).then_inc(pe_a, 1)
                n2 = l * B + t - 2
                tile_back(l, t, EARLY, n2 * 2)
                if w := at(l, t, 0, B, LB):
                    n, b, _ = w
                    pe.wait_ge(q_done, n + 1)
                    for c in range(C):
                        at_c = slice(c * P, (c + 1) * P)
                        last = mm(pair[:, 0, at_c], hT[:, b, at_c], q_sb[:, at_c], start=True, stop=True)
                    last.then_inc(pe_A, 1)
                    if start:
                        logits(L + 1)
                if first and t == 1:
                    pe.wait_ge(r_shift, 2)
                    oh = r_oh[:, :, :].rearrange("p t e -> p (t e)")
                    mm(bank[5][:, 0:TE], before[:, :], oh, start=True, stop=True)
                    mm(bank[5][:, TE:2 * TE], ones[:, 0:P], oh, start=True, stop=True).then_inc(pe_prefix, 1)
                tile_front(l, t, EARLY, n2 * 2)
                if not turn(l, t, EARLY):
                    gelu_first(l, t, 0)
                w = at(l, t, 3, B, LB)
                if w and w[0] is not LB - 1:
                    n, b, _ = w
                    pe.wait_ge(z_done, n + 1)
                    need(pe, S_done, n + LAG + 1 if not (isinstance(n, int) and n + LAG >= LB) else LB)
                    need(pe, u_done, n + LAG if not (isinstance(n, int) and n + LAG >= LB) else LB)
                    for c in range(C):
                        last = pe.transpose(pair[:, 1, c * P:(c + 1) * P], zhat[:, b % 2, c, :], ident[:, :])
                    last.then_inc(pe_zT, 1)
                if turn(l, t, EARLY):
                    gelu_first(l, t, 0)
                gelu_first(l, t, 1)
                if w := at(l, t, 0, B, LB):
                    n, b, _ = w
                    tok = (lambda c: xn[:, b * C + c, 0:H1]) if first else (lambda c: htok[:, b * C + c, :])
                    pe.wait_ge(A_done, n + 1)
                    pe.wait_ge(S_done, n + 1)
                    need(pe, hT_done, n - LAG + 1)
                    for c in range(C):
                        dst = pair[:, c // 2, (c % 2) * H1:(c % 2 + 1) * H1]
                        last = mm(dst, A_sb[:, c, :], tok(c), start=True, stop=c == 0)
                        if c:
                            last = mm(dst, q_sb[:, c * P:(c + 1) * P], S_sb[:, c - 1, :], start=False, stop=True)
                    last.then_inc(pe_u, 1)
                    if start:
                        logits(L + 2)
                        logits(L + 3)
                if w := at(l, t, 1, B, LB):
                    n, b, _ = w
                    pe.wait_ge(act_done, n + 1)
                    if b == 0:
                        pe.wait_ge(w2_set, w[2] + 1)
                    need(pe, gn_done, n)
                    mm(bank[6][:, :], w2_l[:, :], act_sb[:, :], start=True, stop=True).then_inc(pe_w2, 1)
                if first and t == 1:
                    pe.wait_ge(rows_done, 1)
                    pe.wait_ge(f1_in, 16)
                    for i in range(2 * L):
                        last = mm(bank[7][:, i:i + 1], all_f1[:, i // 2, i % 2 * D:(i % 2 + 1) * D],
                                  rowsT[:, R_BF2 + i // 2:R_BF2 + i // 2 + 1], start=True, stop=True)
                    last.then_inc(pe_fb, 1)
                tile_back(l, t, LATE, n2 * 2 + 2)
                if w := at(l, t, 2, B, LB):
                    n, b, _ = w
                    need(pe, z_done, n)
                    if isinstance(n, int) and n == 0:
                        pe.wait_ge(fb_done, 1)
                    pe.wait_ge(G_done, 2 * n + 2)
                    if b == 0:
                        pe.wait_ge(f2_set, w[2] + 1)
                    for c in range(C):
                        at_c = slice(c * P, (c + 1) * P)
                        mm(bank[7][:, at_c], y_sb[:, at_c], ident[:, :], start=True, stop=False, is_transpose=True)
                        for k in range(2):
                            last = mm(bank[7][:, at_c], G_sb[:, k, at_c], f2_l[:, k, :], start=False, stop=k == 1)
                    last.then_inc(pe_z, 1)
                if w := at(l, t, 1, B, LB):
                    n, b, _ = w
                    pe.wait_ge(gs_done, n + 1)
                    need(pe, G_done, 2 * n)
                    pe.wait_ge(gg_done, n + 1)
                    mm(bank[3][:, 0:2], mean_of[:, :], gs[:, :], start=True, stop=True).then_inc(pe_gn, 1)
                tile_front(l, t, LATE, n2 * 2 + 2)
                if w := at(l, t, 0, B, LB):
                    n, b, _ = w
                    pe.wait_ge(u_done, n + 1)
                    need(pe, act_done, n)
                    for c in range(C):
                        last = pe.transpose(bank[2][:, c * P:(c + 1) * P], u_sb[:, c, :], ident[:, :])
                    last.then_inc(pe_uT, 1)

                tile_back(l, t, LAST, n2 * 2 + 2)
                tile_front(l, t, LAST, n2 * 2 + 2)
                if isinstance(l, int) and l == 0 and t == B - 2:
                    pe.wait_ge(route_done, 1)

            steps(pe, step, L, B, LAG)


_INS = ['L0_attn_x', 'L0_attn_Wkqv', 'L0_attn_Wm1', 'L0_attn_bm1', 'L0_attn_Wm2', 'L0_attn_bm2', 'L0_attn_gn_g',
        'L0_attn_gn_b', 'L0_attn_Wf1', 'L0_attn_bf1', 'L0_attn_Wf2', 'L0_attn_bf2', 'L0_attn_ln_g', 'L0_attn_ln_b',
        'L0_ffn_gate_w', 'L0_ffn_w1', 'L0_ffn_b1', 'L0_ffn_w2', 'L0_ffn_b2']


def kernel(**inputs):
    import numpy as np
    import concourse.bacc as bacc
    from concourse import mybir as mb
    from concourse.bass_utils import run_bass_kernel_spmd

    nc = bacc.Bacc("TRN2", target_bir_lowering=False, num_devices=1)
    arrays, args = {}, []
    for name in _INS:
        a = np.ascontiguousarray(inputs[name])
        arrays[f"in_{name}"] = a
        args.append(nc.dram_tensor(f"in_{name}", a.shape, mb.dt.from_np(a.dtype), kind="ExternalInput").ap())
    B, S, D = inputs['L0_attn_x'].shape
    i = np.arange(S, dtype=np.float32).reshape(S // 128, 128).T
    arrays["row_floor"] = np.ascontiguousarray(np.sqrt(np.float32(D)) * (1 + np.sqrt(i))).astype(np.float32)
    args.append(nc.dram_tensor("row_floor", arrays["row_floor"].shape, mb.dt.float32, kind="ExternalInput").ap())
    out = nc.dram_tensor("out", (B, S, D), mb.dt.float32, kind="ExternalOutput").ap()
    retention_moe_kernel(nc, *args, out)
    r = run_bass_kernel_spmd(nc, [arrays], core_ids=[0])
    return r.results[0]["out"]
```

```python
import concourse.bass as bass
from concourse import mybir
from contextlib import ExitStack



def retention_moe_kernel(nc, x, Wkqv, Wm1, bm1, Wm2, bm2, gn_g, gn_b, Wf1, bf1, Wf2, bf2, ln_g, ln_b,
                         gate_w, w1, b1, w2, b2, row_floor, out):
    f32 = mybir.dt.float32
    f32r = mybir.dt.float32r
    i32 = mybir.dt.int32
    u32 = mybir.dt.uint32
    ALU = mybir.AluOpType
    ACT = mybir.ActivationFunctionType
    AX = mybir.AxisListType.X

    B, S, D = x.shape
    L = Wkqv.shape[0]
    E, FF = w1.shape[0], w1.shape[2]
    P = 128
    C = S // P
    KF = FF // P
    NT = B * C
    TOK = B * S
    SLOT_TILES = (TOK + E * (P - 1)) // P
    H1 = D + 1
    ROW = D + 2
    EPS = 1e-5
    TILE_LAG = 2
    TURN_TILES = SLOT_TILES // (L - 1)
    TILES = SLOT_TILES + TILE_LAG
    assert D == P and SLOT_TILES % (L - 1) == 0 and KF == C and B == 2 * L and TURN_TILES == 13

    x_slots = nc.dram_tensor("x_slots", [TILES * P, ROW], f32, kind="Internal").ap()
    y_rows = nc.dram_tensor("y_rows", [TOK + TILES * P, D], f32, kind="Internal").ap()

    ctx = ExitStack()
    with ctx:
        def sb(name, shape, dt=f32):
            return ctx.enter_context(nc.sbuf_tensor(name, shape, dt))

        def sem(name):
            return ctx.enter_context(nc.semaphore(name))

        pair = ctx.enter_context(nc.psum_tensor("pair", [P, 2, 512], f32))
        bank = {k: ctx.enter_context(nc.psum_tensor(f"bank{k}", [P, 512], f32)) for k in range(2, 8)}

        x_sb = sb("x_sb", [P, NT, D])
        xn = sb("xn", [P, NT, ROW])
        htok = sb("htok", [P, NT, H1])
        hT = sb("hT", [P, B, S])
        moe_w1 = sb("moe_w1", [P, E, FF + KF])
        moe_w2 = sb("moe_w2", [P, E, KF, D])
        moe_b2 = sb("moe_b2", [P, E, D])
        next_m = sb("next_m", [P, L, D])
        all_w = sb("all_w", [P, L, 2, 2 * D], f32r)
        all_w2 = sb("all_w2", [P, L, D])
        all_f1 = sb("all_f1", [P, L, 2 * D])
        f1_parts = sb("f1_parts", [P, L, 2, 2 * D], f32r)
        all_f2 = sb("all_f2", [P, L, 2, D])
        all_lg = sb("all_lg", [P, L, D])
        all_lb = sb("all_lb", [P, L, D])
        NPAR = 9
        GATE_B, VAL_B, W2_B, GN_G, GN_B, F_B, LN_G, LN_B = 0, 1, 2, 3, 4, 5, 7, 8
        all_par = sb("all_par", [P, L, NPAR])
        m_l = sb("m_l", [P, D])
        w_l = sb("w_l", [P, 2, 2 * D], f32r)
        w2_l = sb("w2_l", [P, D])
        f1_l = sb("f1_l", [P, 2 * D])
        f1_parts_l = sb("f1_parts_l", [P, 2, 2 * D], f32r)
        f2_l = sb("f2_l", [P, 2, D])
        lg_l = sb("lg_l", [P, D])
        lb_l = sb("lb_l", [P, D])
        par = sb("par", [P, NPAR])
        ident = sb("ident", [P, P])
        causal = sb("causal", [P, P])
        before = sb("before", [P, P])
        ones = sb("ones", [P, 2 * P])
        mean_of = sb("mean_of", [P, P])
        half_neg = sb("half_neg", [P, C])
        floor_sb = sb("floor_sb", [P, C])
        gate_sb = sb("gate_sb", [P, E])
        q_sb = sb("q_sb", [P, S])
        A_sb = sb("A_sb", [P, C, P])
        S_sb = sb("S_sb", [P, C - 1, H1])
        u_sb = sb("u_sb", [P, C, D])
        uT_h = sb("uT_h", [P, S], f32r)
        uT_l = sb("uT_l", [P, S], f32r)
        y_h = sb("y_h", [P, S], f32r)
        y_l = sb("y_l", [P, S], f32r)
        gg_sb = sb("gg_sb", [P, S])
        th_sb = sb("th_sb", [P, S])
        y_sb = sb("y_sb", [P, S])
        G_sb = sb("G_sb", [P, 2, S])
        zhat = sb("zhat", [P, 2, C, D])
        rs1 = sb("rs1", [P, C])
        rs2 = sb("rs2", [P, C])
        rs3 = sb("rs3", [P, C])
        ln_st = sb("ln_st", [P, 2, C, 6])
        ln_mv = sb("ln_mv", [P, 2, C, 2])
        ln_ve = sb("ln_ve", [P, 2, C])
        ln_rs = sb("ln_rs", [P, 2, C])
        ln_nb = sb("ln_nb", [P, 2, C])
        x_st = sb("x_st", [P, NT, 6])
        x_mv = sb("x_mv", [P, NT, 2])
        x_ve = sb("x_ve", [P, NT])
        x_rs = sb("x_rs", [P, NT])
        x_nb = sb("x_nb", [P, NT])
        gs_st = sb("gs_st", [P, 6])
        gs_mv = sb("gs_mv", [P, 2])
        gs = sb("gs", [P, 2])
        gn_m = sb("gn_m", [P, 2])
        gn_nv = sb("gn_nv", [P, 1])
        gn_ve = sb("gn_ve", [P, 1])
        gn_rs = sb("gn_rs", [P, 1])
        gn_sc = sb("gn_sc", [P, 1])
        gn_d = sb("gn_d", [P, 1])
        gn_bi = sb("gn_bi", [P, 1])

        NROWS = 10 * L
        R_BM1, R_BM2, R_GG, R_GB, R_BF1, R_BF2, R_LG, R_LB = (L * k for k in (0, 2, 3, 4, 5, 7, 8, 9))
        rows = sb("rows", [NROWS, P])
        rowsT = sb("rowsT", [P, NROWS])
        scratch = moe_w2[:, :, :, :].rearrange("p e k d -> p (e k d)")
        wkqv_sb = scratch[:, 0:3 * L * D].rearrange("p (l f) -> p l f", l=L)
        w_whole = [wkqv_sb[:, l, 0:2 * D] for l in range(L)]
        wm1_sb = scratch[:, 3 * L * D:5 * L * D].rearrange("p (l f) -> p l f", l=L)
        wT_sb = [scratch[:, (5 * L + 3 * i) * D:(5 * L + 3 * i + 3) * D] for i in range(2)]
        fill = scratch[:, (5 * L + 6) * D:(5 * L + 6) * D + H1]
        b1_rows = sb("b1_rows", [E * KF, P])
        fill_id = sb("fill_id", [P, TILES], i32)
        TE = NT * E
        r_lg = sb("r_lg", [P, NT, E])
        r_a = sb("r_a", [P, NT, E])
        r_c = sb("r_c", [P, NT, E])
        r_oh = sb("r_oh", [P, NT, E])
        r_tot = sb("r_tot", [P, E, NT])
        r_cum = sb("r_cum", [P, E, NT])
        r_mx = sb("r_mx", [P, NT])
        r_ix = sb("r_ix", [P, NT])
        r_sum = sb("r_sum", [P, NT])
        weight = sb("weight", [P, NT])
        posf = sb("posf", [P, NT])
        pos = sb("pos", [P, NT], i32)
        iota_e = sb("iota_e", [P, E])
        tile_at = sb("tile_at", [P, TILES])
        filled = sb("filled", [P, NT])
        r_prev = sb("r_prev", [P, E])
        r_n = sb("r_n", [P, E])
        r_nt = sb("r_nt", [P, E])
        r_end = sb("r_end", [P, E])
        r_base = sb("r_base", [P, E])
        r_k = sb("r_k", [P, E, NT])
        r_te = sb("r_te", [P, TILES, E])
        tile_ef = sb("tile_ef", [P, TILES])
        tile_e = sb("tile_e", [P, TILES], i32)
        xt = [sb(f"xt{i}", [P, ROW]) for i in range(5)]
        yt = [sb(f"yt{i}", [P, D]) for i in range(5)]
        tile_ids = [sb(f"tile_ids{i}", [P, 1], i32) for i in range(5)]
        slot_ids = sb("slot_ids", [P, TILES], i32)
        xtT = sb("xtT", [P, P])
        w1_t = [sb(f"w1_t{i}", [P, FF + KF]) for i in range(5)]
        h_T = sb("h_T", [P, FF])
        half_w = sb("half_w", [P, NT])
        y_tok = moe_w1[:, :, :].rearrange("p e f -> p (e f)")[:, 0:B * S].rearrange("p (b s) -> p b s", b=B)
        th_y = xn

        x_in = [sem(f"x_in{b}") for b in range(B)]
        kqv_in, m1_in, rows_in, gate_in, floor_in = sem("kqv_in"), sem("m1_in"), sem("rows_in"), sem("gate_in"), sem("floor_in")
        w2_in, f1_in, f2_in, ln_in = sem("w2_in"), sem("f1_in"), sem("f2_in"), sem("ln_in")
        experts_in, bias1_in = sem("experts_in"), sem("bias1_in")
        const_made = sem("const_made")
        fill_made, filled_out = sem("fill_made"), sem("filled_out")
        col_made, ids_made = sem("col_made"), sem("ids_made")
        ln_chain, ln_var, ln_rstd = sem("ln_chain"), sem("ln_var"), sem("ln_rstd")
        ln_shift = sem("ln_shift")
        x_chain, x_var, x_rstd, x_shift = sem("x_chain"), sem("x_var"), sem("x_rstd"), sem("x_shift")
        xn_last = sem("xn_last")
        xn_done, pe_xT, xT_done, pe_gate = sem("xn_done"), sem("pe_xT"), sem("xT_done"), sem("pe_gate")
        pe_wT, wT_done, pe_prod, prod_done = sem("pe_wT"), sem("wT_done"), sem("pe_prod"), sem("prod_done")
        pe_rows, rows_done, pe_fb, fb_done = sem("pe_rows"), sem("rows_done"), sem("pe_fb"), sem("fb_done")
        par_done = sem("par_done")
        r_step, r_exp, pe_prefix, route_done = sem("r_step"), sem("r_exp"), sem("pe_prefix"), sem("route_done")
        slots_found = sem("slots_found")
        r_shift = sem("r_shift")
        scattered = sem("scattered")
        m_set, w_set, w2_set = sem("m_set"), sem("w_set"), sem("w2_set")
        f1_set, f2_set, ln_set = sem("f1_set"), sem("f2_set"), sem("ln_set")
        pe_S, pe_q, pe_A, pe_u, pe_uT = sem("pe_S"), sem("pe_q"), sem("pe_A"), sem("pe_u"), sem("pe_uT")
        pe_g, pe_a, pe_w2, pe_gn, pe_f1 = sem("pe_g"), sem("pe_a"), sem("pe_w2"), sem("pe_gn"), sem("pe_f1")
        pe_z, pe_zT = sem("pe_z"), sem("pe_zT")
        S_part, S_done, q_done, A_done = sem("S_part"), sem("S_done"), sem("q_done"), sem("A_done")
        u_chain, u_done, uT_done = sem("u_chain"), sem("u_done"), sem("uT_done")
        gg_done, th_done, gt_done, act_done = sem("gg_done"), sem("th_done"), sem("gt_done"), sem("act_done")
        gs_chain, gs_done = sem("gs_chain"), sem("gs_done")
        gn_chain, gn_var, gn_rstd, gn_affine = sem("gn_chain"), sem("gn_var"), sem("gn_rstd"), sem("gn_affine")
        gn_done, y_done, G_done = sem("gn_done"), sem("y_done"), sem("G_done")
        z_half, part_made, w_split = sem("z_half"), sem("part_made"), sem("w_split")
        f1_parts_set, uT_split, y_high, y_split = sem("f1_parts_set"), sem("uT_split"), sem("y_high"), sem("y_split")
        z_done, hg_done, htok_done, hT_done = sem("z_done"), sem("hg_done"), sem("htok_done"), sem("hT_done")
        xt_in = [sem(f"xt_in{i}") for i in range(5)]
        yt_out = [sem(f"yt_out{i}") for i in range(5)]
        yt_zeroed = sem("yt_zeroed")
        ids_in, ids_set = sem("ids_in"), sem("ids_set")
        w1_in = [sem(f"w1_in{i}") for i in range(5)]
        pe_xt, xtT_done, pe_h, h_done = sem("pe_xt"), sem("xtT_done"), sem("pe_h"), sem("h_done")
        pe_y, yt_done = sem("pe_y"), sem("yt_done")
        y_in = [sem(f"y_in{b}") for b in range(B)]
        e_half, e_th, e_silu, e_weighed = sem("e_half"), sem("e_th"), sem("e_silu"), sem("e_weighed")
        e_s, e_last, dve_out, pool_out = sem("e_s"), sem("e_last"), sem("dve_out"), sem("pool_out")
        out_done, passed = sem("out_done"), sem("passed")

        block = ctx.enter_context(nc.Block())

        def need(eng, s, v):
            if not isinstance(v, int) or v > 0:
                eng.wait_ge(s, v)

        def alone(eng, s, v):
            eng.wait_ge(s, v)
            if not isinstance(v, int):
                eng.sem_inc(passed, 1)

        def steps(eng, step, turns, width, lag):
            for t in range(width):
                step(0, t)
            with eng.Fori(1, turns) as l:
                for t in range(width):
                    step(l, t)
            for t in range(lag):
                step(turns, t)

        def at(l, t, late, width, count):
            b, l = (t - late) % width, l + (t - late) // width
            if isinstance(l, int) and (l < 0 or l * width + b >= count):
                return None
            return l * width + b, b, l

        LB = L * B
        LAG = 3

        EARLY, LATE = range(2)
        FIRST_TURNS = [(B - 1, EARLY), (B - 1, LATE)]
        TURNS = [[LATE] if t in (0, 3, 5) else [EARLY, LATE] for t in range(B)]
        assert sum(map(len, TURNS)) == TURN_TILES and EARLY not in TURNS[0]

        def turn(l, t, place):
            if isinstance(l, int) and (l == 0 or l >= L):
                if l == 0 and (t, place) in FIRST_TURNS:
                    j = FIRST_TURNS.index((t, place))
                    return j, TURN_TILES - TILE_LAG + j
                return None
            if place not in TURNS[t]:
                return None
            k = sum(map(len, TURNS[:t])) + TURNS[t].index(place)
            return (l - 1) * TURN_TILES + TILE_LAG + k, k

        def turns_before(l, t, place):
            if isinstance(l, int) and l == 0:
                return sum(at < (t, place) for at in FIRST_TURNS)
            if isinstance(l, int) and l >= L:
                return TILES
            k = sum(map(len, TURNS[:t])) + sum(p < place for p in TURNS[t])
            return (l - 1) * TURN_TILES + TILE_LAG + k

        def parted(l, t):
            return turn(l, t, EARLY) is not None and not (isinstance(l, int) and l == 0)

        def parted_steps(l, t):
            early = [k for k in range(B) if EARLY in TURNS[k]]
            return (l - 1) * len(early) + early.index(t) + 1

        def halves(l, t):
            return (0, 1) if parted(l, t) else (1, 0)

        def first_turns(j):
            return isinstance(j, int) and j < TILE_LAG

        def buffer_of(k):
            return k % 4 if k < 12 else 4

        FIRST_BUFFERS = [buffer_of(TURN_TILES - TILE_LAG + j) for j in range(TILE_LAG)]

        def used_before(l, k):
            return (l - 1) * (3 if k < 12 else 1) + (k // 4 if k < 12 else 0)

        def loaded_before(l, k):
            if isinstance(l, int) and l == 0:
                return 0
            return used_before(l, k) + (1 if buffer_of(k) in FIRST_BUFFERS else 0)

        LAST_B = B - 1
        ORDER = [LAST_B] + list(range(B - 1))
        DVE_OUT = [0, 1, LAST_B, 5, 6]
        POOL_OUT = [2, 3, 4]
        assert sorted(DVE_OUT + POOL_OUT) == list(range(B))

        def nth(order, b):
            return order.index(b) + 1

        @block.sync
        def _(sp):
            def load_x(b):
                sp.dma_start(x_sb[:, b * C:(b + 1) * C, :],
                             x[b].rearrange("(c p) d -> p c d", p=P)).then_inc(x_in[b], 16)

            load_x(0)
            load_x(1)
            sp.dma_start(wm1_sb, Wm1.rearrange("l p f -> p l f")).then_inc(m1_in, 16)
            for b in range(2, 6):
                load_x(b)
            sp.dma_start(gate_sb[:, :], gate_w).then_inc(gate_in, 16)
            load_x(6)
            load_x(7)
            for v, r in ((bm1.rearrange("l (k p) -> (l k) p", p=P), R_BM1), (bm2, R_BM2), (gn_g, R_GG),
                         (gn_b, R_GB), (bf1.rearrange("l (k p) -> (l k) p", p=P), R_BF1), (bf2, R_BF2),
                         (ln_g, R_LG), (ln_b, R_LB)):
                sp.dma_start(rows[r:r + v.shape[0], :], v).then_inc(rows_in, 16)
            sp.dma_start(all_f1[:, :, :], Wf1.rearrange("l p f -> p l f")).then_inc(f1_in, 16)
            sp.dma_start(floor_sb[:, :], row_floor).then_inc(floor_in, 16)
            sp.dma_start(b1_rows[:, :], b1.rearrange("e (k p) -> (e k) p", p=P)).then_inc(bias1_in, 16)
            sp.dma_start(all_w2[:, :, :], Wm2.rearrange("l p d -> p l d")).then_inc(w2_in, 16)
            sp.dma_start(all_f2[:, :, :, :].rearrange("p l k d -> p (l k) d"),
                         Wf2.rearrange("l (k p) d -> p (l k) d", p=P)).then_inc(f2_in, 16)
            sp.dma_start(all_lg[:, :, :], ln_g.partition_broadcast(P)).then_inc(ln_in, 16)
            sp.dma_start(all_lb[:, :, :], ln_b.partition_broadcast(P)).then_inc(ln_in, 16)
            sp.wait_ge(fill_made, 2)
            slots = x_slots.rearrange("(t p) w -> p t w", p=P)
            sp.dma_start(slots[:, :, 0:H1],
                         fill.unsqueeze(1).broadcast_to([P, TILES, H1])).then_inc(filled_out, 16)
            with nc.allow_non_contiguous_dma(reason="one word a slot"):
                sp.dma_start(slots[:, :, H1:ROW].rearrange("p t w -> p (t w)"),
                             fill_id[:, :].bitcast(f32)).then_inc(filled_out, 16)
            sp.dma_start(moe_w1[:, :, 0:FF], w1.rearrange("e p f -> p e f")).then_inc(experts_in, 16)
            sp.dma_start(moe_b2[:, :, :], b2.partition_broadcast(P)).then_inc(experts_in, 16)
            sp.wait_ge(prod_done, L)
            sp.wait_ge(filled_out, 32)
            sp.wait_ge(w_split, 1)
            sp.dma_start(moe_w2[:, :, :, :].rearrange("p e k d -> p (e k) d"),
                         w2.rearrange("e (k p) d -> p (e k) d", p=P)).then_inc(experts_in, 16)
            sp.wait_ge(scattered, 16 * NT)
            sp.wait_ge(experts_in, 48)
            sp.wait_ge(fb_done, 1)
            sp.wait_ge(route_done, 1)

            def load_tile(j, k):
                if not isinstance(j, int):
                    alone(sp, pe_xt, j - TILE_LAG + 1)
                q = buffer_of(k)
                sp.dma_start(xt[q][:, :], x_slots[bass.ds(j * P, P), :]).then_inc(xt_in[q], 16)
                e = sp.value_load(tile_e[0:1, bass.ds(j, 1)], min_val=0, max_val=E - 1)
                sp.dma_start(w1_t[q][:, :], moe_w1[:, bass.ds(e, 1), :].rearrange("p a f -> p (a f)"))\
                    .then_inc(w1_in[q], 16)

            for j in range(TILE_LAG):
                load_tile(j, TURN_TILES - TILE_LAG + j)
            with nc.allow_non_contiguous_dma(reason="one word a slot"):
                sp.dma_start(slot_ids[:, :].bitcast(f32), slots[:, :, H1:ROW].rearrange("p t w -> p (t w)"))\
                    .then_inc(ids_in, 16)
            with sp.Fori(1, L) as l:
                for k in range(TURN_TILES):
                    load_tile((l - 1) * TURN_TILES + TILE_LAG + k, k)
            for q in range(5):
                sp.wait_ge(yt_out[q], 16 * (1 + used_before(L, q if q < 4 else 12)))
            for q in range(5):
                k = q + 8 if q < 4 else 12
                sp.wait_ge(w1_in[q], 16 * (loaded_before(L - 1, k) + 1))
            for b in ORDER:
                sp.dma_start(y_tok[:, b, :].rearrange("p (c d) -> p c d", c=C),
                             y_rows[b * S:(b + 1) * S, :].rearrange("(c p) d -> p c d", p=P)).then_inc(y_in[b], 16)
            for b in (0, 1, LAST_B, 2, 3, 5, 4, 6):
                if b in DVE_OUT:
                    sp.wait_ge(dve_out, nth(DVE_OUT, b))
                else:
                    sp.wait_ge(pool_out, nth(POOL_OUT, b))
                sp.dma_start(out[b].rearrange("(c p) d -> p c d", p=P),
                             y_tok[:, b, :].rearrange("p (c d) -> p c d", c=C)).then_inc(out_done, 16)
            sp.wait_ge(out_done, 16 * B)

        @block.gpsimd
        def _(pool):
            pool.memset(ones[:, :], 1.0).then_inc(const_made, 1)
            pool.memset(half_neg[:, :], -0.5).then_inc(const_made, 1)
            pool.memset(mean_of[:, :], 1.0 / D).then_inc(const_made, 1)
            pool.wait_ge(const_made, 1)
            pool.affine_select(out=ident[:, :], in_=ones[:, 0:P], compare_op=ALU.is_equal, fill=0.0, base=0,
                               pattern=[[-1, P]], channel_multiplier=1).then_inc(const_made, 1)
            pool.affine_select(out=causal[:, :], in_=ones[:, 0:P], compare_op=ALU.is_ge, fill=0.0, base=0,
                               pattern=[[1, P]], channel_multiplier=-1).then_inc(const_made, 1)
            pool.affine_select(out=before[:, :], in_=ones[:, 0:P], compare_op=ALU.is_gt, fill=0.0, base=0,
                               pattern=[[1, P]], channel_multiplier=-1).then_inc(const_made, 1)
            pool.memset(fill, 0.0).then_inc(fill_made, 1)
            pool.iota(fill_id[:, :], pattern=[[P, TILES]], base=TOK, channel_multiplier=1)\
                .then_inc(fill_made, 1)
            pool.memset(xn[:, :, D:H1], 1.0).then_inc(col_made, 1)
            pool.memset(htok[:, :, D:H1], 1.0).then_inc(col_made, 1)
            pool.iota(xn[:, :, H1:ROW].rearrange("p t w -> p (t w)").bitcast(i32), pattern=[[P, NT]],
                      base=0, channel_multiplier=1).then_inc(ids_made, 1)
            pool.iota(iota_e[:, :], pattern=[[1, E]], base=-E, channel_multiplier=0,
                      allow_small_or_imprecise_dtypes=True).then_inc(ids_made, 1)
            pool.iota(tile_at[:, :], pattern=[[1, TILES]], base=0, channel_multiplier=0,
                      allow_small_or_imprecise_dtypes=True).then_inc(ids_made, 1)
            pool.iota(filled[:, :], pattern=[[P, NT]], base=0, channel_multiplier=0,
                      allow_small_or_imprecise_dtypes=True).then_inc(ids_made, 1)

            def ln_pow(k, b):
                pool.wait_ge(ln_var, k + 1)
                pool.tensor_tensor(ln_rs[:, b % 2, :], ln_ve[:, b % 2, :], half_neg[:, :], ALU.pow)\
                    .then_inc(ln_rstd, 1)

            pool.wait_ge(const_made, 6)
            for b in range(B):
                of_b = slice(b * C, (b + 1) * C)
                pool.wait_ge(x_var, b + 1)
                pool.tensor_tensor(x_rs[:, of_b], x_ve[:, of_b], half_neg[:, :], ALU.pow).then_inc(x_rstd, 1)

            def set_m(l):
                need(pool, pe_q, (l + 1) * B)
                pool.tensor_copy(m_l[:, :], next_m[:, l, :]).then_inc(m_set, 1)

            def set_w(l):
                need(pool, pe_a, l * B)
                need(pool, th_done, l * B)
                need(pool, gg_done, l * B)
                need(pool, act_done, l * B)
                pool.tensor_copy(par[:, GATE_B:VAL_B + 1], all_par[:, l, GATE_B:VAL_B + 1])
                pool.tensor_copy(w_l[:, :, :], all_w[:, l, :, :]).then_inc(w_set, 1)

            def set_w2(l):
                need(pool, pe_w2, l * B)
                need(pool, gn_affine, l * B)
                pool.tensor_copy(w2_l[:, :], all_w2[:, l, :])
                pool.tensor_copy(par[:, W2_B:GN_B + 1], all_par[:, l, W2_B:GN_B + 1]).then_inc(w2_set, 1)

            def set_f1(l):
                need(pool, G_done, l * B * 2)
                if isinstance(l, int) and l == 0:
                    pool.wait_ge(fb_done, 1)
                pool.tensor_copy(par[:, F_B:F_B + 2], all_par[:, l, F_B:F_B + 2])
                pool.tensor_copy(f1_l[:, :], all_f1[:, l, :]).then_inc(f1_set, 1)

            def set_f2(l):
                need(pool, pe_z, l * B)
                pool.tensor_copy(f2_l[:, :, :], all_f2[:, l, :, :]).then_inc(f2_set, 1)

            def set_ln(l):
                need(pool, hT_done, l * B)
                need(pool, htok_done, l * B)
                pool.tensor_copy(par[:, LN_G:LN_B + 1], all_par[:, l, LN_G:LN_B + 1])
                pool.tensor_copy(lg_l[:, :], all_lg[:, l, :])
                pool.tensor_copy(lb_l[:, :], all_lb[:, l, :]).then_inc(ln_set, 1)

            pool.wait_ge(prod_done, L)
            pool.tensor_copy(m_l[:, :], next_m[:, L - 1, :]).then_inc(m_set, 1)
            parts = [0]

            def split(whole, high, low):
                pool.tensor_copy(high, whole).then_inc(part_made, 1)
                parts[0] += 1
                pool.wait_ge(part_made, parts[0])
                pool.tensor_tensor(low, whole, high, ALU.subtract).then_inc(part_made, 1)
                parts[0] += 1
                pool.wait_ge(part_made, parts[0])

            def split_w(l):
                split(w_whole[l], all_w[:, l, 0, :], all_w[:, l, 1, :])

            def split_f1(l):
                split(all_f1[:, l, :], f1_parts[:, l, 0, :], f1_parts[:, l, 1, :])

            split_w(0)
            pool.wait_ge(par_done, 1)
            pool.wait_ge(w2_in, 16)
            pool.wait_ge(f1_in, 16)
            pool.wait_ge(f2_in, 16)
            pool.wait_ge(ln_in, 32)

            SCATTERS = {2: (0, 2, 4), 3: (2, 1, 4), 4: (2, 1, 4), 5: (2, 1, 4), 6: (2, 1, 2)}
            assert sum(map(sum, SCATTERS.values())) == NT

            def scatter(l, t, place):
                if not (isinstance(l, int) and l == 0 and t in SCATTERS):
                    return
                start = sum(sum(SCATTERS[k]) for k in SCATTERS if k < t) + sum(SCATTERS[t][:place])
                if start == 0 and SCATTERS[t][place]:
                    pool.wait_ge(slots_found, 1)
                    pool.wait_ge(filled_out, 32)
                for k in range(start, start + SCATTERS[t][place]):
                    pool.indirect_dma_start(x_slots[:, :], bass.IndirectOffsetOnAxis(ap=pos[:, k:k + 1], axis=0),
                                            xn[:, k, :], None).then_inc(scattered, 16)

            def weigh(b):
                pool.wait_ge(e_silu, nth(ORDER, b))
                y = y_tok[:, b, :].rearrange("p (c d) -> p c d", c=C)
                pool.tensor_tensor(y, y, half_w[:, b * C:(b + 1) * C].unsqueeze(2).broadcast_to([P, C, D]),
                                   ALU.mult).then_inc(e_weighed, 1)

            def add_x(b):
                pool.wait_ge(e_s, b + 1)
                pool.tensor_tensor(y_tok[:, b, :], y_tok[:, b, :],
                                   x_sb[:, b * C:(b + 1) * C, :].rearrange("p c d -> p (c d)"), ALU.add)\
                    .then_inc(pool_out, 1)

            def step(l, t):
                first = isinstance(l, int) and l == 0
                ends = isinstance(l, int) and l == L
                if not ends and t in (1, 2):
                    (set_w2 if t == 1 else set_f2)(l)
                w = at(l, t, 3, B, LB)
                if w and w[0] is not LB - 1:
                    n, b, _ = w
                    if b == 0:
                        pool.wait_ge(ln_set, w[2] + 1)
                    pool.wait_ge(pe_zT, n + 1)
                    pool.tensor_tensor(zhat[:, b % 2, :, :], zhat[:, b % 2, :, :],
                                       lg_l[:, :].unsqueeze(1).broadcast_to([P, C, D]), ALU.mult)\
                        .then_inc(hg_done, 1)
                    pool.wait_ge(hg_done, n + 1)
                    pool.tensor_tensor(htok[:, b * C:(b + 1) * C, 0:D], zhat[:, b % 2, :, :],
                                       lb_l[:, :].unsqueeze(1).broadcast_to([P, C, D]), ALU.add)\
                        .then_inc(htok_done, 1)
                tile_rows(l, t, EARLY)
                scatter(l, t, 0)
                if not ends and t in (0, 1, 2, B - 1):
                    if not (first and t == 1):
                        {0: set_w, 1: set_f1, 2: set_ln, B - 1: set_m}[t](l)
                if first and t == B - 1:
                    for k in range(1, L - 1):
                        split_f1(k)
                tile_rows(l, t, LATE)
                if ends and t == 1:
                    weigh(2)
                if first and t == 1:
                    first_rows()
                if w := at(l, t, 1, B, LB):
                    pool.wait_ge(gn_var, w[0] + 1)
                    pool.tensor_tensor(gn_rs[:, :], gn_ve[:, :], half_neg[:, 0:1], ALU.pow).then_inc(gn_rstd, 1)
                scatter(l, t, 1)
                if w := at(l, t, 2, B, LB):
                    ln_pow(w[0], w[1])
                if first and t == 1:
                    set_f1(l)
                if first and t == B - 1:
                    split_f1(L - 1)
                scatter(l, t, 2)
                if ends and t == 0:
                    for b in (LAST_B, 0, 1):
                        weigh(b)
                if ends and t == 1:
                    for b in (3, 4, 5, 6):
                        weigh(b)
                if ends and t == 2:
                    for b in POOL_OUT:
                        add_x(b)

            def tile_rows(l, t, place):
                w = turn(l, t, place)
                if w is None or first_turns(w[0]):
                    return
                j, k = w
                q = buffer_of(k)
                pool.wait_ge(yt_out[q], 16 * (1 + used_before(l, k)))
                pool.tensor_copy(tile_ids[q][:, :], slot_ids[:, bass.ds(j - TILE_LAG, 1)]).then_inc(ids_set, 1)
                alone(pool, ids_set, j - TILE_LAG + 1)
                alone(pool, yt_done, j - TILE_LAG + 1)
                pool.indirect_dma_start(y_rows[:, :], bass.IndirectOffsetOnAxis(ap=tile_ids[q][:, :], axis=0),
                                        yt[q][:, :], None).then_inc(yt_out[q], 16)

            def first_rows():
                for q in range(5):
                    pool.memset(yt[q][:, :], 0.0).then_inc(yt_zeroed, 1)
                    pool.tensor_copy(tile_ids[q][:, :], fill_id[:, q:q + 1]).then_inc(yt_zeroed, 1)
                pool.wait_ge(yt_zeroed, 10)
                for q in range(5):
                    pool.indirect_dma_start(y_rows[:, :], bass.IndirectOffsetOnAxis(ap=tile_ids[q][:, :], axis=0),
                                            yt[q][:, :], None).then_inc(yt_out[q], 16)

            for t in range(B):
                step(0, t)
                if t == 0:
                    split_f1(0)
                    for l in range(1, L):
                        split_w(l)
                    pool.sem_inc(w_split, 1)
                if t == B - 1:
                    pool.sem_inc(w_split, 1)
            pool.wait_ge(ids_in, 16)
            with pool.Fori(1, L) as l:
                for t in range(B):
                    step(l, t)
            for t in range(LAG):
                step(L, t)

        @block.scalar
        def _(act):
            act.dma_start(wkqv_sb, Wkqv.rearrange("l p f -> p l f")).then_inc(kqv_in, 16)

            for b in range(B + 1):
                if b < B:
                    act.wait_ge(x_shift, b + 1)
                    for c in range(C - 1):
                        k = b * C + c
                        last = act.activation(xn[:, k, 0:D], x_sb[:, k, :], ACT.Identity, bias=x_nb[:, k:k + 1],
                                              scale=x_rs[:, k:k + 1])
                    last.then_inc(xn_done, 1)
                if b:
                    act.wait_ge(pe_xT, b)
                    act.activation(hT[:, b - 1, :], pair[:, (b - 1) % 2, :], ACT.Copy).then_inc(xT_done, 1)
                if 1 <= b <= L:
                    act.wait_ge(pe_wT, b)
                    need(act, pe_prod, b - 2)
                    act.activation(wT_sb[(b - 1) % 2], bank[2 + (b - 1) % 2][:, 0:3 * D], ACT.Copy)\
                        .then_inc(wT_done, 1)

            def tile_gelu(w):
                if w is not None and not (isinstance(w[0], int) and w[0] < 1):
                    j, k = w
                    act.wait_ge(pe_h, j)
                    for i in range(KF):
                        last = act.activation(h_T[:, i * P:(i + 1) * P], bank[5][:, i * P:(i + 1) * P], ACT.Gelu,
                                              bias=w1_t[buffer_of((k - 1) % TURN_TILES)][:, FF + i:FF + i + 1])
                    last.then_inc(h_done, 1)

            def gate(l, t):
                if w := at(l, t, 1, B, LB):
                    act.wait_ge(pe_g, w[0] + 1)
                    act.activation(th_sb[:, :], bank[3][:, :], ACT.Tanh, bias=par[:, GATE_B:GATE_B + 1],
                                   scale=0.5).then_inc(th_done, 1)
                    act.activation(gg_sb[:, :], bank[3][:, :], ACT.Identity, bias=par[:, GATE_B:GATE_B + 1],
                                   scale=0.5).then_inc(gg_done, 1)

            def layernorm(l, t):
                if w := at(l, t, 3, B, LB):
                    n, b, _ = w
                    act.wait_ge(z_half, n + 1)
                    for c in range(C // 2, C):
                        last = act.activation(zhat[:, b % 2, c, :], bank[7][:, c * D:(c + 1) * D], ACT.Identity,
                                              bias=ln_nb[:, b % 2, c:c + 1], scale=ln_rs[:, b % 2, c:c + 1])
                    last.then_inc(z_done, 1)

            def late_turn_before(l, t):
                if EARLY in TURNS[t] or isinstance(l, int):
                    return None
                return turn(l, t - 1, LATE) if t else ((l - 1) * TURN_TILES + TILE_LAG - 1, TURN_TILES - 1)

            def tanh_y(b):
                act.wait_ge(y_in[b], 16)
                for c in range(C):
                    k = b * C + c
                    last = act.activation(th_y[:, k, 0:D], y_tok[:, b, c * D:(c + 1) * D], ACT.Tanh,
                                          scale=half_w[:, k:k + 1])
                last.then_inc(e_th, 1)

            def queries(l, t):
                if w := at(l, t, 0, B, LB):
                    act.wait_ge(pe_q, w[0] + 1)
                    act.activation(q_sb[:, :], pair[:, 0, :], ACT.Copy).then_inc(q_done, 1)

            def step(l, t):
                first = isinstance(l, int) and l == 0
                ends = isinstance(l, int) and l == L
                if not first or t < 2:
                    queries(l, t)
                if parted(l, t):
                    w = at(l, t, 2, B, LB)
                    act.wait_ge(y_done, w[0] + 1)
                    act.activation(y_h[:, :], y_sb[:, :], ACT.Copy).then_inc(y_high, 1)
                if not parted(l, t):
                    gate(l, t)
                layernorm(l, t)
                tile_gelu(late_turn_before(l, t))
                if parted(l, t):
                    gate(l, t)
                if first and t == 1:
                    act.wait_ge(r_shift, 1)
                    act.activation(r_a[:, :, :], r_c[:, :, :], ACT.Exp).then_inc(r_exp, 1)
                tile_gelu(turn(l, t, EARLY))
                if w := at(l, t, 2, B, LB):
                    for i, k in enumerate(halves(l, t)):
                        act.wait_ge(pe_f1, w[0] * 2 + i + 1)
                        act.activation(G_sb[:, k, :], bank[3 + k][:, :], ACT.Gelu,
                                       bias=par[:, F_B + k:F_B + k + 1]).then_inc(G_done, 1)
                w = at(l, t, 3, B, LB)
                if w and w[0] is not LB - 1:
                    n, b, _ = w
                    act.wait_ge(pe_zT, n + 1)
                    if b == 0:
                        act.wait_ge(ln_set, w[2] + 1)
                    act.activation(hT[:, b, :], bank[7][:, :], ACT.Identity, bias=par[:, LN_B:LN_B + 1],
                                   scale=par[:, LN_G:LN_G + 1]).then_inc(hT_done, 1)
                if t == (B - 2 if first else 1) and not ends:
                    act.wait_ge(w_split, 1 if first else 2)
                    act.activation(f1_parts_l[:, :, :], f1_parts[:, l, :, :], ACT.Copy).then_inc(f1_parts_set, 1)
                if ends and t == 0:
                    act.wait_ge(e_half, 1)
                    act.wait_ge(scattered, 16 * NT)
                    for b in ORDER[:3]:
                        tanh_y(b)
                if ends and t == 1:
                    for b in ORDER[3:]:
                        tanh_y(b)
                if w := at(l, t, 0, B, LB):
                    act.wait_ge(pe_uT, w[0] + 1)
                    act.activation(uT_h[:, :], bank[2][:, :], ACT.Copy).then_inc(uT_done, 1)
                if first and 1 <= t < B - 1:
                    queries(l, t + 1)
                if w := at(l, t, 1, B, LB):
                    act.wait_ge(gn_affine, w[0] + 1)
                    act.activation(y_sb[:, :], bank[6][:, :], ACT.Identity, bias=gn_bi[:, :],
                                   scale=gn_sc[:, :]).then_inc(gn_done, 1)
                if EARLY in TURNS[(t + 1) % B]:
                    tile_gelu(turn(l, t, LATE))

            steps(act, step, L, B, LAG)

        @block.vector
        def _(dve):
            loaded = {}

            def ln_stats(k, b):
                for c in range(C):
                    last = dve.bn_stats(ln_st[:, b % 2, c, :], bank[7][:, c * D:(c + 1) * D])
                last.then_inc(ln_chain, 1)

            def ln_moments(k, b):
                alone(dve, ln_chain, 2 * k + 1)
                for c in range(C):
                    last = dve.bn_aggr(ln_mv[:, b % 2, c, :], ln_st[:, b % 2, c, :])
                last.then_inc(ln_chain, 1)
                dve.wait_ge(ln_chain, 2 * k + 2)
                dve.tensor_scalar(ln_ve[:, b % 2, :], ln_mv[:, b % 2, :, 1], EPS, None, ALU.add)\
                    .then_inc(ln_var, 1)

            def ln_shifts(k, b):
                dve.wait_ge(ln_rstd, k + 1)
                dve.scalar_tensor_tensor(ln_nb[:, b % 2, :], ln_mv[:, b % 2, :, 0], -1.0, ln_rs[:, b % 2, :],
                                         ALU.mult, ALU.mult).then_inc(ln_shift, 1)

            bm1T = rowsT[:, R_BM1:R_BM1 + 2 * L].rearrange("p (l k) -> p l k", k=2)
            bf1T = rowsT[:, R_BF1:R_BF1 + 2 * L].rearrange("p (l k) -> p l k", k=2)

            def products(l):
                dve.wait_ge(pe_prod, l + 1)
                src = bank[4 + l % 2]
                dve.tensor_copy(next_m[:, (l - 1) % L, :], src[:, 0:D])
                dve.tensor_copy(w_whole[l], src[:, D:3 * D]).then_inc(prod_done, 1)

            x_steps = [0]

            def x_step(inst):
                inst.then_inc(x_chain, 1)
                x_steps[0] += 1
                return x_steps[0]

            for b in range(B + 1):
                of_b, of_last = slice(b * C, (b + 1) * C), slice((b - 1) * C, b * C)
                if b < B:
                    dve.wait_ge(x_in[b], 16)
                    for c in range(C):
                        last = dve.bn_stats(x_st[:, b * C + c, :], x_sb[:, b * C + c, :])
                    chained = x_step(last)
                if b:
                    dve.wait_ge(x_rstd, b)
                    dve.scalar_tensor_tensor(x_nb[:, of_last], x_mv[:, of_last, 0], -1.0, x_rs[:, of_last],
                                             ALU.mult, ALU.mult).then_inc(x_shift, 1)
                if b < B:
                    alone(dve, x_chain, chained)
                    for c in range(C):
                        last = dve.bn_aggr(x_mv[:, b * C + c, :], x_st[:, b * C + c, :])
                    chained = x_step(last)
                if b:
                    k = b * C - 1
                    dve.wait_ge(x_shift, b)
                    dve.tensor_scalar(xn[:, k, 0:D], x_sb[:, k, :], x_rs[:, k:k + 1], x_nb[:, k:k + 1],
                                      ALU.mult, ALU.add).then_inc(xn_last, 1)
                if b < B:
                    dve.wait_ge(x_chain, chained)
                    dve.tensor_scalar(x_ve[:, of_b], x_mv[:, of_b, 1], EPS, None, ALU.add).then_inc(x_var, 1)
                if 4 <= b < 4 + L:
                    products(b - 4)
            dve.wait_ge(pe_rows, 1)
            dve.tensor_copy(rowsT[:, :], bank[6][:, 0:NROWS]).then_inc(rows_done, 1)
            dve.wait_ge(rows_done, 1)
            dve.tensor_scalar(all_par[:, :, GATE_B], bm1T[:, :, 1], 0.5, None, ALU.mult)
            dve.tensor_copy(all_par[:, :, VAL_B], bm1T[:, :, 0])
            dve.tensor_copy(all_par[:, :, W2_B], rowsT[:, R_BM2:R_BM2 + L])
            dve.tensor_copy(all_par[:, :, GN_G], rowsT[:, R_GG:R_GG + L])
            dve.tensor_tensor(all_par[:, :, GN_B], rowsT[:, R_GB:R_GB + L], rowsT[:, R_BF2:R_BF2 + L], ALU.add)
            dve.tensor_copy(all_par[:, :, LN_G], rowsT[:, R_LG:R_LG + L])
            dve.tensor_copy(all_par[:, :, LN_B], rowsT[:, R_LB:R_LB + L]).then_inc(par_done, 1)

            def gelu_bias():
                dve.wait_ge(pe_fb, 1)
                dve.tensor_tensor(all_par[:, :, F_B:F_B + 2], bf1T, bank[7][:, 0:2 * L]
                                  .rearrange("p (l k) -> p l k", k=2), ALU.subtract)
                dve.tensor_copy(moe_w1[:, :, FF:FF + KF], bank[7][:, 2 * L:2 * L + E * KF]
                                .rearrange("p (e k) -> p e k", k=KF)).then_inc(fb_done, 1)

            done = [0]

            def chain(inst):
                inst.then_inc(r_step, 1)
                done[0] += 1
                dve.wait_ge(r_step, done[0])

            def over_e(v):
                return v.unsqueeze(2).broadcast_to([P, NT, E])

            def over_t(v):
                return v.unsqueeze(1).broadcast_to([P, NT, E])

            def shift_logits():
                dve.wait_ge(ids_made, 4)
                dve.wait_ge(pe_gate, B)
                chain(dve.tensor_copy(r_lg[:, :, :].rearrange("p t e -> p (t e)"), bank[7][:, 0:TE]))
                chain(dve.tensor_reduce(r_mx[:, :], r_lg[:, :, :], AX, ALU.max))
                dve.tensor_tensor(r_c[:, :, :], r_lg[:, :, :], over_e(r_mx[:, :]), ALU.subtract).then_inc(r_shift, 1)

            def choose_expert():
                chain(dve.tensor_tensor(r_oh[:, :, :], r_lg[:, :, :], over_e(r_mx[:, :]), ALU.is_equal))
                chain(dve.tensor_tensor(r_lg[:, :, :], r_oh[:, :, :], over_t(iota_e[:, :]), ALU.mult))
                chain(dve.tensor_reduce(r_ix[:, :], r_lg[:, :, :], AX, ALU.min))
                dve.tensor_tensor(r_oh[:, :, :], over_t(iota_e[:, :]), over_e(r_ix[:, :]), ALU.is_equal)\
                    .then_inc(r_shift, 1)

            def expert_weight():
                dve.wait_ge(r_exp, 1)
                chain(dve.tensor_reduce(r_sum[:, :], r_a[:, :, :], AX, ALU.add))
                chain(dve.reciprocal(weight[:, :], r_sum[:, :]))
                dve.tensor_scalar(half_w[:, :], weight[:, :], 0.5, None, ALU.mult).then_inc(e_half, 1)

            prefix = bank[5][:, 0:TE].rearrange("p (t e) -> p t e", e=E)
            total = bank[5][:, TE:2 * TE].rearrange("p (t e) -> p t e", e=E)

            def count_tokens():
                dve.wait_ge(pe_prefix, 1)
                chain(dve.tensor_copy(r_tot[:, :, :], total.rearrange("p t e -> p e t")))
                chain(dve.tensor_tensor_scan(r_cum[:, :, :].rearrange("p e t -> p (e t)"), ones[:, 0:TE],
                                             r_tot[:, :, :].rearrange("p e t -> p (e t)"), 0.0, ALU.mult, ALU.add))
                chain(dve.memset(r_prev[:, :], 0.0))
                chain(dve.tensor_copy(r_prev[:, 1:E], r_cum[:, 0:E - 1, NT - 1]))
                chain(dve.tensor_tensor(r_n[:, :], r_cum[:, :, NT - 1], r_prev[:, :], ALU.subtract))

            def count_tiles():
                chain(dve.tensor_tensor(r_k[:, :, :], r_n[:, :].unsqueeze(2).broadcast_to([P, E, NT]),
                                        filled[:, :].unsqueeze(1).broadcast_to([P, E, NT]), ALU.is_gt))
                chain(dve.tensor_reduce(r_nt[:, :], r_k[:, :, :], AX, ALU.add))
                chain(dve.tensor_tensor_scan(r_end[:, :], ones[:, 0:E], r_nt[:, :], 0.0, ALU.mult, ALU.add))
                chain(dve.tensor_tensor(r_base[:, :], r_end[:, :], r_nt[:, :], ALU.subtract))
                chain(dve.scalar_tensor_tensor(r_base[:, :], r_base[:, :], float(P), r_prev[:, :], ALU.mult, ALU.subtract))

            def find_slots():
                chain(dve.tensor_tensor(r_lg[:, :, :], r_cum[:, :, :].rearrange("p e t -> p t e"), total, ALU.subtract))
                chain(dve.tensor_tensor(r_lg[:, :, :], r_lg[:, :, :], prefix, ALU.add))
                chain(dve.tensor_tensor(r_lg[:, :, :], r_lg[:, :, :], over_t(r_base[:, :]), ALU.add))
                chain(dve.tensor_tensor(r_lg[:, :, :], r_lg[:, :, :], r_oh[:, :, :], ALU.mult))
                chain(dve.tensor_reduce(posf[:, :], r_lg[:, :, :], AX, ALU.add))
                dve.tensor_copy(pos[:, :], posf[:, :]).then_inc(slots_found, 1)

            def find_experts():
                chain(dve.tensor_tensor(r_te[:, :, :], tile_at[:, :].unsqueeze(2).broadcast_to([P, TILES, E]),
                                        r_end[:, :].unsqueeze(1).broadcast_to([P, TILES, E]), ALU.is_ge))
                chain(dve.tensor_reduce(tile_ef[:, :], r_te[:, :, :], AX, ALU.add))
                dve.tensor_scalar(tile_e[:, :], tile_ef[:, :], float(E - 1), None, ALU.min).then_inc(route_done, 1)

            u_pair = pair[:, :, 0:2 * H1].rearrange("p k (c w) -> p k c w", c=2)

            def tokens(v, b):
                return v[:, b * C:(b + 1) * C, 0:D]

            def silu_y(b):
                dve.wait_ge(e_th, nth(ORDER, b))
                y = y_tok[:, b, :].rearrange("p (c d) -> p c d", c=C)
                dve.scalar_tensor_tensor(y, tokens(th_y, b), 1.0, y, ALU.add, ALU.mult).then_inc(e_silu, 1)

            def times_s(b):
                dve.wait_ge(e_weighed, nth(ORDER, b))
                if b > 4:
                    dve.wait_ge(htok_done, LB - B + b + 1)
                y = y_tok[:, b, :].rearrange("p (c d) -> p c d", c=C)
                dve.tensor_tensor(y, y, tokens(htok, b), ALU.mult).then_inc(e_s, 1)

            def add_x(b):
                dve.wait_ge(e_s, b + 1)
                y = y_tok[:, b, :].rearrange("p (c d) -> p c d", c=C)
                dve.tensor_tensor(y, y, tokens(x_sb, b), ALU.add).then_inc(dve_out, 1)

            def prepare_last():
                y = y_tok[:, LAST_B, :].rearrange("p (c d) -> p c d", c=C)
                over_c = lambda v: v[:, :].unsqueeze(1).broadcast_to([P, C, D])
                dve.wait_ge(e_weighed, 1)
                dve.tensor_tensor(tokens(th_y, LAST_B), y, over_c(lg_l), ALU.mult).then_inc(e_last, 1)
                dve.wait_ge(e_last, 1)
                dve.tensor_tensor(y, y, over_c(lb_l), ALU.mult).then_inc(e_last, 1)
                dve.wait_ge(e_last, 2)
                dve.tensor_tensor(y, y, tokens(x_sb, LAST_B), ALU.add).then_inc(e_last, 1)

            def finish_last():
                y = y_tok[:, LAST_B, :].rearrange("p (c d) -> p c d", c=C)
                g = tokens(th_y, LAST_B)
                dve.wait_ge(z_done, LB)
                dve.wait_ge(e_last, 3)
                dve.tensor_tensor(g, zhat[:, LAST_B % 2, :, :], g, ALU.mult).then_inc(e_last, 1)
                dve.wait_ge(e_last, 4)
                dve.tensor_tensor(y, y, g, ALU.add).then_inc(dve_out, 1)

            def split_u(l, t):
                if w := at(l, t, 0, B, LB):
                    dve.wait_ge(uT_done, w[0] + 1)
                    dve.tensor_tensor(uT_l[:, :], bank[2][:, :], uT_h[:, :], ALU.subtract).then_inc(uT_split, 1)

            def gn_moments(l, t):
                if w := at(l, t, 1, B, LB):
                    n, b, _ = w
                    dve.wait_ge(pe_gn, n + 1)
                    dve.tensor_copy(gn_m[:, :], bank[3][:, 0:2]).then_inc(gn_chain, 1)
                    dve.wait_ge(gn_chain, n * 4 + 1)
                    dve.scalar_tensor_tensor(gn_nv[:, :], gn_m[:, 0:1], gn_m[:, 0:1], gn_m[:, 1:2],
                                             ALU.mult, ALU.subtract).then_inc(gn_chain, 1)
                    dve.wait_ge(gn_chain, n * 4 + 2)
                    dve.tensor_scalar(gn_ve[:, :], gn_nv[:, :], -1.0, EPS, ALU.mult, ALU.add).then_inc(gn_var, 1)

            def step(l, t):
                first = isinstance(l, int) and l == 0
                ends = isinstance(l, int) and l == L
                if w := at(l, t, 0, B, LB):
                    n, b, _ = w
                    dve.wait_ge(pe_S, n + 1)
                    dve.tensor_copy(S_sb[:, 0, :], pair[:, 1, 0:H1]).then_inc(S_part, 1)
                    for c in range(1, C - 1):
                        dve.wait_ge(S_part, n * (C - 2) + c)
                        dve.tensor_tensor(S_sb[:, c, :], pair[:, 1, c * H1:(c + 1) * H1], S_sb[:, c - 1, :], ALU.add)\
                            .then_inc(S_part if c < C - 2 else S_done, 1)
                tile_out(l, t, EARLY)
                if parted(l, t):
                    dve.wait_ge(y_high, parted_steps(l, t))
                    dve.tensor_tensor(y_l[:, :], y_sb[:, :], y_h[:, :], ALU.subtract).then_inc(y_split, 1)
                if first and t == 1:
                    choose_expert()
                if first and t == 2:
                    count_tiles()
                if w := at(l, t, 0, B, LB):
                    n, b, _ = w
                    dve.wait_ge(pe_A, n + 1)
                    dve.tensor_tensor(A_sb[:, :, :], pair[:, 0, :].rearrange("p (c i) -> p c i", c=C),
                                      causal[:, :].unsqueeze(1).broadcast_to([P, C, P]), ALU.mult)\
                        .then_inc(A_done, 1)
                if w := at(l, t, 1, B, LB):
                    n, b, _ = w
                    dve.wait_ge(gg_done, n + 1)
                    dve.wait_ge(th_done, n + 1)
                    dve.scalar_tensor_tensor(gg_sb[:, :], th_sb[:, :], 1.0, gg_sb[:, :], ALU.add, ALU.mult)\
                        .then_inc(gt_done, 1)
                if not first:
                    tile_in(l, t, EARLY)
                if w := at(l, t, 1, B, LB):
                    n, b, _ = w
                    dve.wait_ge(gt_done, n + 1)
                    dve.wait_ge(pe_a, n + 1)
                    dve.scalar_tensor_tensor(gg_sb[:, :], bank[2][:, :], par[:, VAL_B:VAL_B + 1], gg_sb[:, :],
                                             ALU.add, ALU.mult).then_inc(act_done, 1)
                if first and t == 1:
                    expert_weight()
                tile_expert(l, t, LATE)
                if w := at(l, t, 0, B, LB):
                    n, b, _ = w
                    dve.wait_ge(pe_u, n + 1)
                    if isinstance(n, int) and n == 0:
                        dve.wait_ge(floor_in, 16)
                    row_sum = u_pair[:, :, :, D]
                    two = lambda v: v[:, :].rearrange("p (k c) -> p k c", k=2)
                    dve.tensor_tensor(two(rs1), row_sum, two(floor_sb), ALU.max).then_inc(u_chain, 1)
                    dve.wait_ge(u_chain, n * 3 + 1)
                    dve.scalar_tensor_tensor(two(rs2), row_sum, -1.0, two(rs1), ALU.mult, ALU.max)\
                        .then_inc(u_chain, 1)
                    dve.wait_ge(u_chain, n * 3 + 2)
                    dve.reciprocal(rs3[:, :], rs2[:, :]).then_inc(u_chain, 1)
                    dve.wait_ge(u_chain, n * 3 + 3)
                    dve.tensor_tensor(u_sb[:, :, :].rearrange("p (k c) d -> p k c d", k=2), u_pair[:, :, :, 0:D],
                                      rs3[:, :].rearrange("p (k c) -> p k c", k=2).unsqueeze(3)
                                      .broadcast_to([P, 2, C // 2, D]), ALU.mult).then_inc(u_done, 1)
                if w := at(l, t, 1, B, LB):
                    n, b, _ = w
                    dve.wait_ge(pe_w2, n + 1)
                    if b == 0:
                        dve.wait_ge(w2_set, w[2] + 1)
                    dve.bn_stats(gs_st[:, :], bank[6][:, :]).then_inc(gs_chain, 1)
                    alone(dve, gs_chain, n * 3 + 1)
                    dve.bn_aggr(gs_mv[:, :], gs_st[:, :]).then_inc(gs_chain, 1)
                    dve.wait_ge(gs_chain, n * 3 + 2)
                    dve.tensor_tensor(gs[:, 0:1], gs_mv[:, 0:1], par[:, W2_B:W2_B + 1], ALU.add).then_inc(gs_chain, 1)
                    dve.wait_ge(gs_chain, n * 3 + 3)
                    dve.scalar_tensor_tensor(gs[:, 1:2], gs[:, 0:1], gs[:, 0:1], gs_mv[:, 1:2], ALU.mult, ALU.add)\
                        .then_inc(gs_done, 1)

                if first:
                    tile_in(l, t, EARLY)
                if first and t == 0:
                    shift_logits()
                if first and t == 1:
                    gelu_bias()
                    count_tokens()
                if first and t == 2:
                    find_slots()
                if first and t == 3:
                    find_experts()
                if ends and t == 1:
                    prepare_last()
                    for b in (0, 1):
                        times_s(b)
                        add_x(b)
                    for b in (2, 3):
                        silu_y(b)
                tile_out(l, t, LATE)
                for stage in (gn_moments, split_u) if first and 2 <= t < B - 1 else (split_u, gn_moments):
                    stage(l, t)
                if w := at(l, t, 2, B, LB):
                    dve.wait_ge(pe_z, w[0] + 1)
                    ln_stats(w[0], w[1])
                if w := at(l, t, 1, B, LB):
                    n, b, _ = w
                    dve.wait_ge(gn_rstd, n + 1)
                    dve.tensor_tensor(gn_sc[:, :], gn_rs[:, :], par[:, GN_G:GN_G + 1], ALU.mult).then_inc(gn_chain, 1)
                    dve.tensor_tensor(gn_d[:, :], par[:, W2_B:W2_B + 1], gn_m[:, 0:1], ALU.subtract)\
                        .then_inc(gn_chain, 1)
                    dve.wait_ge(gn_chain, n * 4 + 4)
                    dve.scalar_tensor_tensor(gn_bi[:, :], gn_d[:, :], gn_sc[:, :], par[:, GN_B:GN_B + 1],
                                             ALU.mult, ALU.add).then_inc(gn_affine, 1)
                if w := at(l, t, 2, B, LB):
                    ln_moments(w[0], w[1])
                if ends and t == 1:
                    silu_y(4)
                tile_in(l, t, LATE)
                if w := at(l, t, 1, B, LB):
                    n, b, _ = w
                    dve.wait_ge(gn_done, n + 1)
                    dve.tensor_tensor(y_sb[:, :], y_sb[:, :], hT[:, b, :], ALU.add).then_inc(y_done, 1)
                if t + 1 < B:
                    tile_expert(l, t + 1, EARLY)
                if w := at(l, t, 2, B, LB):
                    n, b, _ = w
                    ln_shifts(n, b)
                    need(dve, htok_done, n - 1)
                    dve.wait_ge(ln_shift, n + 1)
                    for c in range(C // 2):
                        last = dve.tensor_scalar(zhat[:, b % 2, c, :], bank[7][:, c * D:(c + 1) * D],
                                                 ln_rs[:, b % 2, c:c + 1], ln_nb[:, b % 2, c:c + 1], ALU.mult, ALU.add)
                    last.then_inc(z_half, 1)
                if ends and t == 0:
                    for b in ORDER[:3]:
                        silu_y(b)
                if ends and t == 1:
                    for b in (5, 6):
                        silu_y(b)
                    finish_last()
                if ends and t == 2:
                    for b in (2, 3, 4):
                        times_s(b)
                    for b in (5, 6):
                        times_s(b)
                        add_x(b)

            def tile_out(l, t, place_):
                w = turn(l, t, place_)
                if w is None or first_turns(w[0]):
                    return
                j, k = w
                q = buffer_of(k)
                bias = moe_b2[:, bass.ds(loaded[place_], 1), :].rearrange("p a f -> p (a f)")
                dve.wait_ge(yt_out[q], 16 * (1 + used_before(l, k)))
                dve.wait_ge(pe_y, j - TILE_LAG + 1)
                dve.tensor_tensor(yt[q][:, :], bank[5][:, 0:D], bias, ALU.add).then_inc(yt_done, 1)

            def tile_expert(l, t, place_):
                w = turn(l, t, place_)
                if w is not None and not first_turns(w[0]):
                    loaded[place_] = dve.value_load(tile_e[0:1, bass.ds(w[0] - TILE_LAG, 1)], min_val=0, max_val=E - 1)

            def tile_in(l, t, place_):
                if w := turn(l, t, place_):
                    dve.wait_ge(pe_xt, w[0] + 1)
                    dve.tensor_copy(xtT[:, :], bank[4][:, 0:P]).then_inc(xtT_done, 1)

            steps(dve, step, L, B, LAG)

        @block.tensor
        def _(pe):
            mm = nc.tensor.matmul
            pe.wait_ge(const_made, 6)

            def weights_T(l):
                need(pe, wT_done, l - 1)
                for j, part in enumerate((1, 0, 2)):
                    last = pe.transpose(bank[2 + l % 2][:, j * D:(j + 1) * D],
                                        wkqv_sb[:, l, part * D:(part + 1) * D], ident[:, :])
                last.then_inc(pe_wT, 1)

            def products(l):
                pe.wait_ge(wT_done, l + 1)
                need(pe, prod_done, l - 1)
                dst, src = bank[4 + l % 2], wT_sb[l % 2]
                mm(dst[:, 0:D], src[:, 0:D], src[:, D:2 * D], start=True, stop=True)
                mm(dst[:, D:3 * D], src[:, 2 * D:3 * D], wm1_sb[:, l, :], start=True, stop=True).then_inc(pe_prod, 1)

            def logits(b):
                pe.wait_ge(xT_done, b + 1)
                for c in range(C):
                    k = b * C + c
                    last = mm(bank[7][:, k * E:(k + 1) * E], hT[:, b, c * P:(c + 1) * P], gate_sb[:, :],
                              start=True, stop=True)
                last.then_inc(pe_gate, 1)

            def keep_warm(count):
                for _ in range(count):
                    mm(bank[6][:, 0:2 * P], ident[:, :], ones[:, :], start=True, stop=True)

            keep_warm(8)
            for b in range(B):
                pe.wait_ge(xn_done, b + 1)
                pe.wait_ge(xn_last, b + 1)
                need(pe, xT_done, b - 1)
                for c in range(C):
                    last = pe.transpose(pair[:, b % 2, c * P:(c + 1) * P], xn[:, b * C + c, 0:D], ident[:, :])
                last.then_inc(pe_xT, 1)
                if b == 0:
                    pe.wait_ge(kqv_in, 16)
                if b < L:
                    weights_T(b)
                if 2 <= b < 2 + L:
                    if b == 2:
                        pe.wait_ge(m1_in, 16)
                    products(b - 2)
                if b < B - 1:
                    keep_warm(1)
                if b >= L:
                    if b == L:
                        pe.wait_ge(gate_in, 16)
                    logits(b - L)
                if b == B - 1:
                    pe.wait_ge(rows_in, 16 * 8)
                    pe.transpose(bank[6][:, 0:NROWS], rows[:, :], ident[0:NROWS, 0:NROWS]).then_inc(pe_rows, 1)
            pe.wait_ge(col_made, 2)
            pe.wait_ge(prod_done, L)
            pe.wait_ge(xT_done, B)

            loaded = {}

            def tile_expert(l, t, place):
                w = turn(l, t, place)
                if w is not None and not first_turns(w[0]):
                    loaded[place] = pe.value_load(tile_e[0:1, bass.ds(w[0] - TILE_LAG, 1)], min_val=0, max_val=E - 1)

            def tile_back(l, t, place):
                w = turn(l, t, place)
                if w is None or first_turns(w[0]):
                    return
                j, k = w
                e = loaded[place]
                pe.wait_ge(h_done, j - 1)
                for i in range(KF):
                    last = mm(bank[5][:, 0:D], h_T[:, i * P:(i + 1) * P],
                              moe_w2[:, bass.ds(e, 1), i, :].rearrange("p a d -> p (a d)"),
                              start=i == 0, stop=i == KF - 1)
                last.then_inc(pe_y, 1)

            def tile_front(l, t, place, gelu_read):
                w = turn(l, t, place)
                if w is None:
                    return
                j, k = w
                if not (isinstance(j, int) and j < 1):
                    if k:
                        q, count = buffer_of(k - 1), loaded_before(l, k - 1) + 1
                    else:
                        q, count = buffer_of(TURN_TILES - 1), loaded_before(l - 1, TURN_TILES - 1) + 1
                    pe.wait_ge(w1_in[q], 16 * count)
                    pe.wait_ge(xtT_done, j)
                    need(pe, yt_done, j - 1)
                    for i in range(KF):
                        last = mm(bank[5][:, i * P:(i + 1) * P], w1_t[q][:, i * P:(i + 1) * P], xtT[:, :],
                                  start=True, stop=True)
                    last.then_inc(pe_h, 1)
                q = buffer_of(k)
                pe.wait_ge(xt_in[q], 16 * (loaded_before(l, k) + 1))
                need(pe, xtT_done, j)
                pe.wait_ge(G_done, gelu_read)
                pe.transpose(bank[4][:, 0:P], xt[q][:, 0:D], ident[:, :]).then_inc(pe_xt, 1)

            def parts_product(dst, weights, cols, high, low, done):
                mm(dst[:, :], weights[:, 0, cols], high[:, :], start=True, stop=False)
                mm(dst[:, :], weights[:, 1, cols], high[:, :], start=False, stop=False)
                mm(dst[:, :], weights[:, 0, cols], low[:, :], start=False, stop=True).then_inc(done, 1)

            def gelu_first(l, t, i):
                if w := at(l, t, 2, B, LB):
                    n, b, _ = w
                    k = halves(l, t)[i]
                    if parted(l, t):
                        if t in (1, 2):
                            pe.wait_ge(f1_parts_set, w[2] + 1)
                        pe.wait_ge(y_split, parted_steps(l, t))
                    else:
                        pe.wait_ge(y_done, n + 1)
                    if b == 0:
                        pe.wait_ge(f1_set, w[2] + 1)
                    need(pe, G_done, 2 * n)
                    if k == 0:
                        need(pe, gg_done, n + 2 if not (isinstance(n, int) and n + 2 > LB) else LB)
                    else:
                        if not (isinstance(l, int) and l == 0):
                            need(pe, xtT_done, turns_before(l, t, LATE))
                    cols = slice(k * D, (k + 1) * D)
                    if parted(l, t):
                        parts_product(bank[3 + k], f1_parts_l, cols, y_h, y_l, pe_f1)
                    else:
                        mm(bank[3 + k][:, :], f1_l[:, cols], y_sb[:, :], start=True, stop=True).then_inc(pe_f1, 1)

            def zhat_by_feature(l, t):
                w = at(l, t, 3, B, LB)
                if w and w[0] is not LB - 1:
                    n, b, _ = w
                    pe.wait_ge(z_done, n + 1)
                    for c in range(C):
                        last = pe.transpose(bank[7][:, c * P:(c + 1) * P], zhat[:, b % 2, c, :], ident[:, :])
                    last.then_inc(pe_zT, 1)

            def u_by_feature(l, t):
                if w := at(l, t, 0, B, LB):
                    n, b, _ = w
                    pe.wait_ge(u_done, n + 1)
                    need(pe, act_done, n)
                    for c in range(C):
                        last = pe.transpose(bank[2][:, c * P:(c + 1) * P], u_sb[:, c, :], ident[:, :])
                    last.then_inc(pe_uT, 1)

            def gelu_second(l, t):
                if w := at(l, t, 2, B, LB):
                    n, b, _ = w
                    need(pe, hT_done, n)
                    if isinstance(n, int) and n == 0:
                        pe.wait_ge(fb_done, 1)
                    pe.wait_ge(G_done, 2 * n + 2)
                    if b == 0:
                        pe.wait_ge(f2_set, w[2] + 1)
                    for c in range(C):
                        at_c = slice(c * P, (c + 1) * P)
                        mm(bank[7][:, at_c], y_sb[:, at_c], ident[:, :], start=True, stop=False, is_transpose=True)
                        for k in range(2):
                            last = mm(bank[7][:, at_c], G_sb[:, k, at_c], f2_l[:, k, :], start=False, stop=k == 1)
                    last.then_inc(pe_z, 1)

            def means(l, t):
                if w := at(l, t, 1, B, LB):
                    n, b, _ = w
                    pe.wait_ge(gs_done, n + 1)
                    need(pe, G_done, 2 * n)
                    pe.wait_ge(gg_done, n + 1)
                    mm(bank[3][:, 0:2], mean_of[:, :], gs[:, :], start=True, stop=True).then_inc(pe_gn, 1)

            def step(l, t):
                first = isinstance(l, int) and l == 0
                start = first and t == 0
                tile_expert(l, t, EARLY)
                tile_expert(l, t, LATE)
                if w := at(l, t, 0, B, LB):
                    n, b, _ = w
                    tok = (lambda c: xn[:, b * C + c, 0:H1]) if first else (lambda c: htok[:, b * C + c, :])
                    if not first:
                        pe.wait_ge(htok_done, n - B + 1)
                        pe.wait_ge(hT_done, n - B + 1)
                    need(pe, u_done, n)
                    for c in range(C - 1):
                        last = mm(pair[:, 1, c * H1:(c + 1) * H1], tok(c)[:, 0:D], tok(c), start=True, stop=True)
                    last.then_inc(pe_S, 1)
                    if b == 0:
                        pe.wait_ge(m_set, w[2] + 1)
                    mm(pair[:, 0, :], m_l[:, :], hT[:, b, :], start=True, stop=True).then_inc(pe_q, 1)
                    if start:
                        logits(L)
                if w := at(l, t, 1, B, LB):
                    n, b, _ = w
                    pe.wait_ge(uT_split, n + 1)
                    if b == 0:
                        pe.wait_ge(w_set, w[2] + 1)
                    need(pe, gn_chain, 4 * n - 3)
                    parts_product(bank[3], w_l, slice(D, 2 * D), uT_h, uT_l, pe_g)
                    parts_product(bank[2], w_l, slice(0, D), uT_h, uT_l, pe_a)
                n2 = l * B + t - 2
                tile_back(l, t, EARLY)
                if w := at(l, t, 0, B, LB):
                    n, b, _ = w
                    pe.wait_ge(q_done, n + 1)
                    for c in range(C):
                        at_c = slice(c * P, (c + 1) * P)
                        last = mm(pair[:, 0, at_c], hT[:, b, at_c], q_sb[:, at_c], start=True, stop=True)
                    last.then_inc(pe_A, 1)
                    if start:
                        logits(L + 1)
                if first and t == 1:
                    pe.wait_ge(r_shift, 2)
                    oh = r_oh[:, :, :].rearrange("p t e -> p (t e)")
                    mm(bank[5][:, 0:TE], before[:, :], oh, start=True, stop=True)
                    mm(bank[5][:, TE:2 * TE], ones[:, 0:P], oh, start=True, stop=True).then_inc(pe_prefix, 1)
                if not first:
                    tile_front(l, t, EARLY, n2 * 2)
                if parted(l, t):
                    zhat_by_feature(l, t)
                gelu_first(l, t, 0)
                gelu_first(l, t, 1)
                if not parted(l, t):
                    zhat_by_feature(l, t)
                if w := at(l, t, 0, B, LB):
                    n, b, _ = w
                    tok = (lambda c: xn[:, b * C + c, 0:H1]) if first else (lambda c: htok[:, b * C + c, :])
                    pe.wait_ge(A_done, n + 1)
                    pe.wait_ge(S_done, n + 1)
                    for c in range(C):
                        dst = pair[:, c // 2, (c % 2) * H1:(c % 2 + 1) * H1]
                        last = mm(dst, A_sb[:, c, :], tok(c), start=True, stop=c == 0)
                        if c:
                            last = mm(dst, q_sb[:, c * P:(c + 1) * P], S_sb[:, c - 1, :], start=False, stop=True)
                    last.then_inc(pe_u, 1)
                    if start:
                        logits(L + 2)
                        logits(L + 3)
                if w := at(l, t, 1, B, LB):
                    n, b, _ = w
                    pe.wait_ge(act_done, n + 1)
                    if b == 0:
                        pe.wait_ge(w2_set, w[2] + 1)
                    need(pe, gn_done, n)
                    mm(bank[6][:, :], w2_l[:, :], gg_sb[:, :], start=True, stop=True).then_inc(pe_w2, 1)
                if first and t == 1:
                    pe.wait_ge(rows_done, 1)
                    pe.wait_ge(f1_in, 16)
                    for i in range(2 * L):
                        last = mm(bank[7][:, i:i + 1], all_f1[:, i // 2, i % 2 * D:(i % 2 + 1) * D],
                                  rowsT[:, R_BF2 + i // 2:R_BF2 + i // 2 + 1], start=True, stop=True)
                    pe.wait_ge(bias1_in, 16)
                    pe.transpose(bank[7][:, 2 * L:2 * L + E * KF], b1_rows[:, :], ident[0:E * KF, 0:E * KF])\
                        .then_inc(pe_fb, 1)
                tile_back(l, t, LATE)
                if first:
                    tile_front(l, t, EARLY, n2 * 2 + 2)
                for stage in ((gelu_second, means, u_by_feature) if first and 2 <= t < B - 1 else
                              (u_by_feature, gelu_second, means)):
                    stage(l, t)
                tile_front(l, t, LATE, n2 * 2 + 2)
                if isinstance(l, int) and l == 0 and t == B - 2:
                    pe.wait_ge(route_done, 1)

            steps(pe, step, L, B, LAG)


_INS = ['L0_attn_x', 'L0_attn_Wkqv', 'L0_attn_Wm1', 'L0_attn_bm1', 'L0_attn_Wm2', 'L0_attn_bm2', 'L0_attn_gn_g',
        'L0_attn_gn_b', 'L0_attn_Wf1', 'L0_attn_bf1', 'L0_attn_Wf2', 'L0_attn_bf2', 'L0_attn_ln_g', 'L0_attn_ln_b',
        'L0_ffn_gate_w', 'L0_ffn_w1', 'L0_ffn_b1', 'L0_ffn_w2', 'L0_ffn_b2']


def kernel(**inputs):
    import numpy as np
    import concourse.bacc as bacc
    from concourse import mybir as mb
    from concourse.bass_utils import run_bass_kernel_spmd

    nc = bacc.Bacc("TRN2", target_bir_lowering=False, num_devices=1)
    arrays, args = {}, []
    for name in _INS:
        a = np.ascontiguousarray(inputs[name])
        arrays[f"in_{name}"] = a
        args.append(nc.dram_tensor(f"in_{name}", a.shape, mb.dt.from_np(a.dtype), kind="ExternalInput").ap())
    B, S, D = inputs['L0_attn_x'].shape
    i = np.arange(S, dtype=np.float32).reshape(S // 128, 128).T
    arrays["row_floor"] = np.ascontiguousarray(np.sqrt(np.float32(D)) * (1 + np.sqrt(i))).astype(np.float32)
    args.append(nc.dram_tensor("row_floor", arrays["row_floor"].shape, mb.dt.float32, kind="ExternalInput").ap())
    out = nc.dram_tensor("out", (B, S, D), mb.dt.float32, kind="ExternalOutput").ap()
    retention_moe_kernel(nc, *args, out)
    r = run_bass_kernel_spmd(nc, [arrays], core_ids=[0])
    return r.results[0]["out"]
```
